# Optimizing a Trainium2 kernel written in Bass

```python
import numpy as np
import jax
import jax.numpy as jnp

def _softmax(x, axis=-1):
    return jax.nn.softmax(x, axis=axis)

def _gelu(x):
    return jax.nn.gelu(x, approximate=True)

def _silu(x):
    return jax.nn.silu(x)

def _sigmoid(x):
    return jax.nn.sigmoid(x)

def _layernorm(x, axis=-1, eps=1e-05):
    m = jnp.mean(x, axis=axis, keepdims=True)
    v = jnp.var(x, axis=axis, keepdims=True)
    return (x - m) / jnp.sqrt(v + eps)

def _scatter_add(tgt, idx, src, axis=0):
    return tgt.at[idx].add(src)

def _segment_sum(src, seg, n):
    return jax.ops.segment_sum(src, seg, n)
kernel_name = 'mk_sandwich_d2_jaxref_r8_dae55a'

def setup_inputs(seed: int=0):
    np.random.seed(seed)
    _w = jnp.asarray

    def _L0_attn_setup():
        import jax, jax.numpy as jnp
        import numpy as np
        B, L, E, H = (2, 512, 128, 16)
        D = E // H
        CHUNK = 32

        def _linear_attention(x, W_qkv, W_out):
            Bz, Lz, Ez = x.shape
            scale = D ** (-0.5)
            qkv = x @ W_qkv.T
            qkv = qkv.reshape(Bz, Lz, 3, H, D).transpose(2, 0, 3, 1, 4)
            q, k, v = (qkv[0], qkv[1], qkv[2])
            q = (jax.nn.elu(q) + 1.0) * scale
            k = jax.nn.elu(k) + 1.0
            nc = Lz // CHUNK

            def to_chunks(t):
                return t.reshape(Bz, H, nc, CHUNK, D).transpose(2, 0, 1, 3, 4)
            qc, kc, vc = (to_chunks(q), to_chunks(k), to_chunks(v))
            causal = jnp.tril(jnp.ones((CHUNK, CHUNK), dtype=x.dtype))

            def step(carry, inp):
                S, Z = carry
                qi, ki, vi = inp
                attn = jnp.einsum('bhld,bhmd->bhlm', qi, ki) * causal
                num = jnp.einsum('bhlm,bhme->bhle', attn, vi) + jnp.einsum('bhld,bhde->bhle', qi, S)
                den = attn.sum(-1) + jnp.einsum('bhld,bhd->bhl', qi, Z)
                S = S + jnp.einsum('bhmd,bhme->bhde', ki, vi)
                Z = Z + ki.sum(axis=2)
                return ((S, Z), (num, den))
            S0 = jnp.zeros((Bz, H, D, D), dtype=x.dtype)
            Z0 = jnp.zeros((Bz, H, D), dtype=x.dtype)
            _, (num, den) = jax.lax.scan(step, (S0, Z0), (qc, kc, vc))
            num = num.transpose(1, 2, 0, 3, 4).reshape(Bz, H, Lz, D)
            den = den.transpose(1, 2, 0, 3).reshape(Bz, H, Lz)
            den = jnp.maximum(den, 1e-06)
            out = num / den[..., None]
            out = out.transpose(0, 2, 1, 3).reshape(Bz, Lz, Ez)
            return out @ W_out.T
        key = jax.random.key(seed)
        k1, k2, k3 = jax.random.split(key, 3)
        x = jax.random.normal(k1, (B, L, E), dtype=jnp.float32)
        W_qkv = jax.random.normal(k2, (3 * E, E), dtype=jnp.float32) * 0.02
        W_out = jax.random.normal(k3, (E, E), dtype=jnp.float32) * 0.02
        return {'x': x, 'W_qkv': W_qkv, 'W_out': W_out}
    _L0_attn_in = _L0_attn_setup()

    def _L0_ffn_setup():
        import jax, jax.numpy as jnp
        import numpy as np
        TOP_K = 2
        key = jax.random.key(seed)
        ks = jax.random.split(key, 8)
        B, S, D = (2, 256, 128)
        N_r, N_s = (16, 2)
        u = jax.random.normal(ks[0], (B, S, D), dtype=jnp.float32)
        centroids = jax.random.normal(ks[1], (N_r, D), dtype=jnp.float32)
        expert_biases = jnp.zeros((N_r,), dtype=jnp.float32)
        Wr = jax.random.normal(ks[2], (N_r, D, D), dtype=jnp.float32) * (1.0 / np.sqrt(D))
        br = jax.random.normal(ks[3], (N_r, D), dtype=jnp.float32) * 0.01
        Ws = jax.random.normal(ks[4], (N_s, D, D), dtype=jnp.float32) * (1.0 / np.sqrt(D))
        bs = jax.random.normal(ks[5], (N_s, D), dtype=jnp.float32) * 0.01
        return {'u': u, 'centroids': centroids, 'expert_biases': expert_biases, 'Wr': Wr, 'br': br, 'Ws': Ws, 'bs': bs}
    _L0_ffn_in = _L0_ffn_setup()

    def _L1_attn_setup():
        import jax, jax.numpy as jnp
        import numpy as np
        NUM_HEADS = 16
        DIM_HEAD = 64
        SCALE = DIM_HEAD ** (-0.5)
        ROPE_BASE = 10000.0

        def _rope(t):
            n, d = (t.shape[2], t.shape[3])
            inv_freq = 1.0 / ROPE_BASE ** (jnp.arange(0, d, 2, dtype=jnp.float32) / d)
            freqs = jnp.arange(n, dtype=jnp.float32)[:, None] * inv_freq[None, :]
            cos = jnp.concatenate([jnp.cos(freqs), jnp.cos(freqs)], axis=-1)
            sin = jnp.concatenate([jnp.sin(freqs), jnp.sin(freqs)], axis=-1)
            t1, t2 = jnp.split(t, 2, axis=-1)
            rot = jnp.concatenate([-t2, t1], axis=-1)
            return t * cos + rot * sin
        key = jax.random.key(seed)
        k1, k2, k3 = jax.random.split(key, 3)
        B, N, D = (2, 2049, 128)
        x = jax.random.normal(k1, (B, N, D), dtype=jnp.float32)
        ln_gamma = jnp.ones((D,), dtype=jnp.float32)
        ln_beta = jnp.zeros((D,), dtype=jnp.float32)
        w_qkv = jax.random.normal(k2, (D, 3 * NUM_HEADS * DIM_HEAD), dtype=jnp.float32) * 0.02
        w_out = jax.random.normal(k3, (NUM_HEADS * DIM_HEAD, D), dtype=jnp.float32) * 0.02
        return {'x': x, 'ln_gamma': ln_gamma, 'ln_beta': ln_beta, 'w_qkv': w_qkv, 'w_out': w_out}
    _L1_attn_in = _L1_attn_setup()

    def _L1_ffn_setup():
        import jax, jax.numpy as jnp
        import numpy as np
        D_IN, D_HID = (128, 512)

        def _ternary(key, shape):
            return jax.random.randint(key, shape, -1, 2).astype(jnp.float32)

        def _tlin(x, w, s):
            return jnp.einsum('bsi,oi->bso', x, w) * s
        key = jax.random.key(seed)
        ks = jax.random.split(key, 12)
        inv = lambda fan: 1.0 / np.sqrt(fan).astype(np.float32)
        return {'x': jax.random.normal(ks[0], (4, 256, D_IN), dtype=jnp.float32), 'w1_w': _ternary(ks[1], (D_HID, D_IN)), 'w1_s': jax.random.uniform(ks[2], (D_HID,), dtype=jnp.float32) * inv(D_IN), 'w2_w': _ternary(ks[3], (D_HID, D_IN)), 'w2_s': jax.random.uniform(ks[4], (D_HID,), dtype=jnp.float32) * inv(D_IN), 'h1_w': _ternary(ks[5], (D_HID, D_HID)), 'h1_s': jax.random.uniform(ks[6], (D_HID,), dtype=jnp.float32) * inv(D_HID), 'h2_w': _ternary(ks[7], (D_HID, D_HID)), 'h2_s': jax.random.uniform(ks[8], (D_HID,), dtype=jnp.float32) * inv(D_HID), 'w3_w': _ternary(ks[9], (D_IN, D_HID)), 'w3_s': jax.random.uniform(ks[10], (D_IN,), dtype=jnp.float32) * inv(D_HID)}
    _L1_ffn_in = _L1_ffn_setup()
    _d = {'L0_attn_x': _L0_attn_in['x'], 'L0_attn_W_qkv': _L0_attn_in['W_qkv'], 'L0_attn_W_out': _L0_attn_in['W_out'], 'L0_ffn_centroids': _L0_ffn_in['centroids'], 'L0_ffn_expert_biases': _L0_ffn_in['expert_biases'], 'L0_ffn_Wr': _L0_ffn_in['Wr'], 'L0_ffn_br': _L0_ffn_in['br'], 'L0_ffn_Ws': _L0_ffn_in['Ws'], 'L0_ffn_bs': _L0_ffn_in['bs'], 'L1_attn_ln_gamma': _L1_attn_in['ln_gamma'], 'L1_attn_ln_beta': _L1_attn_in['ln_beta'], 'L1_attn_w_qkv': _L1_attn_in['w_qkv'], 'L1_attn_w_out': _L1_attn_in['w_out'], 'L1_ffn_w1_w': _L1_ffn_in['w1_w'], 'L1_ffn_w1_s': _L1_ffn_in['w1_s'], 'L1_ffn_w2_w': _L1_ffn_in['w2_w'], 'L1_ffn_w2_s': _L1_ffn_in['w2_s'], 'L1_ffn_h1_w': _L1_ffn_in['h1_w'], 'L1_ffn_h1_s': _L1_ffn_in['h1_s'], 'L1_ffn_h2_w': _L1_ffn_in['h2_w'], 'L1_ffn_h2_s': _L1_ffn_in['h2_s'], 'L1_ffn_w3_w': _L1_ffn_in['w3_w'], 'L1_ffn_w3_s': _L1_ffn_in['w3_s']}
    _x0 = _d['L0_attn_x']
    _d['L0_attn_x'] = jax.random.normal(jax.random.fold_in(jax.random.key(seed), 1), (16, 256, 128), dtype=_x0.dtype)
    del _x0
    return _d

def reference(L0_attn_x, L0_attn_W_qkv, L0_attn_W_out, L0_ffn_centroids, L0_ffn_expert_biases, L0_ffn_Wr, L0_ffn_br, L0_ffn_Ws, L0_ffn_bs, L1_attn_ln_gamma, L1_attn_ln_beta, L1_attn_w_qkv, L1_attn_w_out, L1_ffn_w1_w, L1_ffn_w1_s, L1_ffn_w2_w, L1_ffn_w2_s, L1_ffn_h1_w, L1_ffn_h1_s, L1_ffn_h2_w, L1_ffn_h2_s, L1_ffn_w3_w, L1_ffn_w3_s):

    def _L0_attn_ref(x, W_qkv, W_out):
        import jax, jax.numpy as jnp
        import numpy as np
        B, L, E, H = (2, 512, 128, 16)
        D = E // H
        CHUNK = 32

        def _linear_attention(x, W_qkv, W_out):
            Bz, Lz, Ez = x.shape
            scale = D ** (-0.5)
            qkv = x @ W_qkv.T
            qkv = qkv.reshape(Bz, Lz, 3, H, D).transpose(2, 0, 3, 1, 4)
            q, k, v = (qkv[0], qkv[1], qkv[2])
            q = (jax.nn.elu(q) + 1.0) * scale
            k = jax.nn.elu(k) + 1.0
            nc = Lz // CHUNK

            def to_chunks(t):
                return t.reshape(Bz, H, nc, CHUNK, D).transpose(2, 0, 1, 3, 4)
            qc, kc, vc = (to_chunks(q), to_chunks(k), to_chunks(v))
            causal = jnp.tril(jnp.ones((CHUNK, CHUNK), dtype=x.dtype))

            def step(carry, inp):
                S, Z = carry
                qi, ki, vi = inp
                attn = jnp.einsum('bhld,bhmd->bhlm', qi, ki) * causal
                num = jnp.einsum('bhlm,bhme->bhle', attn, vi) + jnp.einsum('bhld,bhde->bhle', qi, S)
                den = attn.sum(-1) + jnp.einsum('bhld,bhd->bhl', qi, Z)
                S = S + jnp.einsum('bhmd,bhme->bhde', ki, vi)
                Z = Z + ki.sum(axis=2)
                return ((S, Z), (num, den))
            S0 = jnp.zeros((Bz, H, D, D), dtype=x.dtype)
            Z0 = jnp.zeros((Bz, H, D), dtype=x.dtype)
            _, (num, den) = jax.lax.scan(step, (S0, Z0), (qc, kc, vc))
            num = num.transpose(1, 2, 0, 3, 4).reshape(Bz, H, Lz, D)
            den = den.transpose(1, 2, 0, 3).reshape(Bz, H, Lz)
            den = jnp.maximum(den, 1e-06)
            out = num / den[..., None]
            out = out.transpose(0, 2, 1, 3).reshape(Bz, Lz, Ez)
            return out @ W_out.T
        return _linear_attention(x, W_qkv, W_out)

    def _L0_ffn_ref(u, centroids, expert_biases, Wr, br, Ws, bs):
        import jax, jax.numpy as jnp
        import numpy as np
        TOP_K = 2
        N_r = centroids.shape[0]
        N_s = Ws.shape[0]
        raw_scores = jnp.einsum('bsd,ed->bse', u, centroids)
        s = jax.nn.softmax(raw_scores + expert_biases, axis=-1)
        topk_vals, topk_idx = jax.lax.top_k(s, TOP_K)
        g_topk = jnp.sum(jax.nn.one_hot(topk_idx, N_r, dtype=s.dtype) * topk_vals[..., None], axis=-2)
        xe = jnp.einsum('bsd,eod->bseo', u, Wr) + br
        routed = jnp.einsum('bse,bseo->bso', g_topk, xe)
        shared = (jnp.einsum('bsd,eod->bso', u, Ws) + jnp.sum(bs, axis=0)) / N_s
        return u + routed + shared

    def _L1_attn_ref(x, ln_gamma, ln_beta, w_qkv, w_out):
        import jax, jax.numpy as jnp
        import numpy as np
        NUM_HEADS = 16
        DIM_HEAD = 64
        SCALE = DIM_HEAD ** (-0.5)
        ROPE_BASE = 10000.0

        def _rope(t):
            n, d = (t.shape[2], t.shape[3])
            inv_freq = 1.0 / ROPE_BASE ** (jnp.arange(0, d, 2, dtype=jnp.float32) / d)
            freqs = jnp.arange(n, dtype=jnp.float32)[:, None] * inv_freq[None, :]
            cos = jnp.concatenate([jnp.cos(freqs), jnp.cos(freqs)], axis=-1)
            sin = jnp.concatenate([jnp.sin(freqs), jnp.sin(freqs)], axis=-1)
            t1, t2 = jnp.split(t, 2, axis=-1)
            rot = jnp.concatenate([-t2, t1], axis=-1)
            return t * cos + rot * sin
        B, N, D = x.shape
        mu = jnp.mean(x, axis=-1, keepdims=True)
        var = jnp.mean(jnp.square(x - mu), axis=-1, keepdims=True)
        xn = (x - mu) * jax.lax.rsqrt(var + 1e-05) * ln_gamma + ln_beta
        qkv = xn @ w_qkv
        q, k, v = jnp.split(qkv, 3, axis=-1)

        def to_heads(t):
            return t.reshape(B, N, NUM_HEADS, DIM_HEAD).transpose(0, 2, 1, 3)
        q, k, v = (to_heads(q), to_heads(k), to_heads(v))
        q = jnp.concatenate([q[:, :, :1, :], _rope(q[:, :, 1:, :])], axis=2)
        k = jnp.concatenate([k[:, :, :1, :], _rope(k[:, :, 1:, :])], axis=2)
        dots = jnp.einsum('bhqd,bhkd->bhqk', q, k) * SCALE
        attn = jax.nn.softmax(dots, axis=-1)
        out = jnp.einsum('bhqk,bhkd->bhqd', attn, v)
        out = out.transpose(0, 2, 1, 3).reshape(B, N, NUM_HEADS * DIM_HEAD)
        return out @ w_out

    def _L1_ffn_ref(x, w1_w, w1_s, w2_w, w2_s, h1_w, h1_s, h2_w, h2_s, w3_w, w3_s):
        import jax, jax.numpy as jnp
        import numpy as np
        D_IN, D_HID = (128, 512)

        def _ternary(key, shape):
            return jax.random.randint(key, shape, -1, 2).astype(jnp.float32)

        def _tlin(x, w, s):
            return jnp.einsum('bsi,oi->bso', x, w) * s
        h = jax.nn.silu(_tlin(x, w1_w, w1_s)) * _tlin(x, w2_w, w2_s)
        h = jax.nn.gelu(_tlin(h, h1_w, h1_s), approximate=False)
        h = jax.nn.gelu(_tlin(h, h2_w, h2_s), approximate=False)
        return _tlin(h, w3_w, w3_s)
    x = L0_attn_x
    x = x + _layernorm(_L0_attn_ref(_layernorm(x, axis=-1), L0_attn_W_qkv, L0_attn_W_out), axis=-1)
    x = x + _layernorm(_L0_ffn_ref(_layernorm(x, axis=-1), L0_ffn_centroids, L0_ffn_expert_biases, L0_ffn_Wr, L0_ffn_br, L0_ffn_Ws, L0_ffn_bs), axis=-1)
    x = x + _layernorm(_L1_attn_ref(_layernorm(x, axis=-1), L1_attn_ln_gamma, L1_attn_ln_beta, L1_attn_w_qkv, L1_attn_w_out), axis=-1)
    x = x + _layernorm(_L1_ffn_ref(_layernorm(x, axis=-1), L1_ffn_w1_w, L1_ffn_w1_s, L1_ffn_w2_w, L1_ffn_w2_s, L1_ffn_h1_w, L1_ffn_h1_s, L1_ffn_h2_w, L1_ffn_h2_s, L1_ffn_w3_w, L1_ffn_w3_s), axis=-1)
    return x

_drawn_inputs = setup_inputs


def setup_inputs(seed=0):
    import zlib

    import numpy as np

    out = dict(_drawn_inputs(seed))
    spreads = {'L0_ffn_expert_biases': (0.0, 0.8),
     'L1_attn_ln_gamma': (1.0, 0.2),
     'L1_attn_ln_beta': (0.0, 0.1)}
    factors = {'L0_ffn_br': 8.0, 'L0_ffn_bs': 8.0}
    for name, (base, spread) in spreads.items():
        noise = np.random.default_rng([zlib.crc32(name.encode()), seed]).standard_normal(out[name].shape)
        drawn = base * np.exp(spread * noise) if base else spread * noise
        out[name] = jnp.asarray(drawn.astype(out[name].dtype))
    for name, factor in factors.items():
        out[name] = (out[name] * factor).astype(out[name].dtype)
    return out
```

```python
import concourse.bass as bass
from concourse import mybir
from contextlib import ExitStack


def block_kernel(nc, x, w, const, out):
    F32 = mybir.dt.float32
    U32 = mybir.dt.uint32
    ALU = mybir.AluOpType
    ACT = mybir.ActivationFunctionType
    AX = mybir.AxisListType

    P = 128
    SEQS, LEN, E = x.shape
    T = LEN // P
    EPS = 1e-5
    LA_GROUPS, LA_PER_GROUP, LA_D = 4, 4, 8
    EXPERTS, PER_BANK = 16, 4
    UNITS_B = T * EXPERTS // PER_BANK
    HEADS, D = 16, 64
    PAIRS = HEADS // 2
    INNER = HEADS * D
    BLK = 512
    BLOCKS = 3 * INNER // BLK
    HID_T = 512 // P
    LAYERS = 4
    LA, MOE, SA, FFN = range(LAYERS)

    ctx = ExitStack()
    with ctx:
        def sb(name, shape, dt=F32):
            return ctx.enter_context(nc.sbuf_tensor(name, shape, dt))

        def sem(name):
            return ctx.enter_context(nc.semaphore(name))

        X = sb("X", [P, SEQS * T, E])
        XnT = sb("XnT", [P, SEQS * LEN])
        U = sb("U", [P, SEQS * T, E])
        xT = sb("xT", [P, 2, LEN])
        stat = sb("stat", [P, T, 6])
        mv = sb("mv", [P, T, 2])
        ve = sb("ve", [P, T])
        rstd = sb("rstd", [P, T])
        nhalf = sb("nhalf", [P, T])
        yn = sb("yn", [P, T, E])
        xa = sb("xa", [P, T, E])
        xn = sb("xn", [P, T, E])

        ident = sb("ident", [P, P])
        tri = sb("tri", [P, P])
        hm = sb("hm", [P, LA_PER_GROUP])
        om = sb("om", [P, LA_PER_GROUP, 32])
        iota = sb("iota", [P, EXPERTS])
        half = sb("half", [2, P])
        rope = sb("rope", [P, T, 2, 2, D])
        la_qkv = sb("la_qkv", [P, 3 * E])
        la_out = sb("la_out", [P, E])
        centT = sb("centT", [P, EXPERTS])
        ebias = sb("ebias", [P, EXPERTS])
        WrT = sb("WrT", [P, EXPERTS * E])
        br = sb("br", [EXPERTS, E])
        WsT = sb("WsT", [P, 2, E])
        Wsh = sb("Wsh", [P, E])
        bs = sb("bs", [2, E])
        gb = sb("gb", [P, 2])
        w_qkv = sb("w_qkv", [P, 3 * INNER])
        w_out = sb("w_out", [P, PAIRS, E])
        w1T = sb("w1T", [P, HID_T * P])
        w2T = sb("w2T", [P, HID_T * P])
        h1T = sb("h1T", [P, HID_T, HID_T * P])
        h2T = sb("h2T", [P, HID_T, HID_T * P])
        w3T = sb("w3T", [P, HID_T, E])
        fs = sb("fs", [P, 4, HID_T])
        s1h = sb("s1h", [P, HID_T])
        s12 = sb("s12", [P, HID_T])
        s3 = sb("s3", [P, E])

        WORK = 2 * (2 * PAIRS * LEN + T * INNER) + 3 * 2 * LEN * 2 + PAIRS * LEN + 6 * BLK + 8 * HEADS
        work = sb("work", [P, WORK])
        top = [0]

        def carve(*shape):
            n = 1
            for s in shape:
                n *= s
            a = work[:, top[0]:top[0] + n]
            top[0] += n
            assert top[0] <= WORK
            names = "abcde"[:len(shape)]
            if len(shape) > 1:
                a = a.rearrange(f"p ({' '.join(names)}) -> p {' '.join(names)}",
                                **{c: s for c, s in zip(names, shape)})
            return a

        bank = [ctx.enter_context(nc.psum_tensor(f"bank{b}", [P, BLK], F32)) for b in range(8)]
        Y = bank[0]
        Yt = Y[:, 0:T * E].rearrange("p (t e) -> p t e", t=T)
        NT = Y[:, 256:256 + LEN]

        s_x = sem("s_x")
        s_const = sem("s_const")
        s_w = [sem(f"s_w{l}") for l in range(LAYERS)]
        s_out = sem("s_out")
        s_nhalf, s_vm, s_wsh, s_fs, b_rch = (sem(n) for n in ("s_nhalf", "s_vm", "s_wsh", "s_fs", "b_rch"))
        x_ready = [sem(f"x_ready{l}") for l in range(LAYERS)]
        a_proj = sem("a_proj")
        y_ready = [sem(f"y_ready{l}") for l in range(LAYERS)]
        n_stats = [sem(f"n_stats{r}") for r in range(5)]
        n_rstd = [sem(f"n_rstd{r}") for r in range(5)]
        n_yn = [sem(f"n_yn{r}") for r in range(5)]
        n_x = [sem(f"n_x{r}") for r in range(5)]
        n_xn = [sem(f"n_xn{r}") for r in range(5)]
        n_u = [sem(f"n_u{r}") for r in range(5)]
        n_tp = [sem(f"n_tp{r}") for r in range(5)]
        n_xnT = [sem(f"n_xnT{r}") for r in range(5)]
        v_chain = [sem(f"v_chain{r}") for r in range(5)]
        p_chain = [sem(f"p_chain{r}") for r in range(5)]

        def reached(count):
            return max(count, 0) if isinstance(count, int) else count

        def wait_apart(eng, s, value, held, held_value):
            if not isinstance(value, int):
                eng.lower_val(value)
            eng.wait_ge(held, held_value)
            eng.wait_ge(s, value)

        def i_is(i, n):
            return isinstance(i, int) and i == n

        class Chain:

            def __init__(self, eng, s, per_step):
                self.eng, self.s, self.n = eng, s, per_step

            def begin(self, i):
                self.i, self.k = i, 0

            def mark(self, ins):
                ins.then_inc(self.s, 1)
                self.k += 1

            def need(self, back=0):
                self.eng.wait_ge(self.s, reached(self.i * self.n + self.k - back))

            def need_apart(self):
                wait_apart(self.eng, self.s, self.i * self.n + self.k, s_x, 64)

            def end(self):
                assert self.k == self.n, (self.k, self.n)

        def over_sequences(eng, step):
            step(0, 0)
            step(1, 1)
            with eng.Fori(1, SEQS // 2 - 1) as j:
                for p in range(2):
                    step(eng.snap(j * 2 + p), p)
            step(SEQS - 2, 0)
            step(SEQS - 1, 1)

        def over_all(eng, step):
            step(0)
            with eng.Fori(1, SEQS) as i:
                step(i)

        def seq_tiles(buf, i):
            return buf[:, bass.ds(i * T, T), :] if not isinstance(i, int) else buf[:, i * T:(i + 1) * T, :]

        def tile_of(buf, i, t):
            return (buf[:, bass.ds(i * T + t, 1), :] if not isinstance(i, int)
                    else buf[:, i * T + t:i * T + t + 1, :])

        def seq_cols(buf, i):
            return buf[:, bass.ds(i * LEN, LEN)] if not isinstance(i, int) else buf[:, i * LEN:(i + 1) * LEN]

        POST = [0, 1, 1, 1, 1]
        PRE = [1, 1, 2, 1, 0]
        ROUNDS = [a + b for a, b in zip(POST, PRE)]

        def norm_vector(dve, r, ch, y_of, y_count=1):
            def stats(i, k, src):
                for t in range(T):
                    ch.mark(nc.vector.bn_stats(stat[:, t, :], src(t)))
                ch.need_apart()
                for t in range(T):
                    ins = nc.vector.bn_aggr(mv[:, t, :], stat[:, t, :])
                ins.then_inc(n_stats[r], 1)

            def post_stats(i, p):
                dve.wait_ge(y_ready[r - 1], (i + 1) * y_count)
                stats(i, 0, lambda t: y_of(p)[:, t, :])

            def post_apply(i, p):
                dve.wait_ge(n_rstd[r], i * ROUNDS[r] + 1)
                dve.wait_ge(n_x[r], reached(i))
                for t in range(T):
                    ins = nc.vector.tensor_scalar(yn[:, t, :], y_of(p)[:, t, :], mv[:, t, 0:1],
                                                  rstd[:, t:t + 1], ALU.subtract, ALU.mult)
                ins.then_inc(n_yn[r], 1)

            def pre_stats(k):
                def piece(i, p):
                    if k == 0:
                        if r:
                            dve.wait_ge(n_x[r], i + 1)
                        stats(i, k, lambda t: tile_of(X, i, t).rearrange("p a e -> p (a e)"))
                    else:
                        ch.need()
                        stats(i, k, lambda t: xa[:, t, :])
                return piece

            def pre_apply(k):
                final = k == PRE[r] - 1

                def piece(i, p):
                    dve.wait_ge(n_rstd[r], i * ROUNDS[r] + POST[r] + k + 1)
                    if final:
                        dve.wait_ge(n_tp[r], reached(i))
                        if r == 1:
                            dve.wait_ge(n_u[r], reached(i))
                    for t in range(T):
                        src = tile_of(X, i, t).rearrange("p a e -> p (a e)") if k == 0 else xa[:, t, :]
                        ins = nc.vector.tensor_scalar((xn if final else xa)[:, t, :], src, mv[:, t, 0:1],
                                                      rstd[:, t:t + 1], ALU.subtract, ALU.mult)
                        if not final:
                            ch.mark(ins)
                    if final:
                        ins.then_inc(n_xn[r], 1)
                return piece

            pieces = [post_stats, post_apply] if POST[r] else []
            for k in range(PRE[r]):
                pieces += [pre_stats(k), pre_apply(k)]
            return pieces

        def norm_marks(r):
            return T * ROUNDS[r] + (T if PRE[r] == 2 else 0)

        def norm_pool(pool, r, i, k):
            wait_apart(pool, n_stats[r], i * ROUNDS[r] + k + 1, s_nhalf, 1)
            nc.gpsimd.tensor_scalar(ve[:, :], mv[:, :, 1], EPS, None, ALU.add).then_inc(p_chain[r], 1)
            pool.wait_ge(p_chain[r], i * ROUNDS[r] + k + 1)
            nc.gpsimd.tensor_tensor(rstd[:, :], ve[:, :], nhalf[:, :], ALU.pow).then_inc(n_rstd[r], 1)
            if k == 0 and POST[r]:
                pool.wait_ge(n_yn[r], i + 1)
                xs = seq_tiles(X, i)
                nc.gpsimd.tensor_tensor(xs, xs, yn[:, :, :], ALU.add).then_inc(n_x[r], 1)
            if k == ROUNDS[r] - 1 and r == 1:
                pool.wait_ge(n_xn[r], i + 1)
                nc.gpsimd.tensor_copy(seq_tiles(U, i), xn[:, :, :]).then_inc(n_u[r], 1)

        def norm_tensor(pe, r, i):
            pe.wait_ge(n_xn[r], i + 1)
            pe.wait_ge(n_xnT[r], reached(i))
            for t in range(T):
                ins = nc.tensor.transpose(NT[:, t * P:(t + 1) * P], xn[:, t, :], ident[:, :])
            ins.then_inc(n_tp[r], 1)

        def norm_scalar(act, r, i):
            act.wait_ge(n_tp[r], i + 1)
            if r == 2:
                ins = nc.scalar.activation(seq_cols(XnT, i), NT, ACT.Identity, bias=gb[:, 1:2], scale=gb[:, 0:1])
            else:
                ins = nc.scalar.activation(seq_cols(XnT, i), NT, ACT.Copy)
            ins.then_inc(n_xnT[r], 1)

        def layer_begins(eng, l):
            eng.wait_ge(n_xnT[l], SEQS)
            if l == 1:
                eng.wait_ge(n_u[1], SEQS)

        def pool_xT(pool, l, i, p):
            last_use, per_seq = ((a_proj, 1), (b_x, UNITS_B), (c_junit, JUNITS), (d_u, 2))[l]
            pool.wait_ge(last_use, reached(per_seq * (i - 1)))
            nc.gpsimd.tensor_copy(xT[:, p, :], seq_cols(XnT, i)).then_inc(x_ready[l], 1)

        top[0] = 0
        neg = carve(BLK)
        ex = carve(BLK)
        qk = carve(2, BLK)
        qblk = carve(2, LA_PER_GROUP, LEN)
        vm = carve(2, T, LA_GROUPS, LA_PER_GROUP, 32)
        vm_all = work[:, top[0] - 2 * T * LA_GROUPS * LA_PER_GROUP * 32:top[0]]
        at0 = carve(2, LA_PER_GROUP, LEN)
        at1 = carve(2, LA_PER_GROUP, P)
        den = carve(LEN)
        rden = carve(LEN)
        oT = carve(LEN)
        QKB, VB, NB, DB = bank[1], bank[2], bank[3], bank[4]
        SC = bank[5:8]
        a_neg, a_exp, a_feat, a_qb, a_vm = (sem(n) for n in ("a_neg", "a_exp", "a_feat", "a_qb", "a_vm"))
        a_s = [sem(f"a_s{k}") for k in range(3)]
        a_m = [sem(f"a_m{k}") for k in range(3)]
        a_nd, a_den, a_rden, a_oT = (sem(n) for n in ("a_nd", "a_den", "a_rden", "a_oT"))
        G4 = LA_GROUPS

        def la_proj_tensor(pe, i, p):
            pe.wait_ge(x_ready[LA], i + 1)
            pe.wait_ge(a_qb, reached(i))
            pe.wait_ge(a_vm, reached(i))
            nc.tensor.matmul(QKB[:, 0:LEN], la_qkv[:, 0:E], xT[:, p, :], start=True, stop=True)
            nc.tensor.matmul(QKB[:, LEN:2 * LEN], la_qkv[:, E:2 * E], xT[:, p, :], start=True, stop=True)
            for t in range(T):
                ins = nc.tensor.matmul(VB[:, t * E:(t + 1) * E], xT[:, p, t * P:(t + 1) * P],
                                       la_qkv[:, 2 * E:3 * E], start=True, stop=True)
            ins.then_inc(a_proj, 1)

        def la_feat_vector(dve, i, p, part):
            if part == 0:
                dve.wait_ge(a_proj, i + 1)
                dve.wait_ge(a_exp, reached(i))
                nc.vector.tensor_scalar(neg, QKB[:, :], 0.0, None, ALU.min).then_inc(a_neg, 1)
            else:
                dve.wait_ge(a_exp, i + 1)
                dve.wait_ge(a_nd, reached(G4 * (i - 1)))
                nc.vector.scalar_tensor_tensor(qk[:, p, :], QKB[:, :], 0.0, ex, ALU.max, ALU.add)\
                    .then_inc(a_feat, 1)
                dve.wait_ge(a_feat, i + 1)
                for j in range(LA_PER_GROUP):
                    ins = nc.vector.tensor_scalar(qblk[:, p, j, :], qk[:, p, 0:LEN], hm[:, j:j + 1], None,
                                                  ALU.mult)
                ins.then_inc(a_qb, 1)

        def la_feat_scalar(act, i, p):
            act.wait_ge(a_neg, i + 1)
            act.wait_ge(a_feat, reached(i))
            nc.scalar.activation(ex, neg, ACT.Exp).then_inc(a_exp, 1)
            act.wait_ge(a_proj, i + 1)
            act.wait_ge(a_nd, reached(G4 * (i - 1)))
            for j in range(LA_PER_GROUP):
                c = slice(j * LA_D, (j + 1) * LA_D)
                ins = nc.scalar.activation(
                    vm[:, p, :, :, j, c].rearrange("p t g c -> p (t g) c"),
                    VB[:, 0:T * E].rearrange("p (a c) -> p a c", c=32)[:, :, c], ACT.Copy)
            ins.then_inc(a_vm, 1)

        def la_scores_tensor(pe, i, p, g):
            n = i * G4 + g
            rows = slice(32 * g, 32 * g + 32)
            for kind, (kt, qt) in enumerate(((0, 0), (0, 1), (1, 1))):
                pe.wait_ge(a_m[kind], reached(n))
                nc.tensor.matmul(SC[kind][:, :], qk[rows, p, LEN + kt * P:LEN + (kt + 1) * P],
                                 qblk[rows, p, :, qt * P:(qt + 1) * P], start=True, stop=True)\
                    .then_inc(a_s[kind], 1)

        def la_sums_tensor(pe, i, p, g):
            n = i * G4 + g
            if g == 0:
                pe.wait_ge(a_oT, reached(i))
                pe.wait_ge(a_vm, i + 1)
            for kind in range(3):
                pe.wait_ge(a_m[kind], n + 1)
            rows = slice(32 * g, 32 * g + 32)
            s = g % 2
            for bank_, of in ((NB, lambda t, j: vm[:, p, t, g, j, :]), (DB, lambda t, j: om[:, j, :])):
                for j in range(LA_PER_GROUP):
                    nc.tensor.matmul(bank_[rows, 0:LEN], of(0, j), at0[:, s, j, :], start=(j == 0), stop=False)
                for j in range(LA_PER_GROUP):
                    ins = nc.tensor.matmul(bank_[rows, P:LEN], of(1, j), at1[:, s, j, :], start=False,
                                           stop=(j == LA_PER_GROUP - 1))
            ins.then_inc(a_nd, 1)

        def la_mask_vector(dve, i, g):
            n = i * G4 + g
            s = g % 2
            tri4 = tri[:, :].rearrange("p (o l) -> p o l", o=1).to_broadcast([P, LA_PER_GROUP, P])
            dve.wait_ge(a_nd, reached(n - 1))
            for kind, dst in ((0, at0[:, s, :, 0:P]), (2, at1[:, s, :, :])):
                dve.wait_ge(a_s[kind], n + 1)
                nc.vector.tensor_tensor(dst, SC[kind][:, :].rearrange("p (j l) -> p j l", j=LA_PER_GROUP),
                                        tri4, ALU.mult).then_inc(a_m[kind], 1)

        def la_copy_scalar(act, i, g):
            n = i * G4 + g
            act.wait_ge(a_nd, reached(n - 1))
            act.wait_ge(a_s[1], n + 1)
            nc.scalar.activation(at0[:, g % 2, :, P:2 * P],
                                 SC[1][:, :].rearrange("p (j l) -> p j l", j=LA_PER_GROUP), ACT.Copy)\
                .then_inc(a_m[1], 1)

        def la_divide_vector(dve, i):
            dve.wait_ge(a_nd, G4 * (i + 1))
            nc.vector.tensor_scalar(den, DB[:, 0:LEN], 1e-6, None, ALU.max).then_inc(a_den, 1)
            dve.wait_ge(a_den, i + 1)
            nc.vector.reciprocal(rden, den).then_inc(a_rden, 1)
            dve.wait_ge(a_rden, i + 1)
            dve.wait_ge(y_ready[LA], reached(i))
            nc.vector.tensor_tensor(oT, NB[:, 0:LEN], rden, ALU.mult).then_inc(a_oT, 1)

        def la_out_tensor(pe, i):
            pe.wait_ge(a_oT, i + 1)
            pe.wait_ge(n_xnT[1], reached(i))
            for t in range(T):
                ins = nc.tensor.matmul(Yt[:, t, :], oT[:, t * P:(t + 1) * P], la_out[:, :], start=True, stop=True)
            ins.then_inc(y_ready[LA], 1)

        top[0] = 0
        zr = carve(T, EXPERTS)
        t8 = carve(T, 8)
        ixf = carve(T, 2)
        nm = carve(T)
        ez = carve(T, EXPERTS)
        zs = carve(T)
        e2 = carve(T, 2)
        rz = carve(T)
        g2 = carve(T, 2)
        oh = carve(2, T, EXPERTS)
        gates = carve(2, T, EXPERTS)
        gT = carve(2, LEN)[0:EXPERTS, :, :]
        acc = carve(2, T, E)
        ix8 = sb("ix8", [P, T, 8], U32)
        RB, SHB = bank[1], bank[2]
        XB = bank[3:7]
        b_z, b_nm, b_e, b_g, b_gt, b_gs, b_sh, b_acc = (
            sem(n) for n in ("b_z", "b_nm", "b_e", "b_g", "b_gt", "b_gs", "b_sh", "b_acc"))
        y_ready[MOE] = b_acc
        b_x = sem("b_x")

        def moe_router_tensor(pe, i, p):
            pe.wait_ge(x_ready[MOE], i + 1)
            pe.wait_ge(b_gs, reached(i))
            for t in range(T):
                ins = nc.tensor.matmul(RB[:, t * EXPERTS:(t + 1) * EXPERTS], xT[:, p, t * P:(t + 1) * P],
                                       centT[:, :], start=True, stop=True)
            ins.then_inc(b_z, 1)

        def moe_gates_tensor(pe, i, p):
            pe.wait_ge(b_g, i + 1)
            for t in range(T):
                ins = nc.tensor.transpose(RB[0:EXPERTS, 256 + t * P:256 + (t + 1) * P], gates[:, p, t, :],
                                          ident[:, :])
            ins.then_inc(b_gt, 1)

        MOE_ROUTER_MARKS = 13

        def moe_router_vector(dve, ch, i, p):
            dve.wait_ge(b_z, i + 1)
            bias = ebias[:, :].rearrange("p (o e) -> p o e", o=1).to_broadcast([P, T, EXPERTS])
            dve.wait_ge(b_e, reached(i))
            ch.mark(nc.vector.tensor_tensor(zr, RB[:, 0:T * EXPERTS].rearrange("p (t e) -> p t e", t=T), bias,
                                            ALU.add))
            ch.need_apart()
            for t in range(T):
                ch.mark(nc.vector.max(t8[:, t, :], zr[:, t, :]))
            ch.need_apart()
            for t in range(T):
                ch.mark(nc.vector.max_index(ix8[:, t, :], t8[:, t, :], zr[:, t, :]))
            nc.vector.tensor_scalar(nm, t8[:, :, 0], -1.0, None, ALU.mult).then_inc(b_nm, 1)
            ch.need()
            ch.mark(nc.vector.tensor_copy(ixf, ix8[:, :, 0:2]))
            dve.wait_ge(b_e, i + 1)
            ch.mark(nc.vector.reciprocal(rz, zs))
            ch.need()
            for t in range(T):
                ch.mark(nc.vector.tensor_scalar(g2[:, t, :], e2[:, t, :], rz[:, t:t + 1], None, ALU.mult))
            ch.need()
            for t in range(T):
                for k in range(2):
                    ch.mark(nc.vector.tensor_scalar(oh[:, k, t, :], iota[:, :], ixf[:, t, k:k + 1],
                                                    g2[:, t, k:k + 1], ALU.is_equal, ALU.mult))
            ch.need()
            dve.wait_ge(b_gt, reached(i - 1))
            nc.vector.tensor_tensor(gates[:, p, :, :], oh[:, 0, :, :], oh[:, 1, :, :], ALU.add).then_inc(b_g, 1)

        def moe_router_scalar(act, i, p):
            act.wait_ge(b_nm, i + 1)
            act.wait_ge(b_g, reached(i))
            for t in range(T):
                nc.scalar.activation(ez[:, t, :], zr[:, t, :], ACT.Exp, bias=nm[:, t:t + 1],
                                     accum_out=zs[:, t:t + 1])
            for t in range(T):
                ins = nc.scalar.activation(e2[:, t, :], t8[:, t, 0:2], ACT.Exp, bias=nm[:, t:t + 1])
            ins.then_inc(b_e, 1)

        def moe_gates_scalar(act, i, p):
            act.wait_ge(b_gt, i + 1)
            act.wait_ge(b_sh, reached(i - 1))
            nc.scalar.activation(gT[:, p, :], RB[0:EXPERTS, 256:256 + LEN], ACT.Copy).then_inc(b_gs, 1)

        def moe_shared_tensor(pe, i, p):
            pe.wait_ge(b_gs, i + 1)
            pe.wait_ge(b_acc, reached(i * T * (EXPERTS + 1) - T * EXPERTS))
            for t in range(T):
                o = SHB[:, t * E:(t + 1) * E]
                nc.tensor.matmul(o, xT[:, p, t * P:(t + 1) * P], Wsh[:, :], start=True, stop=False)
                nc.tensor.matmul(o, gT[:, p, t * P:(t + 1) * P], br[:, :], start=False, stop=False)
                ins = nc.tensor.matmul(o, half[:, :], bs[:, :], start=False, stop=True)
            ins.then_inc(b_sh, 1)

        def moe_unit_tensor(pe, i, p, u):
            t, b = u % T, u // T
            back, e = (0, (b - 1) * PER_BANK - 1) if b >= 2 else (1, (b + 3) * PER_BANK - 1)
            pe.wait_ge(b_acc, reached((i - back) * T * (EXPERTS + 1) + T * (e + 1) + t + 1))
            ins = nc.tensor.matmul(XB[u % 4][:, :], xT[:, p, t * P:(t + 1) * P], WrT[:, b * BLK:(b + 1) * BLK],
                                   start=True, stop=True)
            ins.then_inc(b_x, 1)

        def moe_start_vector(dve, i, p):
            dve.wait_ge(b_sh, i + 1)
            for t in range(T):
                nc.vector.tensor_tensor(acc[:, p, t, :], SHB[:, t * E:(t + 1) * E],
                                        tile_of(U, i, t).rearrange("p a e -> p (a e)"), ALU.add)\
                    .then_inc(b_acc, 1)

        def moe_units_vector(dve, i, p, b):
            for t in range(T):
                dve.wait_ge(b_x, i * UNITS_B + b * T + t + 1)
            for k in range(PER_BANK):
                e = b * PER_BANK + k
                for t in range(T):
                    u = b * T + t
                    dve.wait_ge(b_acc, reached(i * T * (EXPERTS + 1) + T * (e + 1) + t - 1))
                    ins = nc.vector.scalar_tensor_tensor(
                        acc[:, p, t, :], XB[u % 4][:, k * E:(k + 1) * E], gates[:, p, t, e:e + 1],
                        acc[:, p, t, :], ALU.mult, ALU.add)
                    ins.then_inc(b_acc, 1)

        top[0] = 0
        QT = carve(2, PAIRS, LEN)
        KT = carve(2, PAIRS, LEN)
        V = carve(2, T, INNER)
        pr = carve(2, T, LEN)
        pn = carve(2, T, LEN)
        pT = carve(2, T, LEN)
        oTs = carve(PAIRS, LEN)
        rc = carve(2, BLK)
        rs_ = carve(2, BLK)
        rq = carve(2, BLK)
        nmax = carve(HEADS, T)
        psum_ = carve(HEADS, T)
        prec = carve(HEADS, T)
        SB_, PB, OB, JB = bank[1:3], bank[3:5], bank[5], bank[6:8]
        c_s, c_max, c_exp, c_rec, c_pn, c_t, c_pte, c_v, c_oe = (
            sem(n) for n in ("c_s", "c_max", "c_exp", "c_rec", "c_pn", "c_t", "c_pte", "c_v", "c_oe"))
        c_junit = sem("c_junit")
        c_jv = sem("c_jv")
        c_js = sem("c_js")
        c_mul = sem("c_mul")
        c_rope = sem("c_rope")

        slots = [[] for _ in range(HEADS)]
        for t in range(T):
            for b in range(BLOCKS):
                slots[t * BLOCKS + b].append(("rope" if b < 4 else "v", t, b))
                if b < 4:
                    slots[t * BLOCKS + b + 3].append(("turn", t, b))
        order = [u for s in slots for u in s]
        JUNITS = len(order)
        place = {u: k for k, u in enumerate(order)}
        ROPES, TURNS = 4 * T, JUNITS - 4 * T

        def jcount(k, kinds):
            whole = sum(u[0] in kinds for u in order)
            return (k // JUNITS) * whole + sum(u[0] in kinds for u in order[:k % JUNITS])

        def sa_unit_tensor(pe, i, p, unit):
            kind, t, b = unit
            k = place[unit]
            bank_ = JB[k % 2]
            if order[(k - 2) % JUNITS][0] == "rope":
                pe.wait_ge(c_jv, reached(i * ROPES + jcount(k - 1, ("rope",))))
            else:
                pe.wait_ge(c_js, reached(i * TURNS + jcount(k - 1, ("v", "turn"))))
            if kind == "turn":
                pe.wait_ge(c_rope, i * ROPES + 4 * t + b + 1)
                for q in range(4):
                    ins = nc.tensor.transpose(bank_[:, q * P:(q + 1) * P], rq[:, b % 2, q * P:(q + 1) * P],
                                              ident[:, :])
            else:
                if k == 0:
                    pe.wait_ge(x_ready[SA], i + 1)
                ins = nc.tensor.matmul(bank_[:, :], xT[:, p, t * P:(t + 1) * P], w_qkv[:, b * BLK:(b + 1) * BLK],
                                       start=True, stop=True)
            ins.then_inc(c_junit, 1)

        def sa_unit_vector(dve, i, p, unit):
            kind, t, b = unit
            if kind != "rope":
                return
            k = place[unit]
            ru = 4 * t + b
            dve.wait_ge(c_junit, i * JUNITS + k + 1)
            dve.wait_ge(c_rope, reached(i * ROPES + ru - 1))
            src = JB[k % 2][:, :].rearrange("p (h s d) -> p h s d", s=2, d=D // 2)

            def table(m):
                return rope[:, t, b // 2, m, :].rearrange("p (o s d) -> p o s d", o=1, s=2)\
                    .to_broadcast([P, BLK // D, 2, D // 2])
            dst = [a[:, b % 2, :].rearrange("p (h s d) -> p h s d", s=2, d=D // 2) for a in (rc, rs_)]
            nc.vector.tensor_tensor(dst[0], src, table(0), ALU.mult)
            nc.vector.tensor_tensor(dst[1], src[:, :, ::-1, :], table(1), ALU.mult).then_inc(c_jv, 1)

        def sa_unit_pool(pool, i, p, unit):
            kind, t, b = unit
            if kind != "rope":
                return
            ru = 4 * t + b
            pool.wait_ge(c_jv, i * ROPES + ru + 1)
            before = ("turn", t, b - 2) if b >= 2 else ("turn", (t - 1) % T, b + 2)
            back = 0 if b >= 2 or t > 0 else 1
            pool.wait_ge(c_junit, reached((i - back) * JUNITS + place[before] + 1))
            nc.gpsimd.tensor_tensor(rq[:, b % 2, :], rc[:, b % 2, :], rs_[:, b % 2, :], ALU.add)\
                .then_inc(c_rope, 1)

        def sa_unit_scalar(act, i, p, unit):
            kind, t, b = unit
            if kind == "rope":
                return
            k = place[unit]
            act.wait_ge(c_junit, i * JUNITS + k + 1)
            bank_ = JB[k % 2]
            if kind == "v":
                dst = V[:, p, t, (b - 4) * BLK:(b - 3) * BLK]
                src = bank_[:, :]
            else:
                dst = (QT if b < 2 else KT)[:, p, 4 * (b % 2):4 * (b % 2) + 4, t * P:(t + 1) * P]
                src = bank_[:, :].rearrange("p (q l) -> p q l", q=4)
            nc.scalar.activation(dst, src, ACT.Copy).then_inc(c_js, 1)

        def sa_scores_tensor(pe, i, p, h):
            n = i * HEADS + h
            if h == 0:
                pe.wait_ge(c_js, (i + 1) * TURNS)
            pe.wait_ge(c_exp, reached(n - 1))
            rows = slice(D * (h % 2), D * (h % 2) + D)
            for t in range(T):
                ins = nc.tensor.matmul(SB_[h % 2][:, t * LEN:(t + 1) * LEN], QT[rows, p, h // 2, t * P:(t + 1) * P],
                                       KT[rows, p, h // 2, :], start=True, stop=True)
            ins.then_inc(c_s, 1)

        def sa_max_vector(dve, i, h):
            n = i * HEADS + h
            dve.wait_ge(c_s, n + 1)
            if h == 0:
                dve.wait_ge(c_exp, reached(n))
            nc.vector.tensor_reduce(nmax[:, h, :], SB_[h % 2][:, :].rearrange("p (t k) -> p t k", t=T),
                                    AX.X, ALU.max, negate=True).then_inc(c_max, 1)

        def sa_exp_scalar(act, i, h):
            n = i * HEADS + h
            act.wait_ge(c_max, n + 1)
            act.wait_ge(c_pn, reached(n - 1))
            for t in range(T):
                ins = nc.scalar.activation(pr[:, h % 2, t, :], SB_[h % 2][:, t * LEN:(t + 1) * LEN], ACT.Exp,
                                           bias=nmax[:, h, t:t + 1], accum_out=psum_[:, h, t:t + 1])
            ins.then_inc(c_exp, 1)

        def sa_norm_vector(dve, i, h):
            n = i * HEADS + h
            dve.wait_ge(c_exp, n + 1)
            nc.vector.reciprocal(prec[:, h, :], psum_[:, h, :]).then_inc(c_rec, 1)
            dve.wait_ge(c_rec, n + 1)
            dve.wait_ge(c_t, reached(n - 1))
            for t in range(T):
                ins = nc.vector.tensor_scalar(pn[:, h % 2, t, :], pr[:, h % 2, t, :], prec[:, h, t:t + 1], None,
                                              ALU.mult)
            ins.then_inc(c_pn, 1)

        def sa_turn_tensor(pe, i, h):
            n = i * HEADS + h
            pe.wait_ge(c_pn, n + 1)
            pe.wait_ge(c_pte, reached(n - 1))
            for kt in range(T):
                for t in range(T):
                    ins = nc.tensor.transpose(PB[h % 2][:, kt * LEN + t * P:kt * LEN + (t + 1) * P],
                                              pn[:, h % 2, t, kt * P:(kt + 1) * P], ident[:, :])
            ins.then_inc(c_t, 1)

        def sa_turn_scalar(act, i, h):
            n = i * HEADS + h
            act.wait_ge(c_t, n + 1)
            act.wait_ge(c_v, reached(n - 1))
            nc.scalar.activation(pT[:, h % 2, :, :], PB[h % 2][:, :].rearrange("p (t q) -> p t q", t=T), ACT.Copy)\
                .then_inc(c_pte, 1)

        def sa_pv_tensor(pe, i, p, h):
            n = i * HEADS + h
            pe.wait_ge(c_pte, n + 1)
            if h % 2 == 0:
                pe.wait_ge(c_oe, reached(i * PAIRS + h // 2))
            rows = slice(D * (h % 2), D * (h % 2) + D)
            for kt in range(T):
                ins = nc.tensor.matmul(OB[rows, 0:LEN], V[:, p, kt, h * D:(h + 1) * D], pT[:, h % 2, kt, :],
                                       start=(kt == 0), stop=(kt == T - 1))
            ins.then_inc(c_v, 1)

        def sa_pv_scalar(act, i, h):
            act.wait_ge(c_v, i * HEADS + h + 1)
            act.wait_ge(y_ready[SA], reached(i))
            nc.scalar.activation(oTs[:, h // 2, :], OB[:, 0:LEN], ACT.Copy).then_inc(c_oe, 1)

        def sa_out_tensor(pe, i):
            pe.wait_ge(c_oe, (i + 1) * PAIRS)
            pe.wait_ge(n_xnT[3], reached(i))
            for t in range(T):
                for q in range(PAIRS):
                    ins = nc.tensor.matmul(Yt[:, t, :], oTs[:, q, t * P:(t + 1) * P], w_out[:, q, :],
                                           start=(q == 0), stop=(q == PAIRS - 1))
            ins.then_inc(y_ready[SA], 1)

        SA_PIECE_SLOTS = (1, 3, 5, 7)
        SA_ROUND_SLOTS = (1, 5)

        top[0] = 0
        tg = carve(2, 2, LEN)
        gg = carve(2, 2, LEN)
        hT = carve(2, HID_T, LEN)
        f1 = carve(HID_T, LEN)
        f2 = carve(HID_T, LEN)
        yf = carve(2, T, E)
        GB, UB = (bank[1], bank[3]), (bank[2], bank[4])
        HB = bank[5:7]
        d_g, d_u, d_tanh, d_gg, d_h, d_m1, d_a1, d_m2, d_a2, d_y = (
            sem(n) for n in ("d_g", "d_u", "d_tanh", "d_gg", "d_h", "d_m1", "d_a1", "d_m2", "d_a2", "d_y"))

        def ffn_in_tensor(pe, i, p):
            pe.wait_ge(x_ready[FFN], i + 1)
            for m in range(2):
                for banks, wT, done, empty in ((GB, w1T, d_g, d_gg), (UB, w2T, d_u, d_h)):
                    pe.wait_ge(empty, reached(2 * (i - 1) + m + 1))
                    for k in range(2):
                        ob = 2 * m + k
                        ins = nc.tensor.matmul(banks[m][:, k * LEN:(k + 1) * LEN], wT[:, ob * P:(ob + 1) * P],
                                               xT[:, p, :], start=True, stop=True)
                    ins.then_inc(done, 1)

        def ffn_in_scalar(act, i):
            for m in range(2):
                act.wait_ge(d_g, 2 * i + m + 1)
                act.wait_ge(d_gg, reached(2 * (i - 1) + m + 1))
                for k in range(2):
                    ob = 2 * m + k
                    ins = nc.scalar.activation(tg[:, m, k, :], GB[m][:, k * LEN:(k + 1) * LEN], ACT.Tanh,
                                               scale=s1h[:, ob:ob + 1])
                ins.then_inc(d_tanh, 1)

        def ffn_in_vector(dve, i, p):
            for m in range(2):
                dve.wait_ge(d_tanh, 2 * i + m + 1)
                dve.wait_ge(d_h, reached(2 * (i - 1) + m + 1))
                nc.vector.scalar_tensor_tensor(gg[:, m, :, :].rearrange("p k l -> p (k l)"),
                                               tg[:, m, :, :].rearrange("p k l -> p (k l)"), 1.0, GB[m][:, :],
                                               ALU.add, ALU.mult).then_inc(d_gg, 1)
                dve.wait_ge(d_gg, 2 * i + m + 1)
                dve.wait_ge(d_u, 2 * i + m + 1)
                if m == 0:
                    dve.wait_ge(d_m1, reached(2 * (i - 1)))
                for k in range(2):
                    ob = 2 * m + k
                    ins = nc.vector.scalar_tensor_tensor(hT[:, p, ob, :], UB[m][:, k * LEN:(k + 1) * LEN],
                                                         s12[:, ob:ob + 1], gg[:, m, k, :], ALU.mult, ALU.mult)
                ins.then_inc(d_h, 1)

        def ffn_product(pe, src, wT, written, emptied, base):
            for m in range(2):
                pe.wait_ge(emptied, reached(base + m + 1))
                for k in range(2):
                    ob = 2 * m + k
                    for kb in range(HID_T):
                        ins = nc.tensor.matmul(HB[m][:, k * LEN:(k + 1) * LEN],
                                               wT[:, kb, ob * P:(ob + 1) * P], src[:, kb, :],
                                               start=(kb == 0), stop=(kb == HID_T - 1))
                ins.then_inc(written, 1)

        block = ctx.enter_context(nc.Block())

        @block.sync
        def _(sp):
            xv = x.rearrange("b (t p) e -> p (b t) e", p=P)
            ov = out.rearrange("b (t p) e -> p (b t) e", p=P)
            sp.dma_start(X[:, 0:8, :], xv[:, 0:8, :]).then_inc(s_x, 16)
            for name, dst in (("ident", ident), ("tri", tri), ("hm", hm), ("om", om), ("iota", iota),
                              ("half", half), ("rope", rope)):
                sp.dma_start(dst[:], const[name]).then_inc(s_const, 16)
            sp.dma_start(la_qkv[:, :], w["L0_attn_W_qkv"]).then_inc(s_w[LA], 16)
            sp.dma_start(la_out[:, :], w["L0_attn_W_out"]).then_inc(s_w[LA], 16)
            for c in range(1, 4):
                sp.dma_start(X[:, 8 * c:8 * c + 8, :], xv[:, 8 * c:8 * c + 8, :]).then_inc(s_x, 16)
            for dst, src in ((centT[:, :], w["L0_ffn_centroids"]), (WrT[:, :], w["L0_ffn_Wr"]),
                             (br[:, :], w["L0_ffn_br"]), (WsT[:, :, :], w["L0_ffn_Ws"]), (bs[:, :], w["L0_ffn_bs"]),
                             (ebias[:, :], w["L0_ffn_expert_biases"].to_broadcast([P, EXPERTS]))):
                sp.dma_start(dst, src).then_inc(s_w[MOE], 16)
            for dst, src in ((gb[:, 0:1], w["L1_attn_ln_gamma"]), (gb[:, 1:2], w["L1_attn_ln_beta"]),
                             (w_qkv[:, :], w["L1_attn_w_qkv"]),
                             (w_out[:, :, :], w["L1_attn_w_out"].rearrange("(q p) e -> p q e", p=P))):
                sp.dma_start(dst, src).then_inc(s_w[SA], 16)
            for dst, src in ((w1T[:, :], w["L1_ffn_w1_w"]), (w2T[:, :], w["L1_ffn_w2_w"]),
                             (h1T[:, :, :], w["L1_ffn_h1_w"].rearrange("(k p) o -> p k o", p=P)),
                             (h2T[:, :, :], w["L1_ffn_h2_w"].rearrange("(k p) o -> p k o", p=P)),
                             (w3T[:, :, :], w["L1_ffn_w3_w"].rearrange("(k p) o -> p k o", p=P)),
                             (fs[:, :, :], w["L1_ffn_scales"]),
                             (s3[:, :], w["L1_ffn_w3_s"].to_broadcast([P, E]))):
                sp.dma_start(dst, src).then_inc(s_w[FFN], 16)
            with sp.Fori(0, SEQS) as i:
                sp.wait_ge(n_x[4], i + 1)
                sp.dma_start(ov[:, bass.ds(i * T, T), :], X[:, bass.ds(i * T, T), :]).then_inc(s_out, 16)
            sp.wait_ge(s_out, 16 * SEQS)

        @block.gpsimd
        def _(pool):
            nc.gpsimd.memset(nhalf[:, :], -0.5).then_inc(s_nhalf, 1)
            pool.wait_ge(s_nhalf, 1)
            over_all(pool, lambda i: norm_pool(pool, 0, i, 0))

            pool.wait_ge(n_xnT[0], SEQS)
            pool_xT(pool, LA, 0, 0)

            def la_step(i, p):
                if not (i_is(i, SEQS - 1)):
                    pool_xT(pool, LA, i + 1, 1 - p)
                if not (i_is(i, 0)):
                    for k in range(ROUNDS[1]):
                        norm_pool(pool, 1, i - 1, k)
            over_sequences(pool, la_step)
            for k in range(ROUNDS[1]):
                norm_pool(pool, 1, SEQS - 1, k)

            layer_begins(pool, MOE)
            pool_xT(pool, MOE, 0, 0)

            def moe_step(i, p):
                if not (i_is(i, SEQS - 1)):
                    pool_xT(pool, MOE, i + 1, 1 - p)
                if not (i_is(i, 0)):
                    for k in range(ROUNDS[2]):
                        norm_pool(pool, 2, i - 1, k)
            over_sequences(pool, moe_step)
            for k in range(ROUNDS[2]):
                norm_pool(pool, 2, SEQS - 1, k)

            layer_begins(pool, SA)
            pool_xT(pool, SA, 0, 0)
            for u in order:
                sa_unit_pool(pool, 0, 0, u)

            def sa_step(i, p):
                more = not (i_is(i, SEQS - 1))
                if more:
                    pool_xT(pool, SA, i + 1, 1 - p)
                for h in range(HEADS):
                    if more:
                        for u in slots[h]:
                            sa_unit_pool(pool, i + 1, 1 - p, u)
                    if h in SA_ROUND_SLOTS and not (i_is(i, 0)):
                        norm_pool(pool, 3, i - 1, SA_ROUND_SLOTS.index(h))
            over_sequences(pool, sa_step)
            for k in range(ROUNDS[3]):
                norm_pool(pool, 3, SEQS - 1, k)

            layer_begins(pool, FFN)
            pool_xT(pool, FFN, 0, 0)

            def ffn_step(i, p):
                if not (i_is(i, SEQS - 1)):
                    pool_xT(pool, FFN, i + 1, 1 - p)
                if not (i_is(i, 0)):
                    norm_pool(pool, 4, i - 1, 0)
            over_sequences(pool, ffn_step)
            norm_pool(pool, 4, SEQS - 1, 0)

        @block.vector
        def _(dve):
            chains = [Chain(dve, v_chain[r], n) for r, n in enumerate(
                (norm_marks(0), norm_marks(1), norm_marks(2), norm_marks(3), norm_marks(4)))]

            def run_piece(r, pieces, k, i, p):
                ch = chains[r]
                if k == 0:
                    ch.begin(i)
                pieces[k](i, p)
                if k == len(pieces) - 1:
                    ch.end()

            nc.vector.memset(vm_all, 0.0).then_inc(s_vm, 1)
            pieces = norm_vector(dve, 0, chains[0], None)
            dve.wait_ge(s_x, 64)
            over_all(dve, lambda i: [run_piece(0, pieces, k, i, 0) for k in range(len(pieces))])

            dve.wait_ge(s_const, 16 * 7)
            for part in range(2):
                la_feat_vector(dve, 0, 0, part)
            n1 = norm_vector(dve, 1, chains[1], lambda p: Yt)

            def la_step(i, p):
                more = not (i_is(i, SEQS - 1))
                lag = not (i_is(i, 0))
                for g in range(LA_GROUPS):
                    la_mask_vector(dve, i, g)
                    if more and g >= 2:
                        la_feat_vector(dve, i + 1, 1 - p, g - 2)
                    if lag:
                        run_piece(1, n1, g, i - 1, 1 - p)
                la_divide_vector(dve, i)
            over_sequences(dve, la_step)
            for k in range(len(n1)):
                run_piece(1, n1, k, SEQS - 1, 1)

            layer_begins(dve, MOE)
            dve.wait_ge(s_w[MOE], 16 * 6)
            nc.vector.tensor_tensor(Wsh[:, :], WsT[:, 0, :], WsT[:, 1, :], ALU.add).then_inc(s_wsh, 1)
            dve.wait_ge(s_wsh, 1)
            nc.vector.tensor_scalar(Wsh[:, :], Wsh[:, :], 0.5, None, ALU.mult).then_inc(s_wsh, 1)
            rch = Chain(dve, b_rch, MOE_ROUTER_MARKS)

            def router(i, p):
                rch.begin(i)
                moe_router_vector(dve, rch, i, p)
                rch.end()
            router(0, 0)
            n2 = norm_vector(dve, 2, chains[2], lambda p: acc[:, p, :, :], T * (EXPERTS + 1))

            def moe_step(i, p):
                moe_start_vector(dve, i, p)
                for b in range(EXPERTS // PER_BANK):
                    moe_units_vector(dve, i, p, b)
                    if b == 1 and not (i_is(i, SEQS - 1)):
                        router(i + 1, 1 - p)
                    if not (i_is(i, 0)):
                        run_piece(2, n2, b, i - 1, 1 - p)
                if not (i_is(i, 0)):
                    run_piece(2, n2, 4, i - 1, 1 - p)
                    run_piece(2, n2, 5, i - 1, 1 - p)
            over_sequences(dve, moe_step)
            for k in range(len(n2)):
                run_piece(2, n2, k, SEQS - 1, 1)

            layer_begins(dve, SA)
            for u in order:
                sa_unit_vector(dve, 0, 0, u)
            n3 = norm_vector(dve, 3, chains[3], lambda p: Yt)

            def sa_step(i, p):
                more = not (i_is(i, SEQS - 1))
                lag = not (i_is(i, 0))
                for h in range(HEADS + 1):
                    if h < HEADS:
                        sa_max_vector(dve, i, h)
                    if h >= 1:
                        sa_norm_vector(dve, i, h - 1)
                    if h < HEADS and more:
                        for u in slots[h]:
                            sa_unit_vector(dve, i + 1, 1 - p, u)
                    if lag and h in SA_PIECE_SLOTS:
                        run_piece(3, n3, SA_PIECE_SLOTS.index(h), i - 1, 1 - p)
            over_sequences(dve, sa_step)
            for k in range(len(n3)):
                run_piece(3, n3, k, SEQS - 1, 1)

            layer_begins(dve, FFN)
            dve.wait_ge(s_w[FFN], 16 * 7)
            nc.vector.tensor_scalar(s1h[:, :], fs[:, 0, :], 0.5, None, ALU.mult).then_inc(s_fs, 1)
            dve.wait_ge(s_fs, 1)
            nc.vector.tensor_tensor(s12[:, :], s1h[:, :], fs[:, 1, :], ALU.mult).then_inc(s_fs, 1)
            dve.wait_ge(s_fs, 2)
            ffn_in_vector(dve, 0, 0)
            n4 = norm_vector(dve, 4, chains[4], lambda p: yf[:, p, :, :])

            def ffn_step(i, p):
                if not (i_is(i, 0)):
                    for k in range(len(n4)):
                        run_piece(4, n4, k, i - 1, 1 - p)
                if not (i_is(i, SEQS - 1)):
                    ffn_in_vector(dve, i + 1, 1 - p)
                dve.wait_ge(d_y, i + 1)
                nc.vector.tensor_tensor(
                    yf[:, p, :, :], Yt,
                    s3[:, :].rearrange("p (o e) -> p o e", o=1).to_broadcast([P, T, E]), ALU.mult)\
                    .then_inc(y_ready[FFN], 1)
            over_sequences(dve, ffn_step)
            for k in range(len(n4)):
                run_piece(4, n4, k, SEQS - 1, 1)

        @block.scalar
        def _(act):
            over_all(act, lambda i: norm_scalar(act, 0, i))

            act.wait_ge(s_vm, 1)
            la_feat_scalar(act, 0, 0)

            def la_step(i, p):
                for g in range(LA_GROUPS):
                    la_copy_scalar(act, i, g)
                    if g == 2 and not (i_is(i, SEQS - 1)):
                        la_feat_scalar(act, i + 1, 1 - p)
                if not (i_is(i, 0)):
                    norm_scalar(act, 1, i - 1)
            over_sequences(act, la_step)
            norm_scalar(act, 1, SEQS - 1)

            layer_begins(act, MOE)
            act.wait_ge(s_w[SA], 16 * 4)
            moe_router_scalar(act, 0, 0)
            moe_gates_scalar(act, 0, 0)

            def moe_step(i, p):
                if not (i_is(i, SEQS - 1)):
                    moe_router_scalar(act, i + 1, 1 - p)
                    moe_gates_scalar(act, i + 1, 1 - p)
                if not (i_is(i, 0)):
                    norm_scalar(act, 2, i - 1)
            over_sequences(act, moe_step)
            norm_scalar(act, 2, SEQS - 1)

            layer_begins(act, SA)
            for u in order:
                sa_unit_scalar(act, 0, 0, u)

            def sa_step(i, p):
                for h in range(HEADS + 2):
                    if h < HEADS:
                        sa_exp_scalar(act, i, h)
                        if not (i_is(i, SEQS - 1)):
                            for u in slots[h]:
                                sa_unit_scalar(act, i + 1, 1 - p, u)
                    if 1 <= h <= HEADS:
                        sa_turn_scalar(act, i, h - 1)
                    if h >= 2 and (h - 2) % 2 == 1:
                        sa_pv_scalar(act, i, h - 2)
                if not (i_is(i, 0)):
                    norm_scalar(act, 3, i - 1)
            over_sequences(act, sa_step)
            norm_scalar(act, 3, SEQS - 1)

            layer_begins(act, FFN)
            act.wait_ge(s_fs, 2)
            ffn_in_scalar(act, 0)

            def gelu(i, product, dst, written, done):
                for m in range(2):
                    act.wait_ge(written, 2 * i + m + 1)
                    for k in range(2):
                        ob = 2 * m + k
                        ins = nc.scalar.activation(dst[:, ob, :], HB[m][:, k * LEN:(k + 1) * LEN], ACT.Gelu,
                                                   scale=fs[:, 2 + product, ob:ob + 1])
                    ins.then_inc(done, 1)

            def ffn_step(i, p):
                act.wait_ge(d_m2, reached(2 * i))
                gelu(i, 0, f1, d_m1, d_a1)
                if not (i_is(i, SEQS - 1)):
                    ffn_in_scalar(act, i + 1)
                act.wait_ge(d_y, reached(i))
                gelu(i, 1, f2, d_m2, d_a2)
            over_sequences(act, ffn_step)

        @block.tensor
        def _(pe):
            pe.wait_ge(s_const, 16 * 7)
            over_all(pe, lambda i: norm_tensor(pe, 0, i))

            pe.wait_ge(s_w[LA], 32)
            la_proj_tensor(pe, 0, 0)

            def la_step(i, p):
                pe.wait_ge(a_qb, i + 1)
                for g in range(LA_GROUPS + 1):
                    if g < LA_GROUPS:
                        la_scores_tensor(pe, i, p, g)
                    if g >= 1:
                        la_sums_tensor(pe, i, p, g - 1)
                    if g == 2 and not (i_is(i, SEQS - 1)):
                        la_proj_tensor(pe, i + 1, 1 - p)
                if not (i_is(i, 0)):
                    norm_tensor(pe, 1, i - 1)
                la_out_tensor(pe, i)
            over_sequences(pe, la_step)
            norm_tensor(pe, 1, SEQS - 1)

            layer_begins(pe, MOE)
            pe.wait_ge(s_w[MOE], 16 * 6)
            pe.wait_ge(s_wsh, 2)
            moe_router_tensor(pe, 0, 0)
            moe_gates_tensor(pe, 0, 0)

            def moe_step(i, p):
                moe_shared_tensor(pe, i, p)
                for u in range(UNITS_B):
                    moe_unit_tensor(pe, i, p, u)
                    if u == 3 and not (i_is(i, SEQS - 1)):
                        moe_router_tensor(pe, i + 1, 1 - p)
                    if u == UNITS_B - 1 and not (i_is(i, SEQS - 1)):
                        moe_gates_tensor(pe, i + 1, 1 - p)
                if not (i_is(i, 0)):
                    norm_tensor(pe, 2, i - 1)
            over_sequences(pe, moe_step)
            norm_tensor(pe, 2, SEQS - 1)

            layer_begins(pe, SA)
            pe.wait_ge(s_w[SA], 16 * 4)
            for u in order:
                sa_unit_tensor(pe, 0, 0, u)

            def sa_step(i, p):
                for h in range(HEADS + 2):
                    if h < HEADS:
                        sa_scores_tensor(pe, i, p, h)
                        if not (i_is(i, SEQS - 1)):
                            for u in slots[h]:
                                sa_unit_tensor(pe, i + 1, 1 - p, u)
                    if 1 <= h <= HEADS:
                        sa_turn_tensor(pe, i, h - 1)
                    if h >= 2:
                        sa_pv_tensor(pe, i, p, h - 2)
                if not (i_is(i, 0)):
                    norm_tensor(pe, 3, i - 1)
                sa_out_tensor(pe, i)
            over_sequences(pe, sa_step)
            norm_tensor(pe, 3, SEQS - 1)

            layer_begins(pe, FFN)
            pe.wait_ge(s_w[FFN], 16 * 7)
            ffn_in_tensor(pe, 0, 0)

            def ffn_step(i, p):
                pe.wait_ge(d_h, 2 * (i + 1))
                ffn_product(pe, hT[:, p, :, :], h1T, d_m1, d_a2, 2 * (i - 1))
                if not (i_is(i, SEQS - 1)):
                    ffn_in_tensor(pe, i + 1, 1 - p)
                pe.wait_ge(d_a1, 2 * (i + 1))
                ffn_product(pe, f1, h2T, d_m2, d_a1, 2 * i)
                pe.wait_ge(d_a2, 2 * (i + 1))
                pe.wait_ge(y_ready[FFN], reached(i))
                for t in range(T):
                    for kb in range(HID_T):
                        ins = nc.tensor.matmul(Yt[:, t, :], f2[:, kb, t * P:(t + 1) * P], w3T[:, kb, :],
                                               start=(kb == 0), stop=(kb == HID_T - 1))
                ins.then_inc(d_y, 1)

            over_sequences(pe, ffn_step)


_WEIGHTS = {
    "L0_attn_W_qkv": lambda a: a.T,
    "L0_attn_W_out": lambda a: a.T,
    "L0_ffn_centroids": lambda a: a.T,
    "L0_ffn_expert_biases": lambda a: a[None, :],
    "L0_ffn_Wr": lambda a: a.transpose(2, 0, 1).reshape(a.shape[2], -1),
    "L0_ffn_br": lambda a: a,
    "L0_ffn_Ws": lambda a: a.transpose(2, 0, 1),
    "L0_ffn_bs": lambda a: a,
    "L1_attn_ln_gamma": lambda a: a[:, None],
    "L1_attn_ln_beta": lambda a: a[:, None],
    "L1_attn_w_qkv": lambda a: a,
    "L1_attn_w_out": lambda a: a,
    "L1_ffn_w1_w": lambda a: a.T,
    "L1_ffn_w2_w": lambda a: a.T,
    "L1_ffn_h1_w": lambda a: a.T,
    "L1_ffn_h2_w": lambda a: a.T,
    "L1_ffn_w3_w": lambda a: a.T,
    "L1_ffn_w3_s": lambda a: a[None, :],
}


def _constants(np):
    f = np.float32
    p = np.arange(128)
    c = {"ident": np.eye(128, dtype=f)}
    c["tri"] = (p[:, None] <= p[None, :]).astype(f)
    j = np.arange(4)
    c["hm"] = ((p[:, None] % 32) // 8 == j[None, :]).astype(f) * f(8 ** -0.5)
    col = np.arange(32)
    c["om"] = np.broadcast_to((col[None, :] // 8 == j[:, None]).astype(f)[None], (128, 4, 32))
    c["iota"] = np.broadcast_to(np.arange(16, dtype=f)[None], (128, 16))
    c["half"] = np.full((2, 128), 0.5, f)
    inv = f(1.0) / np.power(f(10000.0), np.arange(0, 64, 2, dtype=f) / f(64))
    pos = np.maximum(np.arange(256) - 1, 0).astype(f)
    ang = pos[:, None] * inv[None, :].astype(f)
    cos = np.concatenate([np.cos(ang), np.cos(ang)], -1)
    sin = np.concatenate([-np.sin(ang), np.sin(ang)], -1)
    cs = np.stack([cos, sin], 1).astype(f)
    both = np.stack([cs * f(64 ** -0.5), cs], 1)
    c["rope"] = both.reshape(2, 128, 2, 2, 64).transpose(1, 0, 2, 3, 4)
    return c


def kernel(**inputs):
    import numpy as np
    import concourse.bacc as bacc
    from concourse import mybir as mb
    from concourse.bass_utils import run_bass_kernel_spmd

    nc = bacc.Bacc("TRN2", target_bir_lowering=False, num_devices=1)
    arrays = {}

    def given(name, a):
        a = np.ascontiguousarray(a)
        arrays[f"in_{name}"] = a
        return nc.dram_tensor(f"in_{name}", a.shape, mb.dt.from_np(a.dtype), kind="ExternalInput").ap()

    x = given("x", np.asarray(inputs["L0_attn_x"]))
    w = {n: given(n, lay(np.asarray(inputs[n]))) for n, lay in _WEIGHTS.items()}
    scales = np.stack([np.asarray(inputs[f"L1_ffn_{n}_s"]).reshape(4, 128) for n in ("w1", "w2", "h1", "h2")])
    w["L1_ffn_scales"] = given("L1_ffn_scales", scales.transpose(2, 0, 1))
    const = {n: given(n, a) for n, a in _constants(np).items()}
    shape = inputs["L0_attn_x"].shape
    out = nc.dram_tensor("out_0", shape, mb.dt.float32, kind="ExternalOutput").ap()
    block_kernel(nc, x, w, const, out)
    r = run_bass_kernel_spmd(nc, [arrays], core_ids=[0])
    return r.results[0]["out_0"]
```

```python
import concourse.bass as bass
from concourse import mybir
from contextlib import ExitStack


def block_kernel(nc, x, w, const, out):
    F32 = mybir.dt.float32
    U32 = mybir.dt.uint32
    ALU = mybir.AluOpType
    ACT = mybir.ActivationFunctionType
    AX = mybir.AxisListType

    P = 128
    SEQS, LEN, E = x.shape
    T = LEN // P
    EPS = 1e-5
    LA_GROUPS, LA_PER_GROUP, LA_D = 4, 4, 8
    EXPERTS, PER_BANK = 16, 4
    UNITS_B = T * EXPERTS // PER_BANK
    HEADS, D = 16, 64
    PAIRS = HEADS // 2
    INNER = HEADS * D
    BLK = 512
    BLOCKS = 3 * INNER // BLK
    HID_T = 512 // P
    LAYERS = 4
    LA, MOE, SA, FFN = range(LAYERS)

    ctx = ExitStack()
    with ctx:
        def sb(name, shape, dt=F32):
            return ctx.enter_context(nc.sbuf_tensor(name, shape, dt))

        def sem(name):
            return ctx.enter_context(nc.semaphore(name))

        X = sb("X", [P, SEQS * T, E])
        XnT = sb("XnT", [P, SEQS * LEN])
        U = sb("U", [P, SEQS * T, E])
        xT = sb("xT", [P, 2, LEN])
        stat = sb("stat", [P, T, 6])
        mv = sb("mv", [P, T, 2])
        ve = sb("ve", [P, T])
        rstd = sb("rstd", [P, T])
        nhalf = sb("nhalf", [P, T])
        yn = sb("yn", [P, T, E])
        xa = sb("xa", [P, T, E])
        xn = sb("xn", [P, T, E])

        ident = sb("ident", [P, P])
        tri = sb("tri", [P, P])
        hm = sb("hm", [P, LA_PER_GROUP])
        om = sb("om", [P, LA_PER_GROUP, 32])
        iota = sb("iota", [P, EXPERTS])
        half = sb("half", [2, P])
        rope = sb("rope", [P, T, 2, 2, D])
        la_qkv = sb("la_qkv", [P, 3 * E])
        la_out = sb("la_out", [P, E])
        centT = sb("centT", [P, EXPERTS])
        ebias = sb("ebias", [P, EXPERTS])
        WrT = sb("WrT", [P, EXPERTS * E])
        br = sb("br", [EXPERTS, E])
        WsT = sb("WsT", [P, 2, E])
        Wsh = sb("Wsh", [P, E])
        bs = sb("bs", [2, E])
        gb = sb("gb", [P, 2])
        w_qkv = sb("w_qkv", [P, 3 * INNER])
        w_out = sb("w_out", [P, PAIRS, E])
        w1T = sb("w1T", [P, HID_T * P])
        w2T = sb("w2T", [P, HID_T * P])
        h1T = sb("h1T", [P, HID_T, HID_T * P])
        h2T = sb("h2T", [P, HID_T, HID_T * P])
        w3T = sb("w3T", [P, HID_T, E])
        fs = sb("fs", [P, 4, HID_T])
        s1h = sb("s1h", [P, HID_T])
        s12 = sb("s12", [P, HID_T])
        s3 = sb("s3", [P, E])

        WORK = 2 * (2 * PAIRS * LEN + T * INNER) + 3 * 2 * LEN * 2 + 2 * PAIRS * LEN + 6 * BLK + 8 * HEADS
        work = sb("work", [P, WORK])
        top = [0]

        def carve(*shape):
            n = 1
            for s in shape:
                n *= s
            a = work[:, top[0]:top[0] + n]
            top[0] += n
            assert top[0] <= WORK
            names = "abcde"[:len(shape)]
            if len(shape) > 1:
                a = a.rearrange(f"p ({' '.join(names)}) -> p {' '.join(names)}",
                                **{c: s for c, s in zip(names, shape)})
            return a

        bank = [ctx.enter_context(nc.psum_tensor(f"bank{b}", [P, BLK], F32)) for b in range(8)]
        Y = bank[0]
        Yt = Y[:, 0:T * E].rearrange("p (t e) -> p t e", t=T)
        NT = Y[:, 256:256 + LEN]

        s_x = sem("s_x")
        s_const = sem("s_const")
        s_w = [sem(f"s_w{l}") for l in range(LAYERS)]
        s_out = sem("s_out")
        s_nhalf, s_vm, s_wsh, s_fs, b_rch = (sem(n) for n in ("s_nhalf", "s_vm", "s_wsh", "s_fs", "b_rch"))
        x_ready = [sem(f"x_ready{l}") for l in range(LAYERS)]
        a_proj = sem("a_proj")
        y_ready = [sem(f"y_ready{l}") for l in range(LAYERS)]
        n_stats = [sem(f"n_stats{r}") for r in range(5)]
        n_rstd = [sem(f"n_rstd{r}") for r in range(5)]
        n_yn = [sem(f"n_yn{r}") for r in range(5)]
        n_x = [sem(f"n_x{r}") for r in range(5)]
        n_xn = [sem(f"n_xn{r}") for r in range(5)]
        n_u = [sem(f"n_u{r}") for r in range(5)]
        n_tp = [sem(f"n_tp{r}") for r in range(5)]
        n_xnT = [sem(f"n_xnT{r}") for r in range(5)]
        v_chain = [sem(f"v_chain{r}") for r in range(5)]
        p_chain = [sem(f"p_chain{r}") for r in range(5)]

        def reached(count):
            return max(count, 0) if isinstance(count, int) else count

        def wait_apart(eng, s, value, held, held_value):
            if not isinstance(value, int):
                eng.lower_val(value)
            eng.wait_ge(held, held_value)
            eng.wait_ge(s, value)

        def i_is(i, *ns):
            return isinstance(i, int) and i in ns

        class Chain:

            def __init__(self, eng, s, per_step):
                self.eng, self.s, self.n = eng, s, per_step

            def begin(self, i):
                self.i, self.k = i, 0

            def mark(self, ins):
                ins.then_inc(self.s, 1)
                self.k += 1

            def need(self, back=0):
                self.eng.wait_ge(self.s, reached(self.i * self.n + self.k - back))

            def need_apart(self):
                wait_apart(self.eng, self.s, self.i * self.n + self.k, s_x, 64)

            def end(self):
                assert self.k == self.n, (self.k, self.n)

        def over_sequences(eng, step, peeled=2):
            for i in range(peeled):
                step(i, i % 2)
            with eng.Fori(peeled // 2, SEQS // 2 - 1) as j:
                for p in range(2):
                    step(eng.snap(j * 2 + p), p)
            step(SEQS - 2, 0)
            step(SEQS - 1, 1)

        def over_all(eng, step):
            step(0)
            with eng.Fori(1, SEQS) as i:
                step(i)

        def seq_tiles(buf, i):
            return buf[:, bass.ds(i * T, T), :] if not isinstance(i, int) else buf[:, i * T:(i + 1) * T, :]

        def tile_of(buf, i, t):
            return (buf[:, bass.ds(i * T + t, 1), :] if not isinstance(i, int)
                    else buf[:, i * T + t:i * T + t + 1, :])

        def seq_cols(buf, i):
            return buf[:, bass.ds(i * LEN, LEN)] if not isinstance(i, int) else buf[:, i * LEN:(i + 1) * LEN]

        POST = [0, 1, 1, 1, 1]
        PRE = [1, 1, 2, 1, 0]
        ROUNDS = [a + b for a, b in zip(POST, PRE)]

        def norm_vector(dve, r, ch, y_of, y_count=1):
            def stats(i, k, src):
                for t in range(T):
                    ch.mark(nc.vector.bn_stats(stat[:, t, :], src(t)))
                ch.need_apart()
                for t in range(T):
                    ins = nc.vector.bn_aggr(mv[:, t, :], stat[:, t, :])
                ins.then_inc(n_stats[r], 1)

            def post_stats(i, p):
                dve.wait_ge(y_ready[r - 1], (i + 1) * y_count)
                stats(i, 0, lambda t: y_of(p)[:, t, :])

            def post_apply(i, p):
                dve.wait_ge(n_rstd[r], i * ROUNDS[r] + 1)
                dve.wait_ge(n_x[r], reached(i))
                for t in range(T):
                    ins = nc.vector.tensor_scalar(yn[:, t, :], y_of(p)[:, t, :], mv[:, t, 0:1],
                                                  rstd[:, t:t + 1], ALU.subtract, ALU.mult)
                ins.then_inc(n_yn[r], 1)

            def pre_stats(k):
                def piece(i, p):
                    if k == 0:
                        if r:
                            dve.wait_ge(n_x[r], i + 1)
                        stats(i, k, lambda t: tile_of(X, i, t).rearrange("p a e -> p (a e)"))
                    else:
                        ch.need()
                        stats(i, k, lambda t: xa[:, t, :])
                return piece

            def pre_apply(k):
                final = k == PRE[r] - 1

                def piece(i, p):
                    dve.wait_ge(n_rstd[r], i * ROUNDS[r] + POST[r] + k + 1)
                    if final:
                        dve.wait_ge(n_tp[r], reached(i))
                        if r == 1:
                            dve.wait_ge(n_u[r], reached(i))
                    for t in range(T):
                        src = tile_of(X, i, t).rearrange("p a e -> p (a e)") if k == 0 else xa[:, t, :]
                        ins = nc.vector.tensor_scalar((xn if final else xa)[:, t, :], src, mv[:, t, 0:1],
                                                      rstd[:, t:t + 1], ALU.subtract, ALU.mult)
                        if not final:
                            ch.mark(ins)
                    if final:
                        ins.then_inc(n_xn[r], 1)
                return piece

            pieces = [post_stats, post_apply] if POST[r] else []
            for k in range(PRE[r]):
                pieces += [pre_stats(k), pre_apply(k)]
            return pieces

        def norm_marks(r):
            return T * ROUNDS[r] + (T if PRE[r] == 2 else 0)

        def norm_pool(pool, r, i, k):
            wait_apart(pool, n_stats[r], i * ROUNDS[r] + k + 1, s_nhalf, 1)
            nc.gpsimd.tensor_scalar(ve[:, :], mv[:, :, 1], EPS, None, ALU.add).then_inc(p_chain[r], 1)
            pool.wait_ge(p_chain[r], i * ROUNDS[r] + k + 1)
            nc.gpsimd.tensor_tensor(rstd[:, :], ve[:, :], nhalf[:, :], ALU.pow).then_inc(n_rstd[r], 1)
            if k == 0 and POST[r]:
                pool.wait_ge(n_yn[r], i + 1)
                xs = seq_tiles(X, i)
                nc.gpsimd.tensor_tensor(xs, xs, yn[:, :, :], ALU.add).then_inc(n_x[r], 1)
            if k == ROUNDS[r] - 1 and r == 1:
                pool.wait_ge(n_xn[r], i + 1)
                nc.gpsimd.tensor_copy(seq_tiles(U, i), xn[:, :, :]).then_inc(n_u[r], 1)

        def norm_tensor(pe, r, i):
            pe.wait_ge(n_xn[r], i + 1)
            pe.wait_ge(n_xnT[r], reached(i))
            for t in range(T):
                ins = nc.tensor.transpose(NT[:, t * P:(t + 1) * P], xn[:, t, :], ident[:, :])
            ins.then_inc(n_tp[r], 1)

        def norm_scalar(act, r, i):
            act.wait_ge(n_tp[r], i + 1)
            if r == 2:
                ins = nc.scalar.activation(seq_cols(XnT, i), NT, ACT.Identity, bias=gb[:, 1:2], scale=gb[:, 0:1])
            else:
                ins = nc.scalar.activation(seq_cols(XnT, i), NT, ACT.Copy)
            ins.then_inc(n_xnT[r], 1)

        def layer_begins(eng, l):
            eng.wait_ge(n_xnT[l], SEQS)
            if l == 1:
                eng.wait_ge(n_u[1], SEQS)

        def pool_xT(pool, l, i, p):
            last_use, per_seq = ((a_proj, 1), (b_x, UNITS_B), (c_junit, JUNITS), (d_u, 2))[l]
            pool.wait_ge(last_use, reached(per_seq * (i - 1)))
            nc.gpsimd.tensor_copy(xT[:, p, :], seq_cols(XnT, i)).then_inc(x_ready[l], 1)

        top[0] = 0
        neg = carve(BLK)
        ex = carve(BLK)
        qk = carve(2, BLK)
        qblk = carve(2, LA_PER_GROUP, LEN)
        vm = carve(2, T, LA_GROUPS, LA_PER_GROUP, 32)
        vm_all = work[:, top[0] - 2 * T * LA_GROUPS * LA_PER_GROUP * 32:top[0]]
        at0 = carve(2, LA_PER_GROUP, LEN)
        at1 = carve(2, LA_PER_GROUP, P)
        den = carve(LEN)
        rden = carve(LEN)
        oT = carve(LEN)
        QKB, VB = bank[1], bank[2]
        ND = bank[3:5]
        SC = bank[5:8]
        a_neg, a_exp, a_feat, a_qb, a_vm = (sem(n) for n in ("a_neg", "a_exp", "a_feat", "a_qb", "a_vm"))
        a_s = [sem(f"a_s{k}") for k in range(3)]
        a_m = [sem(f"a_m{k}") for k in range(3)]
        a_nd, a_den, a_rden, a_oT = (sem(n) for n in ("a_nd", "a_den", "a_rden", "a_oT"))
        G4 = LA_GROUPS

        def la_proj_tensor(pe, i, p):
            pe.wait_ge(x_ready[LA], i + 1)
            pe.wait_ge(a_feat, reached(i))
            pe.wait_ge(a_vm, reached(i))
            nc.tensor.matmul(QKB[:, 0:LEN], la_qkv[:, 0:E], xT[:, p, :], start=True, stop=True)
            nc.tensor.matmul(QKB[:, LEN:2 * LEN], la_qkv[:, E:2 * E], xT[:, p, :], start=True, stop=True)
            for t in range(T):
                ins = nc.tensor.matmul(VB[:, t * E:(t + 1) * E], xT[:, p, t * P:(t + 1) * P],
                                       la_qkv[:, 2 * E:3 * E], start=True, stop=True)
            ins.then_inc(a_proj, 1)

        def la_feat_vector(dve, i, p, part):
            if part == 0:
                dve.wait_ge(a_proj, i + 1)
                dve.wait_ge(a_exp, reached(i))
                nc.vector.tensor_scalar(neg, QKB[:, :], 0.0, None, ALU.min).then_inc(a_neg, 1)
            else:
                dve.wait_ge(a_exp, i + 1)
                dve.wait_ge(a_nd, reached(G4 * (i - 1)))
                nc.vector.scalar_tensor_tensor(qk[:, p, :], QKB[:, :], 0.0, ex, ALU.max, ALU.add)\
                    .then_inc(a_feat, 1)

        def la_feat_scalar(act, i, p):
            act.wait_ge(a_neg, i + 1)
            act.wait_ge(a_feat, reached(i))
            nc.scalar.activation(ex, neg, ACT.Exp).then_inc(a_exp, 1)
            act.wait_ge(a_proj, i + 1)
            act.wait_ge(a_nd, reached(G4 * (i - 1)))
            for j in range(LA_PER_GROUP):
                c = slice(j * LA_D, (j + 1) * LA_D)
                ins = nc.scalar.activation(
                    vm[:, p, :, :, j, c].rearrange("p t g c -> p (t g) c"),
                    VB[:, 0:T * E].rearrange("p (a c) -> p a c", c=32)[:, :, c], ACT.Copy)
            ins.then_inc(a_vm, 1)

        def la_qblk_scalar(act, i, p):
            act.wait_ge(a_feat, i + 1)
            act.wait_ge(a_nd, reached(G4 * (i - 1)))
            for j in range(LA_PER_GROUP):
                ins = nc.scalar.activation(qblk[:, p, j, :], qk[:, p, 0:LEN], ACT.Copy, scale=hm[:, j:j + 1])
            ins.then_inc(a_qb, 1)

        def la_scores_tensor(pe, i, p, g):
            n = i * G4 + g
            rows = slice(32 * g, 32 * g + 32)
            for kind, (kt, qt) in enumerate(((0, 0), (0, 1), (1, 1))):
                pe.wait_ge(a_m[kind], reached(n))
                nc.tensor.matmul(SC[kind][:, :], qk[rows, p, LEN + kt * P:LEN + (kt + 1) * P],
                                 qblk[rows, p, :, qt * P:(qt + 1) * P], start=True, stop=True)\
                    .then_inc(a_s[kind], 1)

        def la_sums_tensor(pe, i, p, g):
            n = i * G4 + g
            if g == 0:
                pe.wait_ge(a_oT, reached(i - 1))
                pe.wait_ge(a_vm, i + 1)
            for kind in range(3):
                pe.wait_ge(a_m[kind], n + 1)
            rows = slice(32 * g, 32 * g + 32)
            s = g % 2
            for first, of in ((0, lambda t, j: vm[:, p, t, g, j, :]), (LEN, lambda t, j: om[:, j, :])):
                for j in range(LA_PER_GROUP):
                    nc.tensor.matmul(ND[p][rows, first:first + LEN], of(0, j), at0[:, s, j, :], start=(j == 0),
                                     stop=False)
                for j in range(LA_PER_GROUP):
                    ins = nc.tensor.matmul(ND[p][rows, first + P:first + LEN], of(1, j), at1[:, s, j, :],
                                           start=False, stop=(j == LA_PER_GROUP - 1))
            ins.then_inc(a_nd, 1)

        def la_mask_vector(dve, i, g, kind):
            n = i * G4 + g
            s = g % 2
            tri4 = tri[:, :].rearrange("p (o l) -> p o l", o=1).to_broadcast([P, LA_PER_GROUP, P])
            dst = at0[:, s, :, 0:P] if kind == 0 else at1[:, s, :, :]
            dve.wait_ge(a_s[kind], n + 1)
            dve.wait_ge(a_nd, reached(n - 1))
            nc.vector.tensor_tensor(dst, SC[kind][:, :].rearrange("p (j l) -> p j l", j=LA_PER_GROUP),
                                    tri4, ALU.mult).then_inc(a_m[kind], 1)

        def la_copy_scalar(act, i, g):
            n = i * G4 + g
            act.wait_ge(a_nd, reached(n - 1))
            act.wait_ge(a_s[1], n + 1)
            nc.scalar.activation(at0[:, g % 2, :, P:2 * P],
                                 SC[1][:, :].rearrange("p (j l) -> p j l", j=LA_PER_GROUP), ACT.Copy)\
                .then_inc(a_m[1], 1)

        def la_divide_vector(dve, i, p, part):
            if part == 0:
                dve.wait_ge(a_nd, G4 * (i + 1))
                nc.vector.tensor_scalar(den, ND[p][:, LEN:2 * LEN], 1e-6, None, ALU.max).then_inc(a_den, 1)
                dve.wait_ge(a_den, i + 1)
                dve.wait_ge(a_oT, reached(i))
                nc.vector.reciprocal(rden, den).then_inc(a_rden, 1)
            else:
                dve.wait_ge(a_rden, i + 1)
                dve.wait_ge(y_ready[LA], reached(i))
                nc.vector.tensor_tensor(oT, ND[p][:, 0:LEN], rden, ALU.mult).then_inc(a_oT, 1)

        def la_out_tensor(pe, i):
            pe.wait_ge(a_oT, i + 1)
            pe.wait_ge(n_xnT[1], reached(i))
            for t in range(T):
                ins = nc.tensor.matmul(Yt[:, t, :], oT[:, t * P:(t + 1) * P], la_out[:, :], start=True, stop=True)
            ins.then_inc(y_ready[LA], 1)

        LA_LAG = 2
        LA_PROJ_SLOT, LA_FEAT_SLOTS, LA_QBLK_SLOT = 0, (1, 2), 3
        LA_DIVIDE_SLOTS, LA_OUT_SLOT = (1, 2), 3

        top[0] = 0
        zr = carve(T, EXPERTS)
        t8 = carve(T, 8)
        ixf = carve(T, 2)
        nm = carve(T)
        ez = carve(T, EXPERTS)
        zs = carve(T)
        e2 = carve(T, 2)
        rz = carve(T)
        g2 = carve(T, 2)
        oh = carve(2, T, EXPERTS)
        gates = carve(2, T, EXPERTS)
        gT = carve(2, LEN)[0:EXPERTS, :, :]
        acc = carve(2, T, E)
        ix8 = sb("ix8", [P, T, 8], U32)
        RB, SHB = bank[1], bank[2]
        XB = bank[3:7]
        b_z, b_nm, b_e, b_g, b_gt, b_gs, b_sh, b_acc = (
            sem(n) for n in ("b_z", "b_nm", "b_e", "b_g", "b_gt", "b_gs", "b_sh", "b_acc"))
        y_ready[MOE] = b_acc
        b_x = sem("b_x")

        def moe_router_tensor(pe, i, p):
            pe.wait_ge(x_ready[MOE], i + 1)
            pe.wait_ge(b_gs, reached(i))
            for t in range(T):
                ins = nc.tensor.matmul(RB[:, t * EXPERTS:(t + 1) * EXPERTS], xT[:, p, t * P:(t + 1) * P],
                                       centT[:, :], start=True, stop=True)
            ins.then_inc(b_z, 1)

        def moe_gates_tensor(pe, i, p):
            pe.wait_ge(b_g, i + 1)
            for t in range(T):
                ins = nc.tensor.transpose(RB[0:EXPERTS, 256 + t * P:256 + (t + 1) * P], gates[:, p, t, :],
                                          ident[:, :])
            ins.then_inc(b_gt, 1)

        MOE_ROUTER_MARKS = 13

        def moe_router_vector(dve, ch, i, p, part):
            if part == 0:
                dve.wait_ge(b_z, i + 1)
                bias = ebias[:, :].rearrange("p (o e) -> p o e", o=1).to_broadcast([P, T, EXPERTS])
                dve.wait_ge(b_e, reached(i))
                ch.mark(nc.vector.tensor_tensor(zr, RB[:, 0:T * EXPERTS].rearrange("p (t e) -> p t e", t=T),
                                                bias, ALU.add))
                ch.need_apart()
                for t in range(T):
                    ch.mark(nc.vector.max(t8[:, t, :], zr[:, t, :]))
                ch.need_apart()
                nc.vector.tensor_scalar(nm, t8[:, :, 0], -1.0, None, ALU.mult).then_inc(b_nm, 1)
                for t in range(T):
                    ch.mark(nc.vector.max_index(ix8[:, t, :], t8[:, t, :], zr[:, t, :]))
                ch.need()
                ch.mark(nc.vector.tensor_copy(ixf, ix8[:, :, 0:2]))
                return
            dve.wait_ge(b_e, i + 1)
            ch.mark(nc.vector.reciprocal(rz, zs))
            ch.need()
            for t in range(T):
                ch.mark(nc.vector.tensor_scalar(g2[:, t, :], e2[:, t, :], rz[:, t:t + 1], None, ALU.mult))
            ch.need()
            for t in range(T):
                for k in range(2):
                    ch.mark(nc.vector.tensor_scalar(oh[:, k, t, :], iota[:, :], ixf[:, t, k:k + 1],
                                                    g2[:, t, k:k + 1], ALU.is_equal, ALU.mult))
            ch.need()
            dve.wait_ge(b_gt, reached(i - 1))
            nc.vector.tensor_tensor(gates[:, p, :, :], oh[:, 0, :, :], oh[:, 1, :, :], ALU.add).then_inc(b_g, 1)

        def moe_router_scalar(act, i, p):
            act.wait_ge(b_nm, i + 1)
            act.wait_ge(b_g, reached(i))
            for t in range(T):
                nc.scalar.activation(ez[:, t, :], zr[:, t, :], ACT.Exp, bias=nm[:, t:t + 1],
                                     accum_out=zs[:, t:t + 1])
            for t in range(T):
                ins = nc.scalar.activation(e2[:, t, :], t8[:, t, 0:2], ACT.Exp, bias=nm[:, t:t + 1])
            ins.then_inc(b_e, 1)

        def moe_gates_scalar(act, i, p):
            act.wait_ge(b_gt, i + 1)
            act.wait_ge(b_sh, reached(i - 1))
            nc.scalar.activation(gT[:, p, :], RB[0:EXPERTS, 256:256 + LEN], ACT.Copy).then_inc(b_gs, 1)

        def moe_shared_tensor(pe, i, p):
            pe.wait_ge(b_gs, i + 1)
            pe.wait_ge(b_acc, reached(i * T * (EXPERTS + 1) - T * EXPERTS))
            for t in range(T):
                o = SHB[:, t * E:(t + 1) * E]
                nc.tensor.matmul(o, xT[:, p, t * P:(t + 1) * P], Wsh[:, :], start=True, stop=False)
                nc.tensor.matmul(o, gT[:, p, t * P:(t + 1) * P], br[:, :], start=False, stop=False)
                ins = nc.tensor.matmul(o, half[:, :], bs[:, :], start=False, stop=True)
            ins.then_inc(b_sh, 1)

        def moe_unit_tensor(pe, i, p, u):
            t, b = u % T, u // T
            back, e = (0, (b - 1) * PER_BANK - 1) if b >= 2 else (1, (b + 3) * PER_BANK - 1)
            pe.wait_ge(b_acc, reached((i - back) * T * (EXPERTS + 1) + T * (e + 1) + t + 1))
            ins = nc.tensor.matmul(XB[u % 4][:, :], xT[:, p, t * P:(t + 1) * P], WrT[:, b * BLK:(b + 1) * BLK],
                                   start=True, stop=True)
            ins.then_inc(b_x, 1)

        def moe_start_vector(dve, i, p):
            dve.wait_ge(b_sh, i + 1)
            for t in range(T):
                nc.vector.tensor_tensor(acc[:, p, t, :], SHB[:, t * E:(t + 1) * E],
                                        tile_of(U, i, t).rearrange("p a e -> p (a e)"), ALU.add)\
                    .then_inc(b_acc, 1)

        def moe_units_vector(dve, i, p, b, half_):
            if half_ == 0:
                for t in range(T):
                    dve.wait_ge(b_x, i * UNITS_B + b * T + t + 1)
            for k in range(half_ * PER_BANK // 2, (half_ + 1) * PER_BANK // 2):
                e = b * PER_BANK + k
                for t in range(T):
                    u = b * T + t
                    dve.wait_ge(b_acc, reached(i * T * (EXPERTS + 1) + T * (e + 1) + t - 1))
                    ins = nc.vector.scalar_tensor_tensor(
                        acc[:, p, t, :], XB[u % 4][:, k * E:(k + 1) * E], gates[:, p, t, e:e + 1],
                        acc[:, p, t, :], ALU.mult, ALU.add)
                    ins.then_inc(b_acc, 1)

        MOE_SLOTS = (("norm", 0), ("router", 0), ("norm", 1), ("router", 1),
                     ("norm", 2), ("norm", 3), ("norm", 4), ("norm", 5))

        top[0] = 0
        QT = carve(2, PAIRS, LEN)
        KT = carve(2, PAIRS, LEN)
        V = carve(2, T, INNER)
        pr = carve(2, T, LEN)
        pn = carve(2, T, LEN)
        pT = carve(2, T, LEN)
        oTs = carve(2, PAIRS, LEN)
        rc = carve(2, BLK)
        rs_ = carve(2, BLK)
        rq = carve(2, BLK)
        nmax = carve(HEADS, T)
        psum_ = carve(HEADS, T)
        prec = carve(HEADS, T)
        SB_, PB, OB, JB = bank[1:3], bank[3:5], bank[5], bank[6:8]
        c_s, c_max, c_exp, c_rec, c_pn, c_t, c_pte, c_v, c_oe = (
            sem(n) for n in ("c_s", "c_max", "c_exp", "c_rec", "c_pn", "c_t", "c_pte", "c_v", "c_oe"))
        c_junit = sem("c_junit")
        c_jv = sem("c_jv")
        c_js = sem("c_js")
        c_mul = sem("c_mul")
        c_rope = sem("c_rope")

        slots = [[] for _ in range(HEADS)]
        for t in range(T):
            for b in range(BLOCKS):
                slots[t * BLOCKS + b].append(("rope" if b < 4 else "v", t, b))
                if b < 4:
                    slots[t * BLOCKS + b + 3].append(("turn", t, b))
        order = [u for s in slots for u in s]
        JUNITS = len(order)
        place = {u: k for k, u in enumerate(order)}
        ROPES, TURNS = 4 * T, JUNITS - 4 * T

        def jcount(k, kinds):
            whole = sum(u[0] in kinds for u in order)
            return (k // JUNITS) * whole + sum(u[0] in kinds for u in order[:k % JUNITS])

        def sa_unit_tensor(pe, i, p, unit):
            kind, t, b = unit
            k = place[unit]
            bank_ = JB[k % 2]
            if order[(k - 2) % JUNITS][0] == "rope":
                pe.wait_ge(c_jv, reached(i * ROPES + jcount(k - 1, ("rope",))))
            else:
                pe.wait_ge(c_js, reached(i * TURNS + jcount(k - 1, ("v", "turn"))))
            if kind == "turn":
                pe.wait_ge(c_rope, i * ROPES + 4 * t + b + 1)
                for q in range(4):
                    ins = nc.tensor.transpose(bank_[:, q * P:(q + 1) * P], rq[:, b % 2, q * P:(q + 1) * P],
                                              ident[:, :])
            else:
                if k == 0:
                    pe.wait_ge(x_ready[SA], i + 1)
                ins = nc.tensor.matmul(bank_[:, :], xT[:, p, t * P:(t + 1) * P], w_qkv[:, b * BLK:(b + 1) * BLK],
                                       start=True, stop=True)
            ins.then_inc(c_junit, 1)

        def sa_unit_vector(dve, i, p, unit):
            kind, t, b = unit
            if kind != "rope":
                return
            k = place[unit]
            ru = 4 * t + b
            dve.wait_ge(c_junit, i * JUNITS + k + 1)
            dve.wait_ge(c_rope, reached(i * ROPES + ru - 1))
            src = JB[k % 2][:, :].rearrange("p (h s d) -> p h s d", s=2, d=D // 2)

            def table(m):
                return rope[:, t, b // 2, m, :].rearrange("p (o s d) -> p o s d", o=1, s=2)\
                    .to_broadcast([P, BLK // D, 2, D // 2])
            dst = [a[:, b % 2, :].rearrange("p (h s d) -> p h s d", s=2, d=D // 2) for a in (rc, rs_)]
            nc.vector.tensor_tensor(dst[0], src, table(0), ALU.mult)
            nc.vector.tensor_tensor(dst[1], src[:, :, ::-1, :], table(1), ALU.mult).then_inc(c_jv, 1)

        def sa_unit_pool(pool, i, p, unit):
            kind, t, b = unit
            if kind != "rope":
                return
            ru = 4 * t + b
            pool.wait_ge(c_jv, i * ROPES + ru + 1)
            before = ("turn", t, b - 2) if b >= 2 else ("turn", (t - 1) % T, b + 2)
            back = 0 if b >= 2 or t > 0 else 1
            pool.wait_ge(c_junit, reached((i - back) * JUNITS + place[before] + 1))
            nc.gpsimd.tensor_tensor(rq[:, b % 2, :], rc[:, b % 2, :], rs_[:, b % 2, :], ALU.add)\
                .then_inc(c_rope, 1)

        def sa_unit_scalar(act, i, p, unit):
            kind, t, b = unit
            if kind == "rope":
                return
            k = place[unit]
            act.wait_ge(c_junit, i * JUNITS + k + 1)
            bank_ = JB[k % 2]
            if kind == "v":
                dst = V[:, p, t, (b - 4) * BLK:(b - 3) * BLK]
                src = bank_[:, :]
            else:
                dst = (QT if b < 2 else KT)[:, p, 4 * (b % 2):4 * (b % 2) + 4, t * P:(t + 1) * P]
                src = bank_[:, :].rearrange("p (q l) -> p q l", q=4)
            nc.scalar.activation(dst, src, ACT.Copy).then_inc(c_js, 1)

        def sa_scores_tensor(pe, i, p, h):
            n = i * HEADS + h
            if h == 0:
                pe.wait_ge(c_js, (i + 1) * TURNS)
            pe.wait_ge(c_exp, reached(n - 1))
            rows = slice(D * (h % 2), D * (h % 2) + D)
            for t in range(T):
                ins = nc.tensor.matmul(SB_[h % 2][:, t * LEN:(t + 1) * LEN], QT[rows, p, h // 2, t * P:(t + 1) * P],
                                       KT[rows, p, h // 2, :], start=True, stop=True)
            ins.then_inc(c_s, 1)

        def sa_max_vector(dve, i, h):
            n = i * HEADS + h
            dve.wait_ge(c_s, n + 1)
            if h == 0:
                dve.wait_ge(c_exp, reached(n))
            nc.vector.tensor_reduce(nmax[:, h, :], SB_[h % 2][:, :].rearrange("p (t k) -> p t k", t=T),
                                    AX.X, ALU.max, negate=True).then_inc(c_max, 1)

        def sa_exp_scalar(act, i, h):
            n = i * HEADS + h
            act.wait_ge(c_max, n + 1)
            act.wait_ge(c_pn, reached(n - 1))
            for t in range(T):
                ins = nc.scalar.activation(pr[:, h % 2, t, :], SB_[h % 2][:, t * LEN:(t + 1) * LEN], ACT.Exp,
                                           bias=nmax[:, h, t:t + 1], accum_out=psum_[:, h, t:t + 1])
            ins.then_inc(c_exp, 1)

        def sa_norm_vector(dve, i, h):
            n = i * HEADS + h
            dve.wait_ge(c_exp, n + 1)
            nc.vector.reciprocal(prec[:, h, :], psum_[:, h, :]).then_inc(c_rec, 1)
            dve.wait_ge(c_rec, n + 1)
            dve.wait_ge(c_t, reached(n - 1))
            for t in range(T):
                ins = nc.vector.tensor_scalar(pn[:, h % 2, t, :], pr[:, h % 2, t, :], prec[:, h, t:t + 1], None,
                                              ALU.mult)
            ins.then_inc(c_pn, 1)

        def sa_turn_tensor(pe, i, h):
            n = i * HEADS + h
            pe.wait_ge(c_pn, n + 1)
            pe.wait_ge(c_pte, reached(n - 1))
            for kt in range(T):
                for t in range(T):
                    ins = nc.tensor.transpose(PB[h % 2][:, kt * LEN + t * P:kt * LEN + (t + 1) * P],
                                              pn[:, h % 2, t, kt * P:(kt + 1) * P], ident[:, :])
            ins.then_inc(c_t, 1)

        def sa_turn_scalar(act, i, h):
            n = i * HEADS + h
            act.wait_ge(c_t, n + 1)
            act.wait_ge(c_v, reached(n - 1))
            nc.scalar.activation(pT[:, h % 2, :, :], PB[h % 2][:, :].rearrange("p (t q) -> p t q", t=T), ACT.Copy)\
                .then_inc(c_pte, 1)

        def sa_pv_tensor(pe, i, p, h):
            n = i * HEADS + h
            pe.wait_ge(c_pte, n + 1)
            if h % 2 == 0:
                pe.wait_ge(c_oe, reached(i * PAIRS + h // 2))
            rows = slice(D * (h % 2), D * (h % 2) + D)
            for kt in range(T):
                ins = nc.tensor.matmul(OB[rows, 0:LEN], V[:, p, kt, h * D:(h + 1) * D], pT[:, h % 2, kt, :],
                                       start=(kt == 0), stop=(kt == T - 1))
            ins.then_inc(c_v, 1)

        def sa_pv_scalar(act, i, p, h):
            act.wait_ge(c_v, i * HEADS + h + 1)
            act.wait_ge(y_ready[SA], reached(i - 1))
            nc.scalar.activation(oTs[:, p, h // 2, :], OB[:, 0:LEN], ACT.Copy).then_inc(c_oe, 1)

        def sa_out_tensor(pe, i, p):
            pe.wait_ge(c_oe, (i + 1) * PAIRS)
            pe.wait_ge(n_xnT[3], reached(i))
            for t in range(T):
                for q in range(PAIRS):
                    ins = nc.tensor.matmul(Yt[:, t, :], oTs[:, p, q, t * P:(t + 1) * P], w_out[:, q, :],
                                           start=(q == 0), stop=(q == PAIRS - 1))
            ins.then_inc(y_ready[SA], 1)

        NORM_LAG, TURN_LAG, PV_LAG = 1, 2, 3
        SA_OUT_SLOT = 4
        SA_PIECE_SLOTS = (5, 7, 9, 11)
        SA_ROUND_SLOTS = (5, 9)
        SA_NORM_SLOT = 14
        SA_DRAIN = SA_OUT_SLOT + 1

        def lagged(i, p, h, lag):
            if h >= lag:
                return None if i_is(i, SEQS) else (i, p, h - lag)
            return None if i_is(i, 0) else (i - 1, 1 - p, h - lag + HEADS)

        top[0] = 0
        tg = carve(2, 2, LEN)
        gg = carve(2, 2, LEN)
        hT = carve(2, HID_T, LEN)
        f1 = carve(HID_T, LEN)
        f2 = carve(HID_T, LEN)
        yf = carve(2, T, E)
        GB, UB = (bank[1], bank[3]), (bank[2], bank[4])
        HB = bank[5:7]
        d_g, d_u, d_tanh, d_gg, d_h, d_m1, d_a1, d_m2, d_a2, d_y = (
            sem(n) for n in ("d_g", "d_u", "d_tanh", "d_gg", "d_h", "d_m1", "d_a1", "d_m2", "d_a2", "d_y"))

        def ffn_in_tensor(pe, i, p):
            pe.wait_ge(x_ready[FFN], i + 1)
            for m in range(2):
                for banks, wT, done, empty in ((GB, w1T, d_g, d_gg), (UB, w2T, d_u, d_h)):
                    pe.wait_ge(empty, reached(2 * (i - 1) + m + 1))
                    for k in range(2):
                        ob = 2 * m + k
                        ins = nc.tensor.matmul(banks[m][:, k * LEN:(k + 1) * LEN], wT[:, ob * P:(ob + 1) * P],
                                               xT[:, p, :], start=True, stop=True)
                    ins.then_inc(done, 1)

        def ffn_in_scalar(act, i):
            for m in range(2):
                act.wait_ge(d_g, 2 * i + m + 1)
                act.wait_ge(d_gg, reached(2 * (i - 1) + m + 1))
                for k in range(2):
                    ob = 2 * m + k
                    ins = nc.scalar.activation(tg[:, m, k, :], GB[m][:, k * LEN:(k + 1) * LEN], ACT.Tanh,
                                               scale=s1h[:, ob:ob + 1])
                ins.then_inc(d_tanh, 1)

        def ffn_in_vector(dve, i, p):
            for m in range(2):
                dve.wait_ge(d_tanh, 2 * i + m + 1)
                dve.wait_ge(d_h, reached(2 * (i - 1) + m + 1))
                nc.vector.scalar_tensor_tensor(gg[:, m, :, :].rearrange("p k l -> p (k l)"),
                                               tg[:, m, :, :].rearrange("p k l -> p (k l)"), 1.0, GB[m][:, :],
                                               ALU.add, ALU.mult).then_inc(d_gg, 1)
                dve.wait_ge(d_gg, 2 * i + m + 1)
                dve.wait_ge(d_u, 2 * i + m + 1)
                if m == 0:
                    dve.wait_ge(d_m1, reached(2 * (i - 1)))
                for k in range(2):
                    ob = 2 * m + k
                    ins = nc.vector.scalar_tensor_tensor(hT[:, p, ob, :], UB[m][:, k * LEN:(k + 1) * LEN],
                                                         s12[:, ob:ob + 1], gg[:, m, k, :], ALU.mult, ALU.mult)
                ins.then_inc(d_h, 1)

        def ffn_product(pe, src, wT, written, emptied, base):
            for m in range(2):
                pe.wait_ge(emptied, reached(base + m + 1))
                for k in range(2):
                    ob = 2 * m + k
                    for kb in range(HID_T):
                        ins = nc.tensor.matmul(HB[m][:, k * LEN:(k + 1) * LEN],
                                               wT[:, kb, ob * P:(ob + 1) * P], src[:, kb, :],
                                               start=(kb == 0), stop=(kb == HID_T - 1))
                ins.then_inc(written, 1)

        block = ctx.enter_context(nc.Block())

        @block.sync
        def _(sp):
            xv = x.rearrange("b (t p) e -> p (b t) e", p=P)
            ov = out.rearrange("b (t p) e -> p (b t) e", p=P)
            sp.dma_start(X[:, 0:8, :], xv[:, 0:8, :]).then_inc(s_x, 16)
            for name, dst in (("ident", ident), ("tri", tri), ("hm", hm), ("om", om), ("iota", iota),
                              ("half", half), ("rope", rope)):
                sp.dma_start(dst[:], const[name]).then_inc(s_const, 16)
            sp.dma_start(la_qkv[:, :], w["L0_attn_W_qkv"]).then_inc(s_w[LA], 16)
            sp.dma_start(la_out[:, :], w["L0_attn_W_out"]).then_inc(s_w[LA], 16)
            for c in range(1, 4):
                sp.dma_start(X[:, 8 * c:8 * c + 8, :], xv[:, 8 * c:8 * c + 8, :]).then_inc(s_x, 16)
            for dst, src in ((centT[:, :], w["L0_ffn_centroids"]), (WrT[:, :], w["L0_ffn_Wr"]),
                             (br[:, :], w["L0_ffn_br"]), (WsT[:, :, :], w["L0_ffn_Ws"]), (bs[:, :], w["L0_ffn_bs"]),
                             (ebias[:, :], w["L0_ffn_expert_biases"].to_broadcast([P, EXPERTS]))):
                sp.dma_start(dst, src).then_inc(s_w[MOE], 16)
            for dst, src in ((gb[:, 0:1], w["L1_attn_ln_gamma"]), (gb[:, 1:2], w["L1_attn_ln_beta"]),
                             (w_qkv[:, :], w["L1_attn_w_qkv"]),
                             (w_out[:, :, :], w["L1_attn_w_out"].rearrange("(q p) e -> p q e", p=P))):
                sp.dma_start(dst, src).then_inc(s_w[SA], 16)
            for dst, src in ((w1T[:, :], w["L1_ffn_w1_w"]), (w2T[:, :], w["L1_ffn_w2_w"]),
                             (h1T[:, :, :], w["L1_ffn_h1_w"].rearrange("(k p) o -> p k o", p=P)),
                             (h2T[:, :, :], w["L1_ffn_h2_w"].rearrange("(k p) o -> p k o", p=P)),
                             (w3T[:, :, :], w["L1_ffn_w3_w"].rearrange("(k p) o -> p k o", p=P)),
                             (fs[:, :, :], w["L1_ffn_scales"]),
                             (s3[:, :], w["L1_ffn_w3_s"].to_broadcast([P, E]))):
                sp.dma_start(dst, src).then_inc(s_w[FFN], 16)
            with sp.Fori(0, SEQS) as i:
                sp.wait_ge(n_x[4], i + 1)
                sp.dma_start(ov[:, bass.ds(i * T, T), :], X[:, bass.ds(i * T, T), :]).then_inc(s_out, 16)
            sp.wait_ge(s_out, 16 * SEQS)

        @block.gpsimd
        def _(pool):
            nc.gpsimd.memset(nhalf[:, :], -0.5).then_inc(s_nhalf, 1)
            pool.wait_ge(s_nhalf, 1)
            over_all(pool, lambda i: norm_pool(pool, 0, i, 0))

            pool.wait_ge(n_xnT[0], SEQS)
            pool_xT(pool, LA, 0, 0)
            pool_xT(pool, LA, 1, 1)

            def la_step(i, p):
                if not i_is(i, 0, 1):
                    norm_pool(pool, 1, i - LA_LAG, 0)
                if not i_is(i, SEQS - 2, SEQS - 1):
                    pool_xT(pool, LA, i + 2, p)
                if not i_is(i, 0, 1):
                    norm_pool(pool, 1, i - LA_LAG, 1)
            over_sequences(pool, la_step, 4)
            for i in range(SEQS - LA_LAG, SEQS):
                for k in range(ROUNDS[1]):
                    norm_pool(pool, 1, i, k)

            layer_begins(pool, MOE)
            pool_xT(pool, MOE, 0, 0)

            def moe_step(i, p):
                if not (i_is(i, SEQS - 1)):
                    pool_xT(pool, MOE, i + 1, 1 - p)
                if not (i_is(i, 0)):
                    for k in range(ROUNDS[2]):
                        norm_pool(pool, 2, i - 1, k)
            over_sequences(pool, moe_step)
            for k in range(ROUNDS[2]):
                norm_pool(pool, 2, SEQS - 1, k)

            layer_begins(pool, SA)
            pool_xT(pool, SA, 0, 0)
            for u in order:
                sa_unit_pool(pool, 0, 0, u)

            def sa_step(i, p):
                more = not (i_is(i, SEQS - 1))
                if more:
                    pool_xT(pool, SA, i + 1, 1 - p)
                for h in range(HEADS):
                    if more:
                        for u in slots[h]:
                            sa_unit_pool(pool, i + 1, 1 - p, u)
                    if h in SA_ROUND_SLOTS and not (i_is(i, 0)):
                        norm_pool(pool, 3, i - 1, SA_ROUND_SLOTS.index(h))
            over_sequences(pool, sa_step)
            for k in range(ROUNDS[3]):
                norm_pool(pool, 3, SEQS - 1, k)

            layer_begins(pool, FFN)
            pool_xT(pool, FFN, 0, 0)

            def ffn_step(i, p):
                if not (i_is(i, SEQS - 1)):
                    pool_xT(pool, FFN, i + 1, 1 - p)
                if not (i_is(i, 0)):
                    norm_pool(pool, 4, i - 1, 0)
            over_sequences(pool, ffn_step)
            norm_pool(pool, 4, SEQS - 1, 0)

        @block.vector
        def _(dve):
            chains = [Chain(dve, v_chain[r], n) for r, n in enumerate(
                (norm_marks(0), norm_marks(1), norm_marks(2), norm_marks(3), norm_marks(4)))]

            def run_piece(r, pieces, k, i, p):
                ch = chains[r]
                if k == 0:
                    ch.begin(i)
                pieces[k](i, p)
                if k == len(pieces) - 1:
                    ch.end()

            nc.vector.memset(vm_all, 0.0).then_inc(s_vm, 1)
            pieces = norm_vector(dve, 0, chains[0], None)
            dve.wait_ge(s_x, 64)
            over_all(dve, lambda i: [run_piece(0, pieces, k, i, 0) for k in range(len(pieces))])

            dve.wait_ge(s_const, 16 * 7)
            for part in range(2):
                la_feat_vector(dve, 0, 0, part)
            n1 = norm_vector(dve, 1, chains[1], lambda p: Yt)

            def la_slot(i, p, g):
                more, behind, lag = (not i_is(i, SEQS - 1, SEQS), not i_is(i, 0), not i_is(i, 0, 1))
                live = not i_is(i, SEQS)
                if live:
                    la_mask_vector(dve, i, g, 0)
                if lag:
                    run_piece(1, n1, g, i - LA_LAG, p)
                if behind and g in LA_DIVIDE_SLOTS:
                    la_divide_vector(dve, i - 1, 1 - p, LA_DIVIDE_SLOTS.index(g))
                if more and g == LA_FEAT_SLOTS[0]:
                    la_feat_vector(dve, i + 1, 1 - p, 0)
                if live:
                    la_mask_vector(dve, i, g, 2)
                if more and g == LA_FEAT_SLOTS[1]:
                    la_feat_vector(dve, i + 1, 1 - p, 1)

            def la_step(i, p):
                for g in range(LA_GROUPS):
                    la_slot(i, p, g)
            over_sequences(dve, la_step, 4)
            la_step(SEQS, 0)
            for k in range(len(n1)):
                run_piece(1, n1, k, SEQS - 1, 1)

            layer_begins(dve, MOE)
            dve.wait_ge(s_w[MOE], 16 * 6)
            nc.vector.tensor_tensor(Wsh[:, :], WsT[:, 0, :], WsT[:, 1, :], ALU.add).then_inc(s_wsh, 1)
            dve.wait_ge(s_wsh, 1)
            nc.vector.tensor_scalar(Wsh[:, :], Wsh[:, :], 0.5, None, ALU.mult).then_inc(s_wsh, 1)
            rch = Chain(dve, b_rch, MOE_ROUTER_MARKS)

            rch.begin(0)
            for part in range(2):
                moe_router_vector(dve, rch, 0, 0, part)
            rch.end()
            n2 = norm_vector(dve, 2, chains[2], lambda p: acc[:, p, :, :], T * (EXPERTS + 1))

            def moe_step(i, p):
                moe_start_vector(dve, i, p)
                for slot, (what, part) in enumerate(MOE_SLOTS):
                    moe_units_vector(dve, i, p, slot // 2, slot % 2)
                    if what == "norm" and not i_is(i, 0):
                        run_piece(2, n2, part, i - 1, 1 - p)
                    if what == "router" and not i_is(i, SEQS - 1):
                        if part == 0:
                            rch.begin(i + 1)
                        moe_router_vector(dve, rch, i + 1, 1 - p, part)
            over_sequences(dve, moe_step)
            for k in range(len(n2)):
                run_piece(2, n2, k, SEQS - 1, 1)

            layer_begins(dve, SA)
            for u in order:
                sa_unit_vector(dve, 0, 0, u)
            n3 = norm_vector(dve, 3, chains[3], lambda p: Yt)

            def sa_slot(i, p, h):
                at = lagged(i, p, h, NORM_LAG)
                if at:
                    sa_norm_vector(dve, at[0], at[2])
                if not i_is(i, SEQS):
                    sa_max_vector(dve, i, h)

            def sa_step(i, p):
                for h in range(HEADS):
                    sa_slot(i, p, h)
                    if not i_is(i, SEQS - 1):
                        for u in slots[h]:
                            sa_unit_vector(dve, i + 1, 1 - p, u)
                    if h in SA_PIECE_SLOTS and not i_is(i, 0):
                        run_piece(3, n3, SA_PIECE_SLOTS.index(h), i - 1, 1 - p)
            over_sequences(dve, sa_step)
            for h in range(SA_DRAIN):
                sa_slot(SEQS, 0, h)
            for k in range(len(n3)):
                run_piece(3, n3, k, SEQS - 1, 1)

            layer_begins(dve, FFN)
            dve.wait_ge(s_w[FFN], 16 * 7)
            nc.vector.tensor_scalar(s1h[:, :], fs[:, 0, :], 0.5, None, ALU.mult).then_inc(s_fs, 1)
            dve.wait_ge(s_fs, 1)
            nc.vector.tensor_tensor(s12[:, :], s1h[:, :], fs[:, 1, :], ALU.mult).then_inc(s_fs, 1)
            dve.wait_ge(s_fs, 2)
            ffn_in_vector(dve, 0, 0)
            n4 = norm_vector(dve, 4, chains[4], lambda p: yf[:, p, :, :])

            def ffn_step(i, p):
                if not (i_is(i, 0)):
                    for k in range(len(n4)):
                        run_piece(4, n4, k, i - 1, 1 - p)
                if not (i_is(i, SEQS - 1)):
                    ffn_in_vector(dve, i + 1, 1 - p)
                dve.wait_ge(d_y, i + 1)
                nc.vector.tensor_tensor(
                    yf[:, p, :, :], Yt,
                    s3[:, :].rearrange("p (o e) -> p o e", o=1).to_broadcast([P, T, E]), ALU.mult)\
                    .then_inc(y_ready[FFN], 1)
            over_sequences(dve, ffn_step)
            for k in range(len(n4)):
                run_piece(4, n4, k, SEQS - 1, 1)

        @block.scalar
        def _(act):
            over_all(act, lambda i: norm_scalar(act, 0, i))

            act.wait_ge(s_vm, 1)
            la_feat_scalar(act, 0, 0)
            la_qblk_scalar(act, 0, 0)

            def la_step(i, p):
                more, live = not i_is(i, SEQS - 1, SEQS), not i_is(i, SEQS)
                for g in range(LA_GROUPS):
                    if more and g == LA_QBLK_SLOT:
                        la_qblk_scalar(act, i + 1, 1 - p)
                    if live:
                        la_copy_scalar(act, i, g)
                    if more and g == LA_FEAT_SLOTS[0]:
                        la_feat_scalar(act, i + 1, 1 - p)
                if not i_is(i, 0, 1):
                    norm_scalar(act, 1, i - LA_LAG)
            over_sequences(act, la_step, 4)
            la_step(SEQS, 0)
            norm_scalar(act, 1, SEQS - 1)

            layer_begins(act, MOE)
            act.wait_ge(s_w[SA], 16 * 4)
            moe_router_scalar(act, 0, 0)
            moe_gates_scalar(act, 0, 0)

            def moe_step(i, p):
                if not i_is(i, SEQS - 1, SEQS):
                    moe_router_scalar(act, i + 1, 1 - p)
                if not i_is(i, 0, 1):
                    norm_scalar(act, 2, i - 2)
                if not i_is(i, SEQS - 1, SEQS):
                    moe_gates_scalar(act, i + 1, 1 - p)
            over_sequences(act, moe_step, 4)
            moe_step(SEQS, 0)
            norm_scalar(act, 2, SEQS - 1)

            layer_begins(act, SA)
            for u in order:
                sa_unit_scalar(act, 0, 0, u)

            def sa_slot(i, p, h):
                if not i_is(i, SEQS):
                    sa_exp_scalar(act, i, h)
                at = lagged(i, p, h, TURN_LAG)
                if at:
                    sa_turn_scalar(act, at[0], at[2])
                if not i_is(i, SEQS) and not i_is(i, SEQS - 1):
                    for u in slots[h]:
                        sa_unit_scalar(act, i + 1, 1 - p, u)
                at = lagged(i, p, h, PV_LAG)
                if at and at[2] % 2 == 1:
                    sa_pv_scalar(act, *at)

            def sa_step(i, p):
                for h in range(HEADS):
                    sa_slot(i, p, h)
                    if h == SA_NORM_SLOT and not i_is(i, 0):
                        norm_scalar(act, 3, i - 1)
            over_sequences(act, sa_step)
            for h in range(SA_DRAIN):
                sa_slot(SEQS, 0, h)
            norm_scalar(act, 3, SEQS - 1)

            layer_begins(act, FFN)
            act.wait_ge(s_fs, 2)
            ffn_in_scalar(act, 0)

            def gelu(i, product, dst, written, done):
                for m in range(2):
                    act.wait_ge(written, 2 * i + m + 1)
                    for k in range(2):
                        ob = 2 * m + k
                        ins = nc.scalar.activation(dst[:, ob, :], HB[m][:, k * LEN:(k + 1) * LEN], ACT.Gelu,
                                                   scale=fs[:, 2 + product, ob:ob + 1])
                    ins.then_inc(done, 1)

            def ffn_step(i, p):
                act.wait_ge(d_m2, reached(2 * i))
                gelu(i, 0, f1, d_m1, d_a1)
                if not (i_is(i, SEQS - 1)):
                    ffn_in_scalar(act, i + 1)
                act.wait_ge(d_y, reached(i))
                gelu(i, 1, f2, d_m2, d_a2)
            over_sequences(act, ffn_step)

        @block.tensor
        def _(pe):
            pe.wait_ge(s_const, 16 * 7)
            over_all(pe, lambda i: norm_tensor(pe, 0, i))

            pe.wait_ge(s_w[LA], 32)
            la_proj_tensor(pe, 0, 0)

            def la_step(i, p):
                more, live = not i_is(i, SEQS - 1, SEQS), not i_is(i, SEQS)
                if live:
                    pe.wait_ge(a_qb, i + 1)
                for g in range(LA_GROUPS):
                    if live:
                        la_scores_tensor(pe, i, p, g)
                    if g >= 1 and live:
                        la_sums_tensor(pe, i, p, g - 1)
                    if g == 0 and not i_is(i, 0):
                        la_sums_tensor(pe, i - 1, 1 - p, LA_GROUPS - 1)
                    if more and g == LA_PROJ_SLOT:
                        la_proj_tensor(pe, i + 1, 1 - p)
                if not i_is(i, 0, 1):
                    norm_tensor(pe, 1, i - LA_LAG)
                if not i_is(i, 0):
                    la_out_tensor(pe, i - 1)
            over_sequences(pe, la_step, 4)
            la_step(SEQS, 0)
            norm_tensor(pe, 1, SEQS - 1)

            layer_begins(pe, MOE)
            pe.wait_ge(s_w[MOE], 16 * 6)
            pe.wait_ge(s_wsh, 2)
            moe_router_tensor(pe, 0, 0)
            moe_gates_tensor(pe, 0, 0)

            moe_shared_tensor(pe, 0, 0)

            def moe_step(i, p):
                more = not i_is(i, SEQS - 1)
                for u in range(UNITS_B):
                    moe_unit_tensor(pe, i, p, u)
                    if u == 3 and more:
                        moe_router_tensor(pe, i + 1, 1 - p)
                    if u == 5 and not i_is(i, 0, 1):
                        norm_tensor(pe, 2, i - 2)
                if more:
                    moe_gates_tensor(pe, i + 1, 1 - p)
                    moe_shared_tensor(pe, i + 1, 1 - p)
            over_sequences(pe, moe_step, 4)
            norm_tensor(pe, 2, SEQS - 2)
            norm_tensor(pe, 2, SEQS - 1)

            layer_begins(pe, SA)
            pe.wait_ge(s_w[SA], 16 * 4)
            for u in order:
                sa_unit_tensor(pe, 0, 0, u)

            def sa_slot(i, p, h):
                if not i_is(i, SEQS):
                    sa_scores_tensor(pe, i, p, h)
                at = lagged(i, p, h, TURN_LAG)
                if at:
                    sa_turn_tensor(pe, at[0], at[2])
                if not i_is(i, SEQS) and not i_is(i, SEQS - 1):
                    for u in slots[h]:
                        sa_unit_tensor(pe, i + 1, 1 - p, u)
                at = lagged(i, p, h, PV_LAG)
                if at:
                    sa_pv_tensor(pe, *at)
                if h == SA_OUT_SLOT and not i_is(i, 0):
                    sa_out_tensor(pe, i - 1, 1 - p)

            def sa_step(i, p):
                for h in range(HEADS):
                    sa_slot(i, p, h)
                    if h == SA_NORM_SLOT and not i_is(i, 0):
                        norm_tensor(pe, 3, i - 1)
            over_sequences(pe, sa_step)
            for h in range(SA_DRAIN):
                sa_slot(SEQS, 0, h)
            norm_tensor(pe, 3, SEQS - 1)

            layer_begins(pe, FFN)
            pe.wait_ge(s_w[FFN], 16 * 7)
            ffn_in_tensor(pe, 0, 0)

            def ffn_step(i, p):
                pe.wait_ge(d_h, 2 * (i + 1))
                ffn_product(pe, hT[:, p, :, :], h1T, d_m1, d_a2, 2 * (i - 1))
                if not (i_is(i, SEQS - 1)):
                    ffn_in_tensor(pe, i + 1, 1 - p)
                pe.wait_ge(d_a1, 2 * (i + 1))
                ffn_product(pe, f1, h2T, d_m2, d_a1, 2 * i)
                pe.wait_ge(d_a2, 2 * (i + 1))
                pe.wait_ge(y_ready[FFN], reached(i))
                for t in range(T):
                    for kb in range(HID_T):
                        ins = nc.tensor.matmul(Yt[:, t, :], f2[:, kb, t * P:(t + 1) * P], w3T[:, kb, :],
                                               start=(kb == 0), stop=(kb == HID_T - 1))
                ins.then_inc(d_y, 1)

            over_sequences(pe, ffn_step)


_WEIGHTS = {
    "L0_attn_W_qkv": lambda a: a.T,
    "L0_attn_W_out": lambda a: a.T,
    "L0_ffn_centroids": lambda a: a.T,
    "L0_ffn_expert_biases": lambda a: a[None, :],
    "L0_ffn_Wr": lambda a: a.transpose(2, 0, 1).reshape(a.shape[2], -1),
    "L0_ffn_br": lambda a: a,
    "L0_ffn_Ws": lambda a: a.transpose(2, 0, 1),
    "L0_ffn_bs": lambda a: a,
    "L1_attn_ln_gamma": lambda a: a[:, None],
    "L1_attn_ln_beta": lambda a: a[:, None],
    "L1_attn_w_qkv": lambda a: a,
    "L1_attn_w_out": lambda a: a,
    "L1_ffn_w1_w": lambda a: a.T,
    "L1_ffn_w2_w": lambda a: a.T,
    "L1_ffn_h1_w": lambda a: a.T,
    "L1_ffn_h2_w": lambda a: a.T,
    "L1_ffn_w3_w": lambda a: a.T,
    "L1_ffn_w3_s": lambda a: a[None, :],
}


def _constants(np):
    f = np.float32
    p = np.arange(128)
    c = {"ident": np.eye(128, dtype=f)}
    c["tri"] = (p[:, None] <= p[None, :]).astype(f)
    j = np.arange(4)
    c["hm"] = ((p[:, None] % 32) // 8 == j[None, :]).astype(f) * f(8 ** -0.5)
    col = np.arange(32)
    c["om"] = np.broadcast_to((col[None, :] // 8 == j[:, None]).astype(f)[None], (128, 4, 32))
    c["iota"] = np.broadcast_to(np.arange(16, dtype=f)[None], (128, 16))
    c["half"] = np.full((2, 128), 0.5, f)
    inv = f(1.0) / np.power(f(10000.0), np.arange(0, 64, 2, dtype=f) / f(64))
    pos = np.maximum(np.arange(256) - 1, 0).astype(f)
    ang = pos[:, None] * inv[None, :].astype(f)
    cos = np.concatenate([np.cos(ang), np.cos(ang)], -1)
    sin = np.concatenate([-np.sin(ang), np.sin(ang)], -1)
    cs = np.stack([cos, sin], 1).astype(f)
    both = np.stack([cs * f(64 ** -0.5), cs], 1)
    c["rope"] = both.reshape(2, 128, 2, 2, 64).transpose(1, 0, 2, 3, 4)
    return c


def kernel(**inputs):
    import numpy as np
    import concourse.bacc as bacc
    from concourse import mybir as mb
    from concourse.bass_utils import run_bass_kernel_spmd

    nc = bacc.Bacc("TRN2", target_bir_lowering=False, num_devices=1)
    arrays = {}

    def given(name, a):
        a = np.ascontiguousarray(a)
        arrays[f"in_{name}"] = a
        return nc.dram_tensor(f"in_{name}", a.shape, mb.dt.from_np(a.dtype), kind="ExternalInput").ap()

    x = given("x", np.asarray(inputs["L0_attn_x"]))
    w = {n: given(n, lay(np.asarray(inputs[n]))) for n, lay in _WEIGHTS.items()}
    scales = np.stack([np.asarray(inputs[f"L1_ffn_{n}_s"]).reshape(4, 128) for n in ("w1", "w2", "h1", "h2")])
    w["L1_ffn_scales"] = given("L1_ffn_scales", scales.transpose(2, 0, 1))
    const = {n: given(n, a) for n, a in _constants(np).items()}
    shape = inputs["L0_attn_x"].shape
    out = nc.dram_tensor("out_0", shape, mb.dt.float32, kind="ExternalOutput").ap()
    block_kernel(nc, x, w, const, out)
    r = run_bass_kernel_spmd(nc, [arrays], core_ids=[0])
    return r.results[0]["out_0"]
```

```python
import concourse.bass as bass
from concourse import mybir
from contextlib import ExitStack


def block_kernel(nc, x, w, const, out):
    F32 = mybir.dt.float32
    F32R = mybir.dt.float32r
    U32 = mybir.dt.uint32
    ALU = mybir.AluOpType
    ACT = mybir.ActivationFunctionType
    AX = mybir.AxisListType

    P = 128
    SEQS, LEN, E = x.shape
    T = LEN // P
    EPS = 1e-5
    LA_GROUPS, LA_PER_GROUP, LA_D = 4, 4, 8
    LA_HEADS = LA_GROUPS * LA_PER_GROUP
    EXPERTS, PER_BANK = 16, 4
    UNITS_B = T * EXPERTS // PER_BANK
    HEADS, D = 16, 64
    PAIRS = HEADS // 2
    INNER = HEADS * D
    BLK = 512
    BLOCKS = 3 * INNER // BLK
    HID_T = 512 // P
    LAYERS = 4
    CHUNKS = 4
    CHUNK = SEQS * T // CHUNKS
    LA, MOE, SA, FFN = range(LAYERS)

    ctx = ExitStack()
    with ctx:
        def sb(name, shape, dt=F32):
            return ctx.enter_context(nc.sbuf_tensor(name, shape, dt))

        def sem(name):
            return ctx.enter_context(nc.semaphore(name))

        X = sb("X", [P, SEQS * T, E])
        XnT = sb("XnT", [P, SEQS * LEN])
        xT = sb("xT", [P, 2, LEN])
        stat = sb("stat", [P, T, 6])
        mv = sb("mv", [P, T, 2])
        ve = sb("ve", [P, T])
        rstd = sb("rstd", [P, T])
        nhalf = sb("nhalf", [P, CHUNK])
        yn = sb("yn", [P, T, E])
        xa = sb("xa", [P, T, E])
        xn = sb("xn", [P, T, E])

        ident = sb("ident", [P, P])
        tri = sb("tri", [P, P])
        hm = sb("hm", [P, LA_PER_GROUP])
        gm = sb("gm", [P, LA_GROUPS])
        sm = sb("sm", [P, LA_HEADS, LA_D + 1])
        iota = sb("iota", [P, EXPERTS])
        half = sb("half", [2, P])
        rope = sb("rope", [P, T, 2, 2, D])
        la_qkv = sb("la_qkv", [P, 3 * E])
        la_out = sb("la_out", [P, E])
        centT = sb("centT", [P, EXPERTS])
        ix8 = sb("ix8", [P, T, 8], U32)
        ebias = sb("ebias", [P, EXPERTS])
        br = sb("br", [EXPERTS, E])
        WsT = sb("WsT", [P, 2, E])
        Wsh = sb("Wsh", [P, E])
        bs = sb("bs", [2, E])
        gb = sb("gb", [P, 2])
        ternary_row = sb("ternary_row", [P, 1])
        ternary = sb("ternary", [1, 1], U32)
        w_qkv = sb("w_qkv", [P, 3 * INNER])
        w_out = sb("w_out", [P, PAIRS, E])
        w1T = sb("w1T", [P, HID_T * P])
        w2T = sb("w2T", [P, HID_T * P])
        h1T = sb("h1T", [P, HID_T, HID_T * P])
        h2T = sb("h2T", [P, HID_T, HID_T * P])
        w3T = sb("w3T", [P, HID_T, E])
        fs = sb("fs", [P, 4, HID_T])
        s1h = sb("s1h", [P, HID_T])
        s12 = sb("s12", [P, HID_T])
        s3 = sb("s3", [P, E])

        first_set, second_set, third_set = ExitStack(), ExitStack(), ExitStack()

        def carver(work, size):
            top = [0]

            def carve(*shape):
                n = 1
                for s in shape:
                    n *= s
                a = work[:, top[0]:top[0] + n]
                top[0] += n
                assert top[0] <= size
                names = "abcde"[:len(shape)]
                if len(shape) > 1:
                    a = a.rearrange(f"p ({' '.join(names)}) -> p {' '.join(names)}",
                                    **{c: s for c, s in zip(names, shape)})
                return a
            return carve

        MOE_WORK, LA_WORK = 2900, 11900
        U = first_set.enter_context(nc.sbuf_tensor("U", [P, SEQS * T, E], F32))
        WrT = first_set.enter_context(nc.sbuf_tensor("WrT", [P, EXPERTS * E], F32))
        moe_work = first_set.enter_context(nc.sbuf_tensor("moe_work", [P, MOE_WORK], F32))
        la_work = first_set.enter_context(nc.sbuf_tensor("la_work", [P, LA_WORK], F32))
        first_set.close()
        SECOND = 2 * (2 * PAIRS * LEN + T * INNER) + 3 * 2 * LEN * 2 + 2 * PAIRS * LEN + 8 * BLK + 8 * HEADS
        MOE_END = SEQS * T * E + EXPERTS * E + MOE_WORK
        assert SECOND >= MOE_END + LA_WORK
        work2 = second_set.enter_context(nc.sbuf_tensor("work2", [P, SECOND], F32))
        w_hi = second_set.enter_context(nc.sbuf_tensor("w_hi", [P, 3 * INNER], F32R))
        w_lo = second_set.enter_context(nc.sbuf_tensor("w_lo", [P, 3 * INNER], F32R))
        sx_hi = second_set.enter_context(nc.sbuf_tensor("sx_hi", [P, LEN], F32R))
        sx_lo = second_set.enter_context(nc.sbuf_tensor("sx_lo", [P, LEN], F32R))
        second_set.close()
        THIRD = 2 * 2 * 2 * LEN + 3 * HID_T * LEN + 2 * T * E
        work3 = third_set.enter_context(nc.sbuf_tensor("work3", [P, THIRD], F32))

        def pair(name, *shape):
            return [third_set.enter_context(nc.sbuf_tensor(f"{name}_{part}", [P, *shape], F32R))
                    for part in ("hi", "lo")]
        h2S = pair("h2", HID_T, HID_T * P)
        hS, f1S = pair("fh", HID_T, LEN), pair("ff", HID_T, LEN)
        third_set.enter_context(nc.sbuf_tensor("gap", [P, SECOND - THIRD - 2 * (HID_T * HID_T * P + 2 * HID_T * LEN)],
                                               F32))
        w1S, w2S = pair("w1", HID_T * P), pair("w2", HID_T * P)
        h1S, xS = pair("h1", HID_T, HID_T * P), pair("fx", LEN)
        third_set.close()

        def split_product(out, a, b, start, stop, a_short=False):
            products = ((a[1], b[0]), (a[0], b[1]), (a[0], b[0]))[1 if a_short else 0:]
            for k, (x_, y_) in enumerate(products):
                ins = nc.tensor.matmul(out, x_, y_, start=start and k == 0, stop=stop and k == len(products) - 1)
            return ins

        bank = [ctx.enter_context(nc.psum_tensor(f"bank{b}", [P, BLK], F32)) for b in range(8)]
        Y = bank[0]
        Yt = Y[:, 0:T * E].rearrange("p (t e) -> p t e", t=T)
        NT = Y[:, 256:256 + LEN]

        s_x = [sem(f"s_x{c}") for c in range(CHUNKS)]
        s_ident, s_const = sem("s_ident"), sem("s_const")
        s_w = [sem(f"s_w{l}") for l in range(LAYERS)]
        s_out = sem("s_out")
        s_nhalf, s_va, s_wsh, s_fs, b_rch = (sem(n) for n in ("s_nhalf", "s_va", "s_wsh", "s_fs", "b_rch"))
        x_ready = [sem(f"x_ready{l}") for l in (LA, MOE)]
        a_qk, a_v = sem("a_qk"), sem("a_v")
        y_ready = [sem(f"y_ready{l}") for l in range(LAYERS)]
        n_stats = [sem(f"n_stats{r}") for r in range(5)]
        n_rstd = [sem(f"n_rstd{r}") for r in range(5)]
        n_yn = [sem(f"n_yn{r}") for r in range(5)]
        n_x = [sem(f"n_x{r}") for r in range(5)]
        n_xn = [sem(f"n_xn{r}") for r in range(5)]
        n_u = [sem(f"n_u{r}") for r in range(5)]
        n_tp = [sem(f"n_tp{r}") for r in range(5)]
        n_xnT = [sem(f"n_xnT{r}") for r in range(5)]
        v_chain = [sem(f"v_chain{r}") for r in range(5)]
        p_chain = [sem(f"p_chain{r}") for r in range(5)]

        def reached(count):
            return max(count, 0) if isinstance(count, int) else count

        def at_most_all(count):
            return min(count, SEQS) if isinstance(count, int) else count

        def wait_apart(eng, s, value, held, held_value):
            if not isinstance(value, int):
                eng.lower_val(value)
            eng.wait_ge(held, held_value)
            eng.wait_ge(s, value)

        def i_is(i, *ns):
            return isinstance(i, int) and i in ns

        class Chain:

            def __init__(self, eng, s, per_step):
                self.eng, self.s, self.n = eng, s, per_step

            def begin(self, i):
                self.i, self.k = i, 0

            def mark(self, ins):
                ins.then_inc(self.s, 1)
                self.k += 1

            def need(self, back=0):
                self.eng.wait_ge(self.s, reached(self.i * self.n + self.k - back))

            def need_apart(self):
                wait_apart(self.eng, self.s, self.i * self.n + self.k, s_x[0], 16)

            def end(self):
                assert self.k == self.n, (self.k, self.n)

        def over_sequences(eng, step, peeled=2):
            for i in range(peeled):
                step(i, i % 2)
            with eng.Fori(peeled // 2, SEQS // 2 - 1) as j:
                for p in range(2):
                    step(eng.snap(j * 2 + p), p)
            step(SEQS - 2, 0)
            step(SEQS - 1, 1)

        def seq_tiles(buf, i):
            return buf[:, bass.ds(i * T, T), :] if not isinstance(i, int) else buf[:, i * T:(i + 1) * T, :]

        def tile_of(buf, i, t):
            return (buf[:, bass.ds(i * T + t, 1), :] if not isinstance(i, int)
                    else buf[:, i * T + t:i * T + t + 1, :])

        def seq_cols(buf, i):
            return buf[:, bass.ds(i * LEN, LEN)] if not isinstance(i, int) else buf[:, i * LEN:(i + 1) * LEN]

        POST = [0, 1, 1, 1, 1]
        PRE = [1, 1, 2, 1, 0]
        ROUNDS = [a + b for a, b in zip(POST, PRE)]

        def norm_vector(dve, r, ch, y_of, y_count=1, fine=False):
            def stats(src):
                for t in range(T):
                    ch.mark(nc.vector.bn_stats(stat[:, t, :], src(t)))

            def aggregate(i, p):
                ch.need_apart()
                for t in range(T):
                    ins = nc.vector.bn_aggr(mv[:, t, :], stat[:, t, :])
                ins.then_inc(n_stats[r], 1)

            def post_stats(i, p):
                dve.wait_ge(y_ready[r - 1], (i + 1) * y_count)
                stats(lambda t: y_of(p)[:, t, :])

            def post_apply(i, p):
                dve.wait_ge(n_rstd[r], i * ROUNDS[r] + 1)
                dve.wait_ge(n_x[r], reached(i))
                for t in range(T):
                    ins = nc.vector.tensor_scalar(yn[:, t, :], y_of(p)[:, t, :], mv[:, t, 0:1],
                                                  rstd[:, t:t + 1], ALU.subtract, ALU.mult)
                ins.then_inc(n_yn[r], 1)

            def pre_stats(k):
                def piece(i, p):
                    if k == 0:
                        dve.wait_ge(n_x[r], i + 1)
                        stats(lambda t: tile_of(X, i, t).rearrange("p a e -> p (a e)"))
                    else:
                        ch.need()
                        stats(lambda t: xa[:, t, :])
                return piece

            def with_aggregate(piece):
                def both(i, p):
                    piece(i, p)
                    aggregate(i, p)
                return [piece, aggregate] if fine else [both]

            def pre_apply(k):
                final = k == PRE[r] - 1

                def piece(i, p):
                    dve.wait_ge(n_rstd[r], i * ROUNDS[r] + POST[r] + k + 1)
                    if final:
                        dve.wait_ge(n_tp[r], reached(i))
                        if r == 1:
                            dve.wait_ge(n_u[r], reached(i))
                    for t in range(T):
                        src = tile_of(X, i, t).rearrange("p a e -> p (a e)") if k == 0 else xa[:, t, :]
                        ins = nc.vector.tensor_scalar((xn if final else xa)[:, t, :], src, mv[:, t, 0:1],
                                                      rstd[:, t:t + 1], ALU.subtract, ALU.mult)
                        if not final:
                            ch.mark(ins)
                    if final:
                        ins.then_inc(n_xn[r], 1)
                return piece

            pieces = [*with_aggregate(post_stats), post_apply]
            for k in range(PRE[r]):
                pieces += [*with_aggregate(pre_stats(k)), pre_apply(k)]
            return pieces

        def norm_marks(r):
            return T * ROUNDS[r] + (T if PRE[r] == 2 else 0)

        def rstd_pool(pool, r, i, k):
            wait_apart(pool, n_stats[r], i * ROUNDS[r] + k + 1, s_nhalf, 1)
            nc.gpsimd.tensor_scalar(ve[:, :], mv[:, :, 1], EPS, None, ALU.add).then_inc(p_chain[r], 1)
            pool.wait_ge(p_chain[r], i * ROUNDS[r] + k + 1)
            nc.gpsimd.tensor_tensor(rstd[:, :], ve[:, :], nhalf[:, 0:T], ALU.pow).then_inc(n_rstd[r], 1)

        def residual_pool(pool, r, i):
            pool.wait_ge(n_yn[r], i + 1)
            xs = seq_tiles(X, i)
            nc.gpsimd.tensor_tensor(xs, xs, yn[:, :, :], ALU.add).then_inc(n_x[r], 1)

        def norm_pool(pool, r, i, k):
            rstd_pool(pool, r, i, k)
            if k == 0 and POST[r]:
                residual_pool(pool, r, i)
            if k == ROUNDS[r] - 1 and r == 1:
                pool.wait_ge(n_xn[r], i + 1)
                nc.gpsimd.tensor_copy(seq_tiles(U, i), xn[:, :, :]).then_inc(n_u[r], 1)

        def norm_tensor(pe, r, i, NT=NT):
            pe.wait_ge(n_xn[r], i + 1)
            pe.wait_ge(n_xnT[r], reached(i))
            for t in range(T):
                ins = nc.tensor.transpose(NT[:, t * P:(t + 1) * P], xn[:, t, :], ident[:, :])
            ins.then_inc(n_tp[r], 1)

        def norm_scalar(act, r, i, NT=NT):
            act.wait_ge(n_tp[r], i + 1)
            if r == 2:
                ins = nc.scalar.activation(seq_cols(XnT, i), NT, ACT.Identity, bias=gb[:, 1:2], scale=gb[:, 0:1])
            else:
                ins = nc.scalar.activation(seq_cols(XnT, i), NT, ACT.Copy)
            ins.then_inc(n_xnT[r], 1)

        def pool_xT(pool, l, i, p):
            last_use, per_seq = ((a_v, 1), (b_x, UNITS_B))[l]
            pool.wait_ge(last_use, reached(per_seq * (i - 1)))
            if l == MOE and i_is(i, 0, 1):
                pool.wait_ge(a_v, SEQS)
                pool.wait_ge(n_xnT[1], i + 1)
            nc.gpsimd.tensor_copy(xT[:, p, :], seq_cols(XnT, i)).then_inc(x_ready[l], 1)

        carve = carver(la_work, LA_WORK)
        VA = LA_D + 1
        neg = carve(BLK)
        ex = carve(BLK)
        qk = carve(2, BLK)
        qblk = carve(2, LA_PER_GROUP, LEN)
        kblk = carve(2, LA_GROUPS, LEN)
        va = carve(2, T, LA_HEADS * VA)
        at = carve(4, LA_PER_GROUP, P)
        ktok = carve(P)
        state = carve(LA_HEADS * VA)
        den = carve(T * LA_HEADS)
        rden = carve(T * LA_HEADS)
        o = carve(T, E)
        oT = carve(LEN)
        QKB, TB, NB = bank[1], bank[2], bank[3]
        KTB = TB[:, 256:256 + P]
        STB = TB[:, 256:256 + LA_HEADS * VA]
        SC = bank[4:8]
        N = NB[:, 0:T * LA_HEADS * VA]
        NH = N.rearrange("p (h c) -> p h c", c=VA)
        a_neg, a_exp, a_feat, a_qb, a_kb, a_va = (
            sem(n) for n in ("a_neg", "a_exp", "a_feat", "a_qb", "a_kb", "a_va"))
        a_s, a_m = sem("a_s"), sem("a_m")
        a_kt, a_ktok, a_sg, a_state = (sem(n) for n in ("a_kt", "a_ktok", "a_sg", "a_state"))
        a_nd, a_den, a_rden, a_o, a_ot, a_oT = (
            sem(n) for n in ("a_nd", "a_den", "a_rden", "a_o", "a_ot", "a_oT"))
        G4 = LA_GROUPS
        UNITS_A = 2 * LA_GROUPS

        def la_qk_tensor(pe, i, p):
            pe.wait_ge(x_ready[LA], i + 1)
            pe.wait_ge(a_feat, reached(i))
            nc.tensor.matmul(QKB[:, 0:LEN], la_qkv[:, 0:E], xT[:, p, :], start=True, stop=True)
            nc.tensor.matmul(QKB[:, LEN:2 * LEN], la_qkv[:, E:2 * E], xT[:, p, :], start=True, stop=True)\
                .then_inc(a_qk, 1)

        def la_v_tensor(pe, i, p):
            pe.wait_ge(x_ready[LA], i + 1)
            pe.wait_ge(a_state, reached(i))
            for t in range(T):
                ins = nc.tensor.matmul(TB[:, t * E:(t + 1) * E], xT[:, p, t * P:(t + 1) * P],
                                       la_qkv[:, 2 * E:3 * E], start=True, stop=True)
            ins.then_inc(a_v, 1)

        def la_feat_vector(dve, i, p, part):
            if part == 0:
                dve.wait_ge(a_qk, i + 1)
                dve.wait_ge(a_exp, reached(i))
                nc.vector.tensor_scalar(neg, QKB[:, :], 0.0, None, ALU.min).then_inc(a_neg, 1)
            else:
                dve.wait_ge(a_exp, i + 1)
                dve.wait_ge(a_nd, reached(G4 * (i - 1)))
                nc.vector.scalar_tensor_tensor(qk[:, p, :], QKB[:, :], 0.0, ex, ALU.max, ALU.add)\
                    .then_inc(a_feat, 1)

        def la_exp_scalar(act, i):
            act.wait_ge(a_neg, i + 1)
            act.wait_ge(a_feat, reached(i))
            nc.scalar.activation(ex, neg, ACT.Exp).then_inc(a_exp, 1)

        def la_v_scalar(act, i, p):
            act.wait_ge(a_v, i + 1)
            act.wait_ge(a_nd, reached(G4 * (i - 1)))
            nc.scalar.activation(va[:, p, :, :].rearrange("p t (h c) -> p (t h) c", c=VA)[:, :, 0:LA_D],
                                 TB[:, 0:T * E].rearrange("p (a c) -> p a c", c=LA_D), ACT.Copy)\
                .then_inc(a_va, 1)

        def la_blocks_scalar(act, i, p):
            act.wait_ge(a_feat, i + 1)
            act.wait_ge(a_nd, reached(G4 * (i - 1)))
            for j in range(LA_PER_GROUP):
                ins = nc.scalar.activation(qblk[:, p, j, :], qk[:, p, 0:LEN], ACT.Copy, scale=hm[:, j:j + 1])
            ins.then_inc(a_qb, 1)
            for g in range(LA_GROUPS):
                nc.scalar.activation(kblk[:, p, g, :], qk[:, p, LEN:2 * LEN], ACT.Copy, scale=gm[:, g:g + 1])\
                    .then_inc(a_kb, 1)

        def la_scores_tensor(pe, i, p, g, t):
            u = 2 * g + t
            if u == 0:
                pe.wait_ge(a_qb, i + 1)
            if t == 0:
                pe.wait_ge(a_kb, G4 * i + g + 1)
            pe.wait_ge(a_m, reached(UNITS_A * i + u - 3))
            nc.tensor.matmul(SC[u % 4][:, :], kblk[:, p, g, t * P:(t + 1) * P],
                             qblk[:, p, :, t * P:(t + 1) * P], start=True, stop=True).then_inc(a_s, 1)

        def la_mask_vector(dve, i, g, t):
            u = 2 * g + t
            tri4 = tri[:, :].rearrange("p (o l) -> p o l", o=1).to_broadcast([P, LA_PER_GROUP, P])
            dve.wait_ge(a_s, UNITS_A * i + u + 1)
            dve.wait_ge(a_nd, reached(G4 * i + g - 1))
            nc.vector.tensor_tensor(at[:, u % 4, :, :], SC[u % 4][:, :].rearrange("p (j l) -> p j l", j=LA_PER_GROUP),
                                    tri4, ALU.mult).then_inc(a_m, 1)

        def la_ktok_tensor(pe, i, p):
            pe.wait_ge(a_va, i + 1)
            pe.wait_ge(a_oT, reached(i - 1))
            pe.wait_ge(a_feat, i + 1)
            nc.tensor.transpose(KTB, qk[:, p, LEN:LEN + P], ident[:, :]).then_inc(a_kt, 1)

        def la_ktok_scalar(act, i):
            act.wait_ge(a_kt, i + 1)
            act.wait_ge(a_sg, reached(i))
            nc.scalar.activation(ktok, KTB, ACT.Copy).then_inc(a_ktok, 1)

        def la_state_tensor(pe, i, p):
            pe.wait_ge(a_ktok, i + 1)
            nc.tensor.matmul(STB, ktok, va[:, p, 0, :], start=True, stop=True).then_inc(a_sg, 1)

        def la_state_vector(dve, i):
            dve.wait_ge(a_sg, i + 1)
            dve.wait_ge(a_nd, reached(G4 * i))
            nc.vector.tensor_tensor(state, STB, sm[:, :, :].rearrange("p h c -> p (h c)"), ALU.mult)\
                .then_inc(a_state, 1)

        def la_sums_tensor(pe, i, p, g):
            if g == 0:
                pe.wait_ge(a_o, reached(i))
                pe.wait_ge(a_va, i + 1)
            if g == 0:
                pe.wait_ge(a_state, i + 1)
                nc.tensor.matmul(N[:, LA_HEADS * VA:2 * LA_HEADS * VA], qk[:, p, P:2 * P], state,
                                 start=True, stop=False)
            pe.wait_ge(a_m, UNITS_A * i + 2 * g + 2)
            for t in range(T):
                for j in range(LA_PER_GROUP):
                    h = LA_PER_GROUP * g + j
                    ins = nc.tensor.matmul(NH[:, t * LA_HEADS + h, :], at[:, (2 * g + t) % 4, j, :],
                                           va[:, p, t, h * VA:(h + 1) * VA], start=False,
                                           stop=(t == T - 1 and h == LA_HEADS - 1))
            ins.then_inc(a_nd, 1)

        def la_divide_vector(dve, i):
            dve.wait_ge(a_nd, G4 * (i + 1))
            nc.vector.tensor_scalar(den, NH[:, :, LA_D], 1e-6, None, ALU.max).then_inc(a_den, 1)
            dve.wait_ge(a_den, i + 1)
            nc.vector.reciprocal(rden, den).then_inc(a_rden, 1)
            dve.wait_ge(a_rden, i + 1)
            dve.wait_ge(a_ot, reached(i))
            nc.vector.tensor_tensor(
                o.rearrange("p t (h c) -> p (t h) c", c=LA_D), NH[:, :, 0:LA_D],
                rden.rearrange("p (h c) -> p h c", c=1).to_broadcast([P, T * LA_HEADS, LA_D]), ALU.mult)\
                .then_inc(a_o, 1)

        def la_turn_tensor(pe, i):
            pe.wait_ge(a_o, i + 1)
            pe.wait_ge(a_state, at_most_all(i + 2))
            pe.wait_ge(a_va, at_most_all(i + 3))
            pe.wait_ge(n_xnT[1], reached(i - 1))
            for t in range(T):
                ins = nc.tensor.transpose(TB[:, t * P:(t + 1) * P], o[:, t, :], ident[:, :])
            ins.then_inc(a_ot, 1)

        def la_turn_scalar(act, i):
            act.wait_ge(a_ot, i + 1)
            act.wait_ge(y_ready[LA], reached(i))
            nc.scalar.activation(oT, TB[:, 0:LEN], ACT.Copy).then_inc(a_oT, 1)

        def la_out_tensor(pe, i):
            pe.wait_ge(a_oT, i + 1)
            pe.wait_ge(n_yn[1], reached(i))
            for t in range(T):
                ins = nc.tensor.matmul(Yt[:, t, :], oT[:, t * P:(t + 1) * P], la_out[:, :], start=True, stop=True)
            ins.then_inc(y_ready[LA], 1)

        zstat = carve(2, CHUNK, 6)
        zmv = carve(2, CHUNK, 2)
        zve = carve(2, CHUNK)
        zrstd = carve(2, CHUNK)
        zxn = carve(2, CHUNK, E)
        ZB = bank[4:8]
        z_chain, z_stats, z_ve, z_rstd, z_xn, z_tp, z_xnT = (
            sem(n) for n in ("z_chain", "z_stats", "z_ve", "z_rstd", "z_xn", "z_tp", "z_xnT"))

        def first_stats_vector(dve, c):
            dve.wait_ge(s_x[c], 16)
            if c >= 2:
                dve.wait_ge(z_rstd, c - 1)
            for k in range(CHUNK):
                nc.vector.bn_stats(zstat[:, c % 2, k, :], X[:, c * CHUNK + k, :]).then_inc(z_chain, 1)
            dve.wait_ge(z_chain, CHUNK * (c + 1))
            for k in range(CHUNK):
                ins = nc.vector.bn_aggr(zmv[:, c % 2, k, :], zstat[:, c % 2, k, :])
            ins.then_inc(z_stats, 1)

        def first_apply_vector(dve, c):
            dve.wait_ge(z_rstd, c + 1)
            if c >= 2:
                dve.wait_ge(z_tp, c - 1)
            for k in range(CHUNK):
                ins = nc.vector.tensor_scalar(zxn[:, c % 2, k, :], X[:, c * CHUNK + k, :],
                                              zmv[:, c % 2, k, 0:1], zrstd[:, c % 2, k:k + 1],
                                              ALU.subtract, ALU.mult)
            ins.then_inc(z_xn, 1)

        def first_rstd_pool(pool, c):
            pool.wait_ge(z_stats, c + 1)
            nc.gpsimd.tensor_scalar(zve[:, c % 2, :], zmv[:, c % 2, :, 1], EPS, None, ALU.add).then_inc(z_ve, 1)
            pool.wait_ge(z_ve, c + 1)
            if c >= 2:
                pool.wait_ge(z_xn, c - 1)
            nc.gpsimd.tensor_tensor(zrstd[:, c % 2, :], zve[:, c % 2, :], nhalf[:, :], ALU.pow)\
                .then_inc(z_rstd, 1)

        def first_turn_tensor(pe, c):
            pe.wait_ge(z_xn, c + 1)
            if c >= 2:
                pe.wait_ge(z_xnT, c - 1)
            for k in range(CHUNK):
                ins = nc.tensor.transpose(ZB[2 * (c % 2) + k // 4][:, k % 4 * P:(k % 4 + 1) * P],
                                          zxn[:, c % 2, k, :], ident[:, :])
            ins.then_inc(z_tp, 1)

        def first_turn_scalar(act, c):
            act.wait_ge(z_tp, c + 1)
            for k in range(2):
                ins = nc.scalar.activation(XnT[:, (2 * c + k) * BLK:(2 * c + k + 1) * BLK],
                                           ZB[2 * (c % 2) + k][:, :], ACT.Copy)
            ins.then_inc(z_xnT, 1)

        LA_LAG = 2

        carve = carver(moe_work, MOE_WORK)
        zr = carve(T, EXPERTS)
        t8 = carve(T, 8)
        ixf = carve(T, 2)
        nm = carve(T)
        ez = carve(T, EXPERTS)
        zs = carve(T)
        e2 = carve(T, 2)
        rz = carve(T)
        g2 = carve(T, 2)
        oh = carve(2, T, EXPERTS)
        gates = carve(2, T, EXPERTS)
        gT = carve(2, LEN)[0:EXPERTS, :, :]
        acc = carve(2, T, E)
        tmp = carve(T, PER_BANK, E)
        tsum = carve(T, E)
        RB, SHB = bank[1], bank[0]
        XB0, XB = bank[2:4], bank[4:8]

        def unit_bank(p, b, t):
            return XB[(p * (UNITS_B - T) + (b - 1) * T + t) % 4] if b else XB0[t]
        b_z, b_nm, b_e, b_g, b_gt, b_gs, b_sh, b_acc = (
            sem(n) for n in ("b_z", "b_nm", "b_e", "b_g", "b_gt", "b_gs", "b_sh", "b_acc"))
        y_ready[MOE] = b_acc
        b_x = sem("b_x")
        b_tmp, b_pair, b_tsum = sem("b_tmp"), sem("b_pair"), sem("b_tsum")
        ACCS = 1 + EXPERTS - PER_BANK + 1

        def added(i, e, t):
            return (i * ACCS + 1 + e - PER_BANK) * T + t + 1

        def moe_router_tensor(pe, i, p):
            pe.wait_ge(x_ready[MOE], i + 1)
            pe.wait_ge(b_gs, reached(i))
            for t in range(T):
                ins = nc.tensor.matmul(RB[:, t * EXPERTS:(t + 1) * EXPERTS], xT[:, p, t * P:(t + 1) * P],
                                       centT[:, :], start=True, stop=True)
            ins.then_inc(b_z, 1)

        def moe_gates_tensor(pe, i, p):
            pe.wait_ge(b_g, i + 1)
            for t in range(T):
                ins = nc.tensor.transpose(RB[0:EXPERTS, 256 + t * P:256 + (t + 1) * P], gates[:, p, t, :],
                                          ident[:, :])
            ins.then_inc(b_gt, 1)

        MOE_ROUTER_MARKS, MOE_ROUTER_PARTS = 13, 8
        MOE_EXP_PART = 4

        def moe_router_vector(dve, ch, i, p, part):
            if part == 0:
                dve.wait_ge(b_z, i + 1)
                bias = ebias[:, :].rearrange("p (o e) -> p o e", o=1).to_broadcast([P, T, EXPERTS])
                dve.wait_ge(b_e, reached(i))
                ch.mark(nc.vector.tensor_tensor(zr, RB[:, 0:T * EXPERTS].rearrange("p (t e) -> p t e", t=T),
                                                bias, ALU.add))
            elif part == 1:
                ch.need_apart()
                for t in range(T):
                    ch.mark(nc.vector.max(t8[:, t, :], zr[:, t, :]))
            elif part == 2:
                ch.need_apart()
                nc.vector.tensor_scalar(nm, t8[:, :, 0], -1.0, None, ALU.mult).then_inc(b_nm, 1)
                for t in range(T):
                    ch.mark(nc.vector.max_index(ix8[:, t, :], t8[:, t, :], zr[:, t, :]))
            elif part == 3:
                ch.need()
                ch.mark(nc.vector.tensor_copy(ixf, ix8[:, :, 0:2]))
            elif part == 4:
                dve.wait_ge(b_e, i + 1)
                ch.mark(nc.vector.reciprocal(rz, zs))
            elif part == 5:
                ch.need()
                for t in range(T):
                    ch.mark(nc.vector.tensor_scalar(g2[:, t, :], e2[:, t, :], rz[:, t:t + 1], None, ALU.mult))
            elif part == 6:
                ch.need()
                for t in range(T):
                    for k in range(2):
                        ch.mark(nc.vector.tensor_scalar(oh[:, k, t, :], iota[:, :], ixf[:, t, k:k + 1],
                                                        g2[:, t, k:k + 1], ALU.is_equal, ALU.mult))
            else:
                ch.need()
                dve.wait_ge(b_gt, reached(i - 1))
                nc.vector.tensor_tensor(gates[:, p, :, :], oh[:, 0, :, :], oh[:, 1, :, :], ALU.add)\
                    .then_inc(b_g, 1)

        def moe_router_scalar(act, i, p):
            act.wait_ge(b_nm, i + 1)
            act.wait_ge(b_g, reached(i))
            for t in range(T):
                nc.scalar.activation(ez[:, t, :], zr[:, t, :], ACT.Exp, bias=nm[:, t:t + 1],
                                     accum_out=zs[:, t:t + 1])
            for t in range(T):
                ins = nc.scalar.activation(e2[:, t, :], t8[:, t, 0:2], ACT.Exp, bias=nm[:, t:t + 1])
            ins.then_inc(b_e, 1)

        def moe_gates_scalar(act, i, p):
            act.wait_ge(b_gt, i + 1)
            act.wait_ge(b_sh, reached(i - 1))
            nc.scalar.activation(gT[:, p, :], RB[0:EXPERTS, 256:256 + LEN], ACT.Copy).then_inc(b_gs, 1)

        def moe_shared_tensor(pe, i, p):
            pe.wait_ge(b_gs, i + 1)
            pe.wait_ge(b_acc, reached((i - 1) * T * ACCS + T))
            pe.wait_ge(n_xnT[2], reached(i - 2))
            for t in range(T):
                o = SHB[:, t * E:(t + 1) * E]
                nc.tensor.matmul(o, xT[:, p, t * P:(t + 1) * P], Wsh[:, :], start=True, stop=False)
                nc.tensor.matmul(o, gT[:, p, t * P:(t + 1) * P], br[:, :], start=False, stop=False)
                ins = nc.tensor.matmul(o, half[:, :], bs[:, :], start=False, stop=True)
            ins.then_inc(b_sh, 1)

        def moe_unit_tensor(pe, i, p, u):
            t, b = u % T, u // T
            if b == 0:
                pe.wait_ge(b_tmp, reached(2 * (i - 1) + t + 1))
            else:
                block, back = (None, (2, 1), (3, 1), (1, 0))[b]
                pe.wait_ge(b_acc, reached(added(i - back, (block + 1) * PER_BANK - 1, t)))
            ins = nc.tensor.matmul(unit_bank(p, b, t)[:, :], xT[:, p, t * P:(t + 1) * P],
                                   WrT[:, b * BLK:(b + 1) * BLK], start=True, stop=True)
            ins.then_inc(b_x, 1)

        def moe_start_vector(dve, i, p):
            dve.wait_ge(b_sh, i + 1)
            dve.wait_ge(n_u[1], i + 1)
            for t in range(T):
                nc.vector.tensor_tensor(acc[:, p, t, :], SHB[:, t * E:(t + 1) * E],
                                        tile_of(U, i, t).rearrange("p a e -> p (a e)"), ALU.add)\
                    .then_inc(b_acc, 1)

        def moe_expert_vector(dve, i, p, e):
            b, k = e // PER_BANK, e % PER_BANK
            for t in range(T):
                if k == 0:
                    dve.wait_ge(b_x, i * UNITS_B + b * T + t + 1)
                dve.wait_ge(b_acc, reached(added(i, e - 1, t)))
                nc.vector.scalar_tensor_tensor(
                    acc[:, p, t, :], unit_bank(p, b, t)[:, k * E:(k + 1) * E], gates[:, p, t, e:e + 1],
                    acc[:, p, t, :], ALU.mult, ALU.add).then_inc(b_acc, 1)

        def moe_block_scalar(act, i, p):
            for t in range(T):
                act.wait_ge(b_x, i * UNITS_B + t + 1)
                if t == 0:
                    act.wait_ge(b_tsum, reached(i))
                for e in range(PER_BANK):
                    ins = nc.scalar.activation(tmp[:, t, e, :], XB0[t][:, e * E:(e + 1) * E], ACT.Copy,
                                               scale=gates[:, p, t, e:e + 1])
                ins.then_inc(b_tmp, 1)

        def moe_block_pool(pool, i):
            pool.wait_ge(b_tmp, 2 * i + 2)
            nc.gpsimd.tensor_tensor(tmp[:, :, 0:2, :], tmp[:, :, 0:2, :], tmp[:, :, 2:4, :], ALU.add)\
                .then_inc(b_pair, 1)
            pool.wait_ge(b_pair, i + 1)
            pool.wait_ge(b_acc, reached(i * T * ACCS))
            nc.gpsimd.tensor_tensor(tsum, tmp[:, :, 0, :], tmp[:, :, 1, :], ALU.add).then_inc(b_tsum, 1)

        def moe_end_vector(dve, i, p):
            dve.wait_ge(b_tsum, i + 1)
            dve.wait_ge(b_acc, (i + 1) * T * ACCS - T)
            nc.vector.tensor_tensor(acc[:, p, :, :], acc[:, p, :, :], tsum, ALU.add).then_inc(b_acc, T)

        MOE_SLOTS = ((("norm", 0), ("router", 0)), (("norm", 1), ("router", 1)), (("router", 2),),
                     (("norm", 2), ("router", 3)), (("router", 4),), (("norm", 3), ("router", 5)),
                     (("norm", 4), ("router", 6)), (("router", 7),), (("norm", 5),),
                     (("norm", 6), ("norm", 7)), (), (("norm", 8),))
        assert len(MOE_SLOTS) == EXPERTS - PER_BANK

        carve = carver(work2, SECOND)
        pr = carve(2, T, LEN)
        pn = carve(2, T, LEN)
        pT = carve(2, T, LEN)
        oTs = carve(2, PAIRS, LEN)
        nmax = carve(HEADS, T)
        psum_ = carve(HEADS, T)
        prec = carve(HEADS, T)
        V = carve(2, T, INNER)[:, ::-1]
        assert MOE_END <= 3 * 2 * T * LEN + 2 * PAIRS * LEN + 3 * HEADS * T + T * INNER
        QT = carve(2, PAIRS, LEN)
        KT = carve(2, PAIRS, LEN)
        rc = carve(2, BLK)
        rs_ = carve(2, BLK)
        rq = carve(4, BLK)
        SB_, PB, OB, JB = bank[1:3], bank[3:5], bank[5], bank[6:8]
        c_s, c_max, c_exp, c_rec, c_pn, c_t, c_pte, c_v, c_oe = (
            sem(n) for n in ("c_s", "c_max", "c_exp", "c_rec", "c_pn", "c_t", "c_pte", "c_v", "c_oe"))
        c_whi, c_w, c_xhi, c_x = (sem(n) for n in ("c_whi", "c_w", "c_xhi", "c_x"))
        c_junit = sem("c_junit")
        c_jv = sem("c_jv")
        c_js = sem("c_js")
        c_mul = sem("c_mul")
        c_rope = sem("c_rope")

        slots = [[] for _ in range(HEADS)]
        for t in range(T):
            for b in range(BLOCKS):
                slots[t * BLOCKS + b].append(("rope" if b < 4 else "v", t, b))
                if b < 4:
                    slots[t * BLOCKS + b + 4].append(("turn", t, b))
        order = [u for s in slots for u in s]
        JUNITS = len(order)
        place = {u: k for k, u in enumerate(order)}
        ROPES, TURNS = 4 * T, JUNITS - 4 * T

        def jcount(k, kinds):
            whole = sum(u[0] in kinds for u in order)
            return (k // JUNITS) * whole + sum(u[0] in kinds for u in order[:k % JUNITS])

        PROJECTIONS = T * BLOCKS
        LAST_PROJECTION = max(place[u] for u in order if u[0] != "turn")

        def sa_weights_pool(pool, part):
            for b in range(BLOCKS):
                c = slice(b * BLK, (b + 1) * BLK)
                if part == 0:
                    nc.gpsimd.tensor_copy(w_hi[:, c], w_qkv[:, c]).then_inc(c_whi, 1)
                else:
                    pool.wait_ge(c_whi, b + 1)
                    nc.gpsimd.tensor_tensor(w_lo[:, c], w_qkv[:, c], w_hi[:, c], ALU.subtract).then_inc(c_w, 1)

        def sa_input_vector(dve, i):
            dve.wait_ge(n_xnT[2], i + 1)
            dve.wait_ge(c_junit, reached((i - 1) * JUNITS + LAST_PROJECTION + 1))
            nc.vector.tensor_copy(sx_hi[:, :], seq_cols(XnT, i)).then_inc(c_xhi, 1)
            dve.wait_ge(c_xhi, i + 1)
            nc.vector.tensor_tensor(sx_lo[:, :], seq_cols(XnT, i), sx_hi[:, :], ALU.subtract).then_inc(c_x, 1)

        FIRST_BANKS = [*JB, *SB_, *PB]

        def unit_bank_sa(k, first):
            return FIRST_BANKS[k % len(FIRST_BANKS)] if first else JB[k % 2]

        def sa_unit_tensor(pe, i, p, unit, first=False):
            kind, t, b = unit
            k = place[unit]
            bank_ = unit_bank_sa(k, first)
            back = len(FIRST_BANKS) if first else 2
            if first and k < back:
                pass
            elif order[(k - back) % JUNITS][0] == "rope":
                pe.wait_ge(c_jv, reached(i * ROPES + jcount(k - back + 1, ("rope",))))
            else:
                pe.wait_ge(c_js, reached(i * TURNS + jcount(k - back + 1, ("v", "turn"))))
            if kind == "turn":
                pe.wait_ge(c_rope, i * ROPES + 4 * t + b + 1)
                for q in range(4):
                    ins = nc.tensor.transpose(bank_[:, q * P:(q + 1) * P], rq[:, b, q * P:(q + 1) * P],
                                              ident[:, :])
            else:
                if k == 0:
                    pe.wait_ge(c_x, i + 1)
                tokens, columns = slice(t * P, (t + 1) * P), slice(b * BLK, (b + 1) * BLK)
                ins = split_product(bank_[:, :], (sx_hi[:, tokens], sx_lo[:, tokens]),
                                    (w_hi[:, columns], w_lo[:, columns]), True, True)
            ins.then_inc(c_junit, 1)

        def sa_unit_vector(dve, i, p, unit, first=False):
            kind, t, b = unit
            if kind != "rope":
                return
            k = place[unit]
            ru = 4 * t + b
            dve.wait_ge(c_junit, i * JUNITS + k + 1)
            dve.wait_ge(c_rope, reached(i * ROPES + ru - 1))
            src = unit_bank_sa(k, first)[:, :].rearrange("p (h s d) -> p h s d", s=2, d=D // 2)

            def table(m):
                return rope[:, t, b // 2, m, :].rearrange("p (o s d) -> p o s d", o=1, s=2)\
                    .to_broadcast([P, BLK // D, 2, D // 2])
            dst = [a[:, b % 2, :].rearrange("p (h s d) -> p h s d", s=2, d=D // 2) for a in (rc, rs_)]
            nc.vector.tensor_tensor(dst[0], src, table(0), ALU.mult)
            nc.vector.tensor_tensor(dst[1], src[:, :, ::-1, :], table(1), ALU.mult).then_inc(c_jv, 1)

        def sa_unit_pool(pool, i, p, unit):
            kind, t, b = unit
            if kind != "rope":
                return
            ru = 4 * t + b
            pool.wait_ge(c_jv, i * ROPES + ru + 1)
            back = 0 if t > 0 else 1
            pool.wait_ge(c_junit, reached((i - back) * JUNITS + place["turn", (t - 1) % T, b] + 1))
            nc.gpsimd.tensor_tensor(rq[:, b, :], rc[:, b % 2, :], rs_[:, b % 2, :], ALU.add)\
                .then_inc(c_rope, 1)

        def sa_unit_scalar(act, i, p, unit, first=False):
            kind, t, b = unit
            if kind == "rope":
                return
            k = place[unit]
            act.wait_ge(c_junit, i * JUNITS + k + 1)
            bank_ = unit_bank_sa(k, first)
            if kind == "v":
                dst = V[:, p, t, (b - 4) * BLK:(b - 3) * BLK]
                src = bank_[:, :]
            else:
                dst = (QT if b < 2 else KT)[:, p, 4 * (b % 2):4 * (b % 2) + 4, t * P:(t + 1) * P]
                src = bank_[:, :].rearrange("p (q l) -> p q l", q=4)
            nc.scalar.activation(dst, src, ACT.Copy).then_inc(c_js, 1)

        def sa_scores_tensor(pe, i, p, h):
            n = i * HEADS + h
            if h == 0:
                pe.wait_ge(c_js, (i + 1) * TURNS)
            pe.wait_ge(c_exp, reached(n - 1))
            rows = slice(D * (h % 2), D * (h % 2) + D)
            for t in range(T):
                ins = nc.tensor.matmul(SB_[h % 2][:, t * LEN:(t + 1) * LEN], QT[rows, p, h // 2, t * P:(t + 1) * P],
                                       KT[rows, p, h // 2, :], start=True, stop=True)
            ins.then_inc(c_s, 1)

        def sa_max_vector(dve, i, h):
            n = i * HEADS + h
            dve.wait_ge(c_s, n + 1)
            if h == 0:
                dve.wait_ge(c_exp, reached(n))
            nc.vector.tensor_reduce(nmax[:, h, :], SB_[h % 2][:, :].rearrange("p (t k) -> p t k", t=T),
                                    AX.X, ALU.max, negate=True).then_inc(c_max, 1)

        def sa_exp_scalar(act, i, h):
            n = i * HEADS + h
            act.wait_ge(c_max, n + 1)
            act.wait_ge(c_pn, reached(n - 1))
            for t in range(T):
                ins = nc.scalar.activation(pr[:, h % 2, t, :], SB_[h % 2][:, t * LEN:(t + 1) * LEN], ACT.Exp,
                                           bias=nmax[:, h, t:t + 1], accum_out=psum_[:, h, t:t + 1])
            ins.then_inc(c_exp, 1)

        def sa_norm_vector(dve, i, h):
            n = i * HEADS + h
            dve.wait_ge(c_exp, n + 1)
            nc.vector.reciprocal(prec[:, h, :], psum_[:, h, :]).then_inc(c_rec, 1)
            dve.wait_ge(c_rec, n + 1)
            dve.wait_ge(c_t, reached(n - 1))
            for t in range(T):
                ins = nc.vector.tensor_scalar(pn[:, h % 2, t, :], pr[:, h % 2, t, :], prec[:, h, t:t + 1], None,
                                              ALU.mult)
            ins.then_inc(c_pn, 1)

        def sa_turn_tensor(pe, i, h):
            n = i * HEADS + h
            pe.wait_ge(c_pn, n + 1)
            pe.wait_ge(c_pte, reached(n - 1))
            for kt in range(T):
                for t in range(T):
                    ins = nc.tensor.transpose(PB[h % 2][:, kt * LEN + t * P:kt * LEN + (t + 1) * P],
                                              pn[:, h % 2, t, kt * P:(kt + 1) * P], ident[:, :])
            ins.then_inc(c_t, 1)

        def sa_turn_scalar(act, i, h):
            n = i * HEADS + h
            act.wait_ge(c_t, n + 1)
            act.wait_ge(c_v, reached(n - 1))
            nc.scalar.activation(pT[:, h % 2, :, :], PB[h % 2][:, :].rearrange("p (t q) -> p t q", t=T), ACT.Copy)\
                .then_inc(c_pte, 1)

        def sa_pv_tensor(pe, i, p, h):
            n = i * HEADS + h
            pe.wait_ge(c_pte, n + 1)
            if h % 2 == 0:
                pe.wait_ge(c_oe, reached(i * PAIRS + h // 2))
            rows = slice(D * (h % 2), D * (h % 2) + D)
            for kt in range(T):
                ins = nc.tensor.matmul(OB[rows, 0:LEN], V[:, p, kt, h * D:(h + 1) * D], pT[:, h % 2, kt, :],
                                       start=(kt == 0), stop=(kt == T - 1))
            ins.then_inc(c_v, 1)

        def sa_pv_scalar(act, i, p, h):
            act.wait_ge(c_v, i * HEADS + h + 1)
            act.wait_ge(y_ready[SA], reached(i - 1))
            nc.scalar.activation(oTs[:, p, h // 2, :], OB[:, 0:LEN], ACT.Copy).then_inc(c_oe, 1)

        def sa_out_tensor(pe, i, p):
            pe.wait_ge(c_oe, (i + 1) * PAIRS)
            pe.wait_ge(n_xnT[3], reached(i))
            for t in range(T):
                for q in range(PAIRS):
                    ins = nc.tensor.matmul(Yt[:, t, :], oTs[:, p, q, t * P:(t + 1) * P], w_out[:, q, :],
                                           start=(q == 0), stop=(q == PAIRS - 1))
            ins.then_inc(y_ready[SA], 1)

        NORM_LAG, TURN_LAG, PV_LAG = 1, 2, 3
        SA_OUT_SLOT = 4
        SA_PIECE_SLOTS = (5, 10, 12, 14)
        SA_ROUND_SLOTS, SA_RESIDUAL_SLOT = (5, 12), 10
        SA_FIRST_PIECES = [u for u in order if u[0] == "rope"][:ROUNDS[2] * 2]
        SA_FIRST_ROUNDS = SA_FIRST_PIECES[::2]
        SA_INPUT_SLOT = 13
        SA_NORM_SLOT = 15
        SA_DRAIN = SA_OUT_SLOT + 1

        def lagged(i, p, h, lag):
            if h >= lag:
                return None if i_is(i, SEQS) else (i, p, h - lag)
            return None if i_is(i, 0) else (i - 1, 1 - p, h - lag + HEADS)

        carve = carver(work3, THIRD)
        tg = carve(2, 2, LEN)
        gg = carve(2, 2, LEN)
        hT = carve(HID_T, LEN)
        f1 = carve(HID_T, LEN)
        f2 = carve(HID_T, LEN)
        yf = carve(2, T, E)
        GB, UB = (bank[1], bank[3]), (bank[2], bank[4])
        HB = bank[5:7]
        d_g, d_u, d_tanh, d_gg, d_h, d_m1, d_a1, d_m2, d_a2, d_y = (
            sem(n) for n in ("d_g", "d_u", "d_tanh", "d_gg", "d_h", "d_m1", "d_a1", "d_m2", "d_a2", "d_y"))

        d_whi, d_w, d_xhi, d_x, d_hhi, d_hs, d_fhi, d_fs = (
            sem(n) for n in ("d_whi", "d_w", "d_xhi", "d_x", "d_hhi", "d_hs", "d_fhi", "d_fs"))
        ffn_weights = [(w1T[:, :], w1S[0][:, :], w1S[1][:, :]), (w2T[:, :], w2S[0][:, :], w2S[1][:, :])]
        for full, parts in ((h1T, h1S), (h2T, h2S)):
            ffn_weights += [(full[:, k, :], parts[0][:, k, :], parts[1][:, k, :]) for k in range(HID_T)]

        def ffn_weights_scalar(act, pieces):
            for k in pieces:
                nc.scalar.activation(ffn_weights[k][1], ffn_weights[k][0], ACT.Copy).then_inc(d_whi, 1)

        def ffn_weights_vector(dve, pieces):
            for k in pieces:
                full, hi, lo = ffn_weights[k]
                dve.wait_ge(d_whi, k + 1)
                nc.vector.tensor_tensor(lo, full, hi, ALU.subtract).then_inc(d_w, 1)

        checked = [(full[:, c:c + LEN]) for full in (w1T, w2T) for c in range(0, HID_T * P, LEN)]
        checked += [full[:, k, c:c + LEN] for full in (h1T, h2T) for k in range(HID_T)
                    for c in range(0, HID_T * P, LEN)]
        WEIGHTS = len(checked) * LEN * P
        CHECK_STEPS = (0, 1, SEQS - 2, SEQS - 1)
        PER_STEP = -(-len(checked) // len(CHECK_STEPS))
        CHECK_SLOTS = range(HEADS - 1 - PER_STEP, HEADS - 1)
        cube, count = xT[:, 0, :], xT[:, 1, :]
        d_square, d_cube, d_equal, d_checked, d_row, d_count, d_ternary = (
            sem(n) for n in ("d_square", "d_cube", "d_equal", "d_checked", "d_row", "d_count", "d_ternary"))

        def check_piece(i, h):
            if not i_is(i, *CHECK_STEPS) or h not in CHECK_SLOTS:
                return None
            k = CHECK_STEPS.index(i) * PER_STEP + CHECK_SLOTS.index(h)
            return k if k < len(checked) else None

        def ffn_cube_pool(pool, k):
            if k == 0:
                pool.wait_ge(s_w[FFN], 16 * 7)
                pool.wait_ge(b_x, SEQS * UNITS_B)
                nc.gpsimd.memset(count, 0.0).then_inc(d_checked, 1)
            pool.wait_ge(d_checked, k + 1)
            nc.gpsimd.tensor_tensor(cube, checked[k], checked[k], ALU.mult).then_inc(d_square, 1)
            pool.wait_ge(d_square, k + 1)
            nc.gpsimd.tensor_tensor(cube, cube, checked[k], ALU.mult).then_inc(d_cube, 1)

        def ffn_equal_vector(dve, k):
            dve.wait_ge(d_cube, k + 1)
            nc.vector.tensor_tensor(cube, cube, checked[k], ALU.is_equal).then_inc(d_equal, 1)

        def ffn_count_pool(pool, k):
            pool.wait_ge(d_equal, k + 1)
            nc.gpsimd.tensor_tensor(count, count, cube, ALU.add).then_inc(d_checked, 1)

        def ffn_row_vector(dve):
            dve.wait_ge(d_checked, len(checked) + 1)
            nc.vector.tensor_reduce(ternary_row[:, :], count, AX.X, ALU.add).then_inc(d_row, 1)

        def ffn_count_tensor(pe):
            pe.wait_ge(d_row, 1)
            pe.wait_ge(c_jv, SEQS * ROPES)
            pe.wait_ge(c_js, SEQS * TURNS)
            nc.tensor.matmul(JB[0][0:1, 0:1], ternary_row[:, :], tri[:, P - 1:P], start=True, stop=True)\
                .then_inc(d_count, 1)

        def ffn_ternary_vector(dve):
            dve.wait_ge(d_count, 1)
            nc.vector.tensor_scalar(ternary[:, :], JB[0][0:1, 0:1], float(WEIGHTS), None, ALU.is_equal)\
                .then_inc(d_ternary, 1)

        EARLY = 2 + HID_T
        EARLY_SLOTS = range(2, 2 + EARLY)

        def ffn_input_vector(dve, i):
            dve.wait_ge(n_xnT[3], i + 1)
            dve.wait_ge(d_u, reached(2 * i))
            nc.vector.tensor_copy(xS[0][:, :], seq_cols(XnT, i)).then_inc(d_xhi, 1)
            dve.wait_ge(d_xhi, i + 1)
            nc.vector.tensor_tensor(xS[1][:, :], seq_cols(XnT, i), xS[0][:, :], ALU.subtract).then_inc(d_x, 1)

        def ffn_split_vector(dve, i, m, full, parts, hi_done, done):
            b = slice(2 * m, 2 * m + 2)
            nc.vector.tensor_copy(parts[0][:, b, :], full[:, b, :]).then_inc(hi_done, 1)
            dve.wait_ge(hi_done, 2 * i + m + 1)
            nc.vector.tensor_tensor(parts[1][:, b, :], full[:, b, :], parts[0][:, b, :], ALU.subtract)\
                .then_inc(done, 1)

        def ffn_in_tensor(pe, i, short=False):
            pe.wait_ge(d_x, i + 1)
            for m in range(2):
                for banks, wS, done, empty in ((GB, w1S, d_g, d_gg), (UB, w2S, d_u, d_h)):
                    pe.wait_ge(empty, reached(2 * (i - 1) + m + 1))
                    for k in range(2):
                        o = slice((2 * m + k) * P, (2 * m + k + 1) * P)
                        ins = split_product(banks[m][:, k * LEN:(k + 1) * LEN], (wS[0][:, o], wS[1][:, o]),
                                            (xS[0][:, :], xS[1][:, :]), True, True, short)
                    ins.then_inc(done, 1)

        def ffn_in_scalar(act, i):
            for m in range(2):
                act.wait_ge(d_g, 2 * i + m + 1)
                act.wait_ge(d_gg, reached(2 * (i - 1) + m + 1))
                for k in range(2):
                    ob = 2 * m + k
                    ins = nc.scalar.activation(tg[:, m, k, :], GB[m][:, k * LEN:(k + 1) * LEN], ACT.Tanh,
                                               scale=s1h[:, ob:ob + 1])
                ins.then_inc(d_tanh, 1)

        def ffn_in_vector(dve, i):
            for m in range(2):
                dve.wait_ge(d_tanh, 2 * i + m + 1)
                dve.wait_ge(d_h, reached(2 * (i - 1) + m + 1))
                nc.vector.scalar_tensor_tensor(gg[:, m, :, :].rearrange("p k l -> p (k l)"),
                                               tg[:, m, :, :].rearrange("p k l -> p (k l)"), 1.0, GB[m][:, :],
                                               ALU.add, ALU.mult).then_inc(d_gg, 1)
                dve.wait_ge(d_gg, 2 * i + m + 1)
                dve.wait_ge(d_u, 2 * i + m + 1)
                dve.wait_ge(d_hs, reached(2 * (i - 1) + m + 1))
                for k in range(2):
                    ob = 2 * m + k
                    ins = nc.vector.scalar_tensor_tensor(hT[:, ob, :], UB[m][:, k * LEN:(k + 1) * LEN],
                                                         s12[:, ob:ob + 1], gg[:, m, k, :], ALU.mult, ALU.mult)
                ins.then_inc(d_h, 1)
                dve.wait_ge(d_h, 2 * i + m + 1)
                if m == 0:
                    dve.wait_ge(d_m1, reached(2 * i))
                ffn_split_vector(dve, i, m, hT, hS, d_hhi, d_hs)

        def ffn_product(pe, src, wS, written, emptied, base, short):
            for m in range(2):
                pe.wait_ge(emptied, reached(base + m + 1))
                for k in range(2):
                    o = slice((2 * m + k) * P, (2 * m + k + 1) * P)
                    for kb in range(HID_T):
                        ins = split_product(HB[m][:, k * LEN:(k + 1) * LEN], (wS[0][:, kb, o], wS[1][:, kb, o]),
                                            (src[0][:, kb, :], src[1][:, kb, :]), kb == 0, kb == HID_T - 1,
                                            short)
                ins.then_inc(written, 1)

        def ffn_out_tensor(pe, i):
            pe.wait_ge(d_a2, 2 * (i + 1))
            pe.wait_ge(y_ready[FFN], reached(i))
            if i_is(i, 0):
                pe.wait_ge(n_xnT[3], SEQS)
            for t in range(T):
                for kb in range(HID_T):
                    ins = nc.tensor.matmul(Yt[:, t, :], f2[:, kb, t * P:(t + 1) * P], w3T[:, kb, :],
                                           start=(kb == 0), stop=(kb == HID_T - 1))
            ins.then_inc(d_y, 1)

        def ffn_out_vector(dve, i, p):
            dve.wait_ge(d_y, i + 1)
            nc.vector.tensor_tensor(yf[:, p, :, :], Yt,
                                    s3[:, :].rearrange("p (o e) -> p o e", o=1).to_broadcast([P, T, E]), ALU.mult)\
                .then_inc(y_ready[FFN], 1)

        block = ctx.enter_context(nc.Block())

        @block.sync
        def _(sp):
            xv = x.rearrange("b (t p) e -> p (b t) e", p=P)
            ov = out.rearrange("b (t p) e -> p (b t) e", p=P)
            for c in range(CHUNKS):
                part = slice(c * CHUNK, (c + 1) * CHUNK)
                sp.dma_start(X[:, part, :], xv[:, part, :]).then_inc(s_x[c], 16)
                if c == 0:
                    sp.dma_start(ident[:, :], const["ident"]).then_inc(s_ident, 16)
            for name, dst in (("tri", tri), ("hm", hm), ("gm", gm), ("sm", sm), ("iota", iota),
                              ("half", half), ("rope", rope)):
                sp.dma_start(dst[:], const[name]).then_inc(s_const, 16)
            sp.dma_start(la_qkv[:, :], w["L0_attn_W_qkv"]).then_inc(s_w[LA], 16)
            sp.dma_start(la_out[:, :], w["L0_attn_W_out"]).then_inc(s_w[LA], 16)
            for dst, src in ((centT[:, :], w["L0_ffn_centroids"]), (WrT[:, :], w["L0_ffn_Wr"]),
                             (br[:, :], w["L0_ffn_br"]), (WsT[:, :, :], w["L0_ffn_Ws"]), (bs[:, :], w["L0_ffn_bs"]),
                             (ebias[:, :], w["L0_ffn_expert_biases"].to_broadcast([P, EXPERTS]))):
                sp.dma_start(dst, src).then_inc(s_w[MOE], 16)
            for dst, src in ((gb[:, 0:1], w["L1_attn_ln_gamma"]), (gb[:, 1:2], w["L1_attn_ln_beta"]),
                             (w_qkv[:, :], w["L1_attn_w_qkv"]),
                             (w_out[:, :, :], w["L1_attn_w_out"].rearrange("(q p) e -> p q e", p=P))):
                sp.dma_start(dst, src).then_inc(s_w[SA], 16)
            for dst, src in ((w1T[:, :], w["L1_ffn_w1_w"]), (w2T[:, :], w["L1_ffn_w2_w"]),
                             (h1T[:, :, :], w["L1_ffn_h1_w"].rearrange("(k p) o -> p k o", p=P)),
                             (h2T[:, :, :], w["L1_ffn_h2_w"].rearrange("(k p) o -> p k o", p=P)),
                             (w3T[:, :, :], w["L1_ffn_w3_w"].rearrange("(k p) o -> p k o", p=P)),
                             (fs[:, :, :], w["L1_ffn_scales"]),
                             (s3[:, :], w["L1_ffn_w3_s"].to_broadcast([P, E]))):
                sp.dma_start(dst, src).then_inc(s_w[FFN], 16)
            with sp.Fori(0, SEQS) as i:
                sp.wait_ge(n_x[4], i + 1)
                sp.dma_start(ov[:, bass.ds(i * T, T), :], X[:, bass.ds(i * T, T), :]).then_inc(s_out, 16)
            sp.wait_ge(s_out, 16 * SEQS)

        @block.gpsimd
        def _(pool):
            nc.gpsimd.memset(nhalf[:, :], -0.5).then_inc(s_nhalf, 1)
            pool.wait_ge(s_nhalf, 1)
            for c in range(CHUNKS):
                first_rstd_pool(pool, c)

            pool.wait_ge(z_xnT, 1)
            pool_xT(pool, LA, 0, 0)
            pool_xT(pool, LA, 1, 1)

            def la_step(i, p):
                if not i_is(i, 0, 1):
                    norm_pool(pool, 1, i - LA_LAG, 0)
                if i_is(i, 0):
                    pool.wait_ge(z_xnT, CHUNKS)
                if not i_is(i, SEQS - 2, SEQS - 1):
                    pool_xT(pool, LA, i + 2, p)
                if i_is(i, 0, 1):
                    pool.wait_ge(s_w[SA], 16 * 4)
                    sa_weights_pool(pool, i)
                if not i_is(i, 0, 1):
                    norm_pool(pool, 1, i - LA_LAG, 1)
            over_sequences(pool, la_step, 4)

            pool_xT(pool, MOE, 0, 0)
            pool_xT(pool, MOE, 1, 1)
            for i in range(SEQS - LA_LAG, SEQS):
                for k in range(ROUNDS[1]):
                    norm_pool(pool, 1, i, k)
            pool.wait_ge(n_xnT[1], SEQS)

            def moe_step(i, p):
                lag = not i_is(i, 0)
                if lag:
                    rstd_pool(pool, 2, i - 1, 0)
                    residual_pool(pool, 2, i - 1)
                    rstd_pool(pool, 2, i - 1, 1)
                moe_block_pool(pool, i)
                if not i_is(i, SEQS - 2, SEQS - 1):
                    pool_xT(pool, MOE, i + 2, p)
                if lag:
                    rstd_pool(pool, 2, i - 1, 2)
            over_sequences(pool, moe_step)

            for u in order:
                sa_unit_pool(pool, 0, 0, u)
                if u in SA_FIRST_ROUNDS:
                    norm_pool(pool, 2, SEQS - 1, SA_FIRST_ROUNDS.index(u))

            def sa_step(i, p):
                more = not (i_is(i, SEQS - 1))
                for h in range(HEADS):
                    if more:
                        for u in slots[h]:
                            sa_unit_pool(pool, i + 1, 1 - p, u)
                    k = check_piece(i, h - 1)
                    if k is not None:
                        ffn_count_pool(pool, k)
                    k = check_piece(i, h)
                    if k is not None:
                        ffn_cube_pool(pool, k)
                    if h in SA_ROUND_SLOTS and not i_is(i, 0):
                        rstd_pool(pool, 3, i - 1, SA_ROUND_SLOTS.index(h))
                    if h == SA_RESIDUAL_SLOT and not i_is(i, 0):
                        residual_pool(pool, 3, i - 1)
            over_sequences(pool, sa_step)
            for k in range(ROUNDS[3]):
                norm_pool(pool, 3, SEQS - 1, k)


            def ffn_step(i, p):
                if not (i_is(i, 0)):
                    norm_pool(pool, 4, i - 1, 0)
            over_sequences(pool, ffn_step)
            norm_pool(pool, 4, SEQS - 1, 0)

        @block.vector
        def _(dve):
            chains = [Chain(dve, v_chain[r], n) for r, n in enumerate(
                (norm_marks(0), norm_marks(1), norm_marks(2), norm_marks(3), norm_marks(4)))]

            def run_piece(r, pieces, k, i, p):
                ch = chains[r]
                if k == 0:
                    ch.begin(i)
                pieces[k](i, p)
                if k == len(pieces) - 1:
                    ch.end()

            nc.vector.memset(va.rearrange("p a t c -> p (a t c)"), 1.0).then_inc(s_va, 1)
            first_stats_vector(dve, 0)
            for c in range(CHUNKS):
                if c < CHUNKS - 1:
                    first_stats_vector(dve, c + 1)
                first_apply_vector(dve, c)

            dve.wait_ge(s_const, 16 * 7)
            for part in range(2):
                la_feat_vector(dve, 0, 0, part)
            n1 = norm_vector(dve, 1, chains[1], lambda p: Yt)

            def la_step(i, p):
                more, live = not i_is(i, SEQS - 1, SEQS), not i_is(i, SEQS)
                for g in range(LA_GROUPS):
                    if g == 1 and not i_is(i, 0):
                        la_divide_vector(dve, i - 1)
                    if live:
                        la_mask_vector(dve, i, g, 0)
                    if g == 0 and live:
                        la_state_vector(dve, i)
                    if g == 1 and more:
                        la_feat_vector(dve, i + 1, 1 - p, 0)
                    if not i_is(i, 0, 1):
                        run_piece(1, n1, g, i - LA_LAG, p)
                    if live:
                        la_mask_vector(dve, i, g, 1)
                    if g == 2 and more:
                        la_feat_vector(dve, i + 1, 1 - p, 1)
            over_sequences(dve, la_step, 4)

            rch = Chain(dve, b_rch, MOE_ROUTER_MARKS)
            rch.begin(0)
            for part in range(MOE_EXP_PART):
                moe_router_vector(dve, rch, 0, 0, part)
            dve.wait_ge(s_w[MOE], 16 * 6)
            nc.vector.tensor_tensor(Wsh[:, :], WsT[:, 0, :], WsT[:, 1, :], ALU.add).then_inc(s_wsh, 1)
            dve.wait_ge(s_wsh, 1)
            nc.vector.tensor_scalar(Wsh[:, :], Wsh[:, :], 0.5, None, ALU.mult).then_inc(s_wsh, 1)
            la_step(SEQS, 0)
            for part in range(MOE_EXP_PART, MOE_ROUTER_PARTS):
                moe_router_vector(dve, rch, 0, 0, part)
            rch.end()
            for k in range(len(n1)):
                run_piece(1, n1, k, SEQS - 1, 1)

            n2 = norm_vector(dve, 2, chains[2], lambda p: acc[:, p, :, :], T * ACCS, fine=True)

            def moe_step(i, p):
                moe_start_vector(dve, i, p)
                for slot, works in enumerate(MOE_SLOTS):
                    moe_expert_vector(dve, i, p, PER_BANK + slot)
                    for what, part in works:
                        if what == "norm" and not i_is(i, 0):
                            run_piece(2, n2, part, i - 1, 1 - p)
                        if what == "router" and not i_is(i, SEQS - 1):
                            if part == 0:
                                rch.begin(i + 1)
                            moe_router_vector(dve, rch, i + 1, 1 - p, part)
                moe_end_vector(dve, i, p)
            over_sequences(dve, moe_step)

            sa_input_vector(dve, 0)
            for u in order:
                sa_unit_vector(dve, 0, 0, u, True)
                if u in SA_FIRST_PIECES:
                    k = SA_FIRST_PIECES.index(u)
                    for piece in ((k // 2 * 3, k // 2 * 3 + 1) if k % 2 == 0 else (k // 2 * 3 + 2,)):
                        run_piece(2, n2, piece, SEQS - 1, 1)
            sa_input_vector(dve, 1)
            n3 = norm_vector(dve, 3, chains[3], lambda p: Yt)

            def sa_slot(i, p, h):
                if not i_is(i, SEQS):
                    sa_max_vector(dve, i, h)
                at = lagged(i, p, h, NORM_LAG)
                if at:
                    sa_norm_vector(dve, at[0], at[2])

            def sa_step(i, p):
                for h in range(HEADS):
                    sa_slot(i, p, h)
                    if not i_is(i, SEQS - 1):
                        for u in slots[h]:
                            sa_unit_vector(dve, i + 1, 1 - p, u)
                    k = check_piece(i, h - 1)
                    if k is not None:
                        ffn_equal_vector(dve, k)
                    if i_is(i, SEQS - 1) and h in EARLY_SLOTS:
                        ffn_weights_vector(dve, [EARLY_SLOTS.index(h)])
                    if h == SA_INPUT_SLOT and not i_is(i, SEQS - 2, SEQS - 1):
                        sa_input_vector(dve, i + 2)
                    if h in SA_PIECE_SLOTS and not i_is(i, 0):
                        run_piece(3, n3, SA_PIECE_SLOTS.index(h), i - 1, 1 - p)
            over_sequences(dve, sa_step)
            for h in range(SA_DRAIN):
                sa_slot(SEQS, 0, h)

            ffn_row_vector(dve)
            nc.vector.tensor_scalar(s1h[:, :], fs[:, 0, :], 0.5, None, ALU.mult).then_inc(s_fs, 1)
            dve.wait_ge(s_fs, 1)
            nc.vector.tensor_tensor(s12[:, :], s1h[:, :], fs[:, 1, :], ALU.mult).then_inc(s_fs, 1)
            dve.wait_ge(s_fs, 2)
            ffn_input_vector(dve, 0)
            ffn_ternary_vector(dve)
            run_piece(3, n3, 0, SEQS - 1, 1)
            ffn_in_vector(dve, 0)
            run_piece(3, n3, 1, SEQS - 1, 1)
            ffn_weights_vector(dve, range(EARLY, EARLY + HID_T // 2))
            run_piece(3, n3, 2, SEQS - 1, 1)
            ffn_weights_vector(dve, range(EARLY + HID_T // 2, EARLY + HID_T))
            run_piece(3, n3, 3, SEQS - 1, 1)
            n4 = norm_vector(dve, 4, chains[4], lambda p: yf[:, p, :, :])

            def ffn_step(i, p):
                more, behind = not i_is(i, SEQS - 1), not i_is(i, 0)
                if more:
                    ffn_input_vector(dve, i + 1)
                for m in range(2):
                    dve.wait_ge(d_a1, 2 * i + m + 1)
                    if m == 0:
                        dve.wait_ge(d_m2, reached(2 * i))
                    ffn_split_vector(dve, i, m, f1, f1S, d_fhi, d_fs)
                if more:
                    ffn_in_vector(dve, i + 1)
                if behind:
                    ffn_out_vector(dve, i - 1, 1 - p)
                    run_piece(4, n4, 0, i - 1, 1 - p)
                    run_piece(4, n4, 1, i - 1, 1 - p)
            over_sequences(dve, ffn_step)
            ffn_out_vector(dve, SEQS - 1, 1)
            for k in range(len(n4)):
                run_piece(4, n4, k, SEQS - 1, 1)

        @block.scalar
        def _(act):
            for c in range(CHUNKS):
                first_turn_scalar(act, c)

            act.wait_ge(s_va, 1)
            la_exp_scalar(act, 0)
            la_v_scalar(act, 0, 0)
            la_blocks_scalar(act, 0, 0)
            la_ktok_scalar(act, 0)

            def la_step(i, p):
                more = not i_is(i, SEQS - 1, SEQS)
                if more:
                    la_exp_scalar(act, i + 1)
                    la_v_scalar(act, i + 1, 1 - p)
                if not i_is(i, 0):
                    la_turn_scalar(act, i - 1)
                if more:
                    la_blocks_scalar(act, i + 1, 1 - p)
                if not i_is(i, 0, 1):
                    norm_scalar(act, 1, i - LA_LAG, TB[:, 0:LEN])
                if more:
                    la_ktok_scalar(act, i + 1)
            over_sequences(act, la_step, 4)

            moe_router_scalar(act, 0, 0)
            la_step(SEQS, 0)
            moe_gates_scalar(act, 0, 0)
            norm_scalar(act, 1, SEQS - 1, TB[:, 0:LEN])
            act.wait_ge(s_w[SA], 16 * 4)

            def moe_step(i, p):
                if not i_is(i, SEQS):
                    moe_block_scalar(act, i, p)
                if not i_is(i, SEQS - 1, SEQS):
                    moe_router_scalar(act, i + 1, 1 - p)
                if not i_is(i, 0, 1):
                    norm_scalar(act, 2, i - 2)
                if not i_is(i, SEQS - 1, SEQS):
                    moe_gates_scalar(act, i + 1, 1 - p)
            over_sequences(act, moe_step, 4)
            moe_step(SEQS, 0)

            for u in order:
                sa_unit_scalar(act, 0, 0, u, True)
            norm_scalar(act, 2, SEQS - 1)

            def sa_slot(i, p, h):
                at = lagged(i, p, h, TURN_LAG)
                if at:
                    sa_turn_scalar(act, at[0], at[2])
                if not i_is(i, SEQS):
                    sa_exp_scalar(act, i, h)
                if not i_is(i, SEQS) and not i_is(i, SEQS - 1):
                    for u in slots[h]:
                        sa_unit_scalar(act, i + 1, 1 - p, u)
                at = lagged(i, p, h, PV_LAG)
                if at and at[2] % 2 == 1:
                    sa_pv_scalar(act, *at)

            def sa_step(i, p):
                for h in range(HEADS):
                    sa_slot(i, p, h)
                    if i_is(i, SEQS - 1) and h in EARLY_SLOTS:
                        if h == EARLY_SLOTS[0]:
                            act.wait_ge(s_w[FFN], 16 * 7)
                            act.wait_ge(c_junit, SEQS * JUNITS)
                        ffn_weights_scalar(act, [EARLY_SLOTS.index(h)])
                    if h == SA_NORM_SLOT and not i_is(i, 0):
                        norm_scalar(act, 3, i - 1)
            over_sequences(act, sa_step)
            for h in range(SA_DRAIN):
                sa_slot(SEQS, 0, h)

            act.wait_ge(s_fs, 2)
            act.wait_ge(y_ready[SA], SEQS)
            ffn_in_scalar(act, 0)
            ffn_weights_scalar(act, range(EARLY, EARLY + HID_T))

            def gelu(i, product, dst, written, done):
                for m in range(2):
                    act.wait_ge(written, 2 * i + m + 1)
                    for k in range(2):
                        ob = 2 * m + k
                        ins = nc.scalar.activation(dst[:, ob, :], HB[m][:, k * LEN:(k + 1) * LEN], ACT.Gelu,
                                                   scale=fs[:, 2 + product, ob:ob + 1])
                    ins.then_inc(done, 1)

            def ffn_step(i, p):
                act.wait_ge(d_fs, reached(2 * i))
                gelu(i, 0, f1, d_m1, d_a1)
                if not (i_is(i, SEQS - 1)):
                    ffn_in_scalar(act, i + 1)
                if i_is(i, 0):
                    norm_scalar(act, 3, SEQS - 1)
                act.wait_ge(d_y, reached(i))
                gelu(i, 1, f2, d_m2, d_a2)
            over_sequences(act, ffn_step)

        @block.tensor
        def _(pe):
            pe.wait_ge(s_ident, 16)
            for c in range(CHUNKS):
                first_turn_tensor(pe, c)

            pe.wait_ge(z_xnT, CHUNKS)
            pe.wait_ge(s_w[LA], 32)
            la_qk_tensor(pe, 0, 0)
            la_v_tensor(pe, 0, 0)
            la_ktok_tensor(pe, 0, 0)

            def la_step(i, p):
                more, live = not i_is(i, SEQS - 1, SEQS), not i_is(i, SEQS)
                for g in range(LA_GROUPS):
                    if live:
                        for t in range(T):
                            la_scores_tensor(pe, i, p, g, t)
                    if g == 0 and live:
                        la_state_tensor(pe, i, p)
                    if g == 2 and not i_is(i, 0):
                        la_turn_tensor(pe, i - 1)
                    if g >= 1 and live:
                        la_sums_tensor(pe, i, p, g - 1)
                    if g == 0 and not i_is(i, 0):
                        la_sums_tensor(pe, i - 1, 1 - p, LA_GROUPS - 1)
                    if g == 0 and more:
                        la_qk_tensor(pe, i + 1, 1 - p)
                    if g == 1 and more:
                        la_v_tensor(pe, i + 1, 1 - p)
                if not i_is(i, 0):
                    la_out_tensor(pe, i - 1)
                if more:
                    la_ktok_tensor(pe, i + 1, 1 - p)
                if not i_is(i, 0, 1):
                    pe.wait_ge(a_oT, reached(i - 1))
                    norm_tensor(pe, 1, i - LA_LAG, TB)
            over_sequences(pe, la_step, 4)

            pe.wait_ge(s_w[MOE], 16 * 6)
            pe.wait_ge(a_feat, SEQS)
            moe_router_tensor(pe, 0, 0)
            la_step(SEQS, 0)
            moe_gates_tensor(pe, 0, 0)
            pe.wait_ge(s_wsh, 2)
            pe.wait_ge(n_yn[1], SEQS)
            moe_shared_tensor(pe, 0, 0)
            norm_tensor(pe, 1, SEQS - 1, TB)
            pe.wait_ge(n_xnT[1], SEQS)
            pe.wait_ge(a_m, UNITS_A * SEQS)
            pe.wait_ge(a_o, SEQS)

            def moe_block_tensor(i, p, b):
                for t in range(T):
                    moe_unit_tensor(pe, i, p, b * T + t)
            for b in range(3):
                moe_block_tensor(0, 0, b)

            def moe_step(i, p):
                more = not i_is(i, SEQS - 1)
                if more:
                    moe_router_tensor(pe, i + 1, 1 - p)
                moe_block_tensor(i, p, 3)
                if not i_is(i, 0, 1):
                    pe.wait_ge(b_acc, i * T * ACCS + T)
                    norm_tensor(pe, 2, i - 2)
                if more:
                    for b in range(2):
                        moe_block_tensor(i + 1, 1 - p, b)
                    moe_gates_tensor(pe, i + 1, 1 - p)
                    moe_shared_tensor(pe, i + 1, 1 - p)
                    moe_block_tensor(i + 1, 1 - p, 2)
            over_sequences(pe, moe_step, 4)
            norm_tensor(pe, 2, SEQS - 2)

            pe.wait_ge(b_acc, SEQS * T * ACCS)
            pe.wait_ge(c_w, BLOCKS)
            for u in order:
                sa_unit_tensor(pe, 0, 0, u, True)
            norm_tensor(pe, 2, SEQS - 1)

            def sa_slot(i, p, h):
                if not i_is(i, SEQS):
                    sa_scores_tensor(pe, i, p, h)
                at = lagged(i, p, h, TURN_LAG)
                if at:
                    sa_turn_tensor(pe, at[0], at[2])
                if not i_is(i, SEQS) and not i_is(i, SEQS - 1):
                    for u in slots[h]:
                        sa_unit_tensor(pe, i + 1, 1 - p, u)
                at = lagged(i, p, h, PV_LAG)
                if at:
                    sa_pv_tensor(pe, *at)
                if h == SA_OUT_SLOT and not i_is(i, 0):
                    sa_out_tensor(pe, i - 1, 1 - p)

            def sa_step(i, p):
                for h in range(HEADS):
                    sa_slot(i, p, h)
                    if h == SA_NORM_SLOT and not i_is(i, 0):
                        norm_tensor(pe, 3, i - 1)
            over_sequences(pe, sa_step)
            for h in range(SA_DRAIN):
                sa_slot(SEQS, 0, h)

            ffn_count_tensor(pe)
            pe.wait_ge(d_w, EARLY)
            pe.wait_ge(c_exp, SEQS * HEADS)
            pe.wait_ge(c_pte, SEQS * HEADS)
            pe.wait_ge(c_oe, SEQS * PAIRS)
            ffn_in_tensor(pe, 0)

            def ffn_steps(short):
                def ffn_step(i, p):
                    pe.wait_ge(d_hs, 2 * (i + 1))
                    ffn_product(pe, hS, h1S, d_m1, d_a2, 2 * (i - 1), short)
                    if not i_is(i, SEQS - 1):
                        ffn_in_tensor(pe, i + 1, short)
                    if not i_is(i, 0):
                        ffn_out_tensor(pe, i - 1)
                    if i_is(i, 0):
                        norm_tensor(pe, 3, SEQS - 1)
                        pe.wait_ge(d_w, EARLY + HID_T)
                    pe.wait_ge(d_fs, 2 * (i + 1))
                    ffn_product(pe, f1S, h2S, d_m2, d_a1, 2 * i, short)
                over_sequences(pe, ffn_step)
            pe.wait_ge(d_ternary, 1)
            is_ternary = pe.value_load(ternary[0:1, 0:1], min_val=0, max_val=1)
            with pe.If(is_ternary):
                ffn_steps(True)
            with pe.Else():
                ffn_steps(False)
            pe.end_ifs()
            ffn_out_tensor(pe, SEQS - 1)


_WEIGHTS = {
    "L0_attn_W_qkv": lambda a: a.T,
    "L0_attn_W_out": lambda a: a.T,
    "L0_ffn_centroids": lambda a: a.T,
    "L0_ffn_expert_biases": lambda a: a[None, :],
    "L0_ffn_Wr": lambda a: a.transpose(2, 0, 1).reshape(a.shape[2], -1),
    "L0_ffn_br": lambda a: a,
    "L0_ffn_Ws": lambda a: a.transpose(2, 0, 1),
    "L0_ffn_bs": lambda a: a,
    "L1_attn_ln_gamma": lambda a: a[:, None],
    "L1_attn_ln_beta": lambda a: a[:, None],
    "L1_attn_w_qkv": lambda a: a,
    "L1_attn_w_out": lambda a: a,
    "L1_ffn_w1_w": lambda a: a.T,
    "L1_ffn_w2_w": lambda a: a.T,
    "L1_ffn_h1_w": lambda a: a.T,
    "L1_ffn_h2_w": lambda a: a.T,
    "L1_ffn_w3_w": lambda a: a.T,
    "L1_ffn_w3_s": lambda a: a[None, :],
}


def _constants(np):
    f = np.float32
    p = np.arange(128)
    c = {"ident": np.eye(128, dtype=f)}
    c["tri"] = (p[:, None] <= p[None, :]).astype(f)
    j = np.arange(4)
    c["hm"] = ((p[:, None] % 32) // 8 == j[None, :]).astype(f) * f(8 ** -0.5)
    c["gm"] = (p[:, None] // 32 == j[None, :]).astype(f)
    own = (p[:, None] // 8 == np.arange(16)[None, :]).astype(f) * f(8 ** -0.5)
    c["sm"] = np.broadcast_to(own[:, :, None], (128, 16, 9))
    c["iota"] = np.broadcast_to(np.arange(16, dtype=f)[None], (128, 16))
    c["half"] = np.full((2, 128), 0.5, f)
    inv = f(1.0) / np.power(f(10000.0), np.arange(0, 64, 2, dtype=f) / f(64))
    pos = np.maximum(np.arange(256) - 1, 0).astype(f)
    ang = pos[:, None] * inv[None, :].astype(f)
    cos = np.concatenate([np.cos(ang), np.cos(ang)], -1)
    sin = np.concatenate([-np.sin(ang), np.sin(ang)], -1)
    cs = np.stack([cos, sin], 1).astype(f)
    both = np.stack([cs * f(64 ** -0.5), cs], 1)
    c["rope"] = both.reshape(2, 128, 2, 2, 64).transpose(1, 0, 2, 3, 4)
    return c


def kernel(**inputs):
    import numpy as np
    import concourse.bacc as bacc
    from concourse import mybir as mb
    from concourse.bass_utils import run_bass_kernel_spmd

    nc = bacc.Bacc("TRN2", target_bir_lowering=False, num_devices=1)
    arrays = {}

    def given(name, a):
        a = np.ascontiguousarray(a)
        arrays[f"in_{name}"] = a
        return nc.dram_tensor(f"in_{name}", a.shape, mb.dt.from_np(a.dtype), kind="ExternalInput").ap()

    x = given("x", np.asarray(inputs["L0_attn_x"]))
    w = {n: given(n, lay(np.asarray(inputs[n]))) for n, lay in _WEIGHTS.items()}
    scales = np.stack([np.asarray(inputs[f"L1_ffn_{n}_s"]).reshape(4, 128) for n in ("w1", "w2", "h1", "h2")])
    w["L1_ffn_scales"] = given("L1_ffn_scales", scales.transpose(2, 0, 1))
    const = {n: given(n, a) for n, a in _constants(np).items()}
    shape = inputs["L0_attn_x"].shape
    out = nc.dram_tensor("out_0", shape, mb.dt.float32, kind="ExternalOutput").ap()
    block_kernel(nc, x, w, const, out)
    r = run_bass_kernel_spmd(nc, [arrays], core_ids=[0])
    return r.results[0]["out_0"]
```
